# Optimizing a Trainium2 kernel written in Bass

```python
import numpy as np
import jax
import jax.numpy as jnp

def _softmax(x, axis=-1):
    return jax.nn.softmax(x, axis=axis)

def _gelu(x):
    return jax.nn.gelu(x, approximate=True)

def _silu(x):
    return jax.nn.silu(x)

def _sigmoid(x):
    return jax.nn.sigmoid(x)

def _layernorm(x, axis=-1, eps=1e-05):
    m = jnp.mean(x, axis=axis, keepdims=True)
    v = jnp.var(x, axis=axis, keepdims=True)
    return (x - m) / jnp.sqrt(v + eps)

def _scatter_add(tgt, idx, src, axis=0):
    return tgt.at[idx].add(src)

def _segment_sum(src, seg, n):
    return jax.ops.segment_sum(src, seg, n)
kernel_name = 'mk_recurrent_d2_jaxref_r8_bbda66'

def setup_inputs(seed: int=0):
    np.random.seed(seed)
    _w = jnp.asarray

    def _L0_attn_setup():
        import jax, jax.numpy as jnp
        import numpy as np
        HEADS, D_MODEL, D_V = (16, 128, 64)
        D_K = D_MODEL // HEADS
        key = jax.random.key(seed)
        k1, k2, k3, k4, k5 = jax.random.split(key, 5)
        B, T = (2, 256)
        s = 1.0 / np.sqrt(D_MODEL)
        return {'x': jax.random.normal(k1, (B, T, D_MODEL), dtype=jnp.float32), 'Wq': jax.random.normal(k2, (D_MODEL, HEADS * D_K), dtype=jnp.float32) * s, 'Wk': jax.random.normal(k3, (D_MODEL, HEADS * D_K), dtype=jnp.float32) * s, 'Wv': jax.random.normal(k4, (D_MODEL, HEADS * D_V), dtype=jnp.float32) * s, 'Wo': jax.random.normal(k5, (HEADS * D_V, D_MODEL), dtype=jnp.float32) * (1.0 / np.sqrt(HEADS * D_V))}
    _L0_attn_in = _L0_attn_setup()

    def _L0_ffn_setup():
        import jax, jax.numpy as jnp
        import numpy as np
        N_EMBD = 128
        N_EXP = 8
        TOP_K = 2
        CAPACITY = 512
        D_FF = 3 * N_EMBD
        key = jax.random.key(seed)
        k1, k2, k3, k4 = jax.random.split(key, 4)
        x = jax.random.normal(k1, (8, 256, N_EMBD), dtype=jnp.float32)
        w_gate = jax.random.normal(k2, (N_EMBD, N_EXP), dtype=jnp.float32) * 0.02
        c_fc = jax.random.normal(k3, (N_EXP, N_EMBD, D_FF), dtype=jnp.float32) * 0.02
        c_proj = jax.random.normal(k4, (N_EXP, D_FF // 2, N_EMBD), dtype=jnp.float32) * 0.02
        return {'x': x, 'w_gate': w_gate, 'c_fc': c_fc, 'c_proj': c_proj}
    _L0_ffn_in = _L0_ffn_setup()

    def _L1_attn_setup():
        import jax, jax.numpy as jnp
        import numpy as np
        CHUNK = 32
        EPS_L2 = 1e-06
        EPS_RMS = 1e-05
        NUM_HEADS = 4

        def _causal_dwconv_silu(x, w):
            k = w.shape[1]
            l = x.shape[1]
            xp = jnp.pad(x, ((0, 0), (k - 1, 0), (0, 0)))
            out = sum((w[:, j] * xp[:, j:j + l, :] for j in range(k)))
            return jax.nn.silu(out)

        def _l2norm(x):
            return x * jax.lax.rsqrt(jnp.sum(x * x, -1, keepdims=True) + EPS_L2)

        def _delta_rule_chunkwise(q, k, v, beta, c=CHUNK):
            b, h, l, dk = q.shape
            dv = v.shape[-1]
            n = l // c
            q = _l2norm(q)
            k = _l2norm(k)
            v = v * beta[..., None]
            kb = k * beta[..., None]
            qc = q.reshape(b, h, n, c, dk)
            kc = k.reshape(b, h, n, c, dk)
            vc = v.reshape(b, h, n, c, dv)
            kbc = kb.reshape(b, h, n, c, dk)
            strict_lower = jnp.tril(jnp.ones((c, c), bool), -1)
            attn = -jnp.einsum('bhnik,bhnjk->bhnij', kbc, kc)
            attn = jnp.where(strict_lower, attn, 0.0)
            for i in range(1, c):
                upd = jnp.einsum('bhnj,bhnjm->bhnm', attn[..., i, :], attn[..., :, :i])
                attn = attn.at[..., i, :i].add(upd)
            attn = attn + jnp.eye(c, dtype=attn.dtype)
            u = attn @ vc
            w = attn @ kbc
            incl_lower = jnp.tril(jnp.ones((c, c), bool))

            def step(S, inp):
                q_i, k_i, u_i, w_i = inp
                a = jnp.where(incl_lower, jnp.einsum('bhik,bhjk->bhij', q_i, k_i), 0.0)
                u_new = u_i - w_i @ S
                o_i = q_i @ S + a @ u_new
                S = S + jnp.einsum('bhck,bhcv->bhkv', k_i, u_new)
                return (S, o_i)
            S0 = jnp.zeros((b, h, dk, dv), q.dtype)
            xs = tuple((jnp.moveaxis(x, 2, 0) for x in (qc, kc, u, w)))
            S, o = jax.lax.scan(step, S0, xs)
            o = jnp.moveaxis(o, 0, 2).reshape(b, h, l, dv)
            return (o, S)

        def _ema(v, gamma):
            vt = jnp.moveaxis(v, 2, 0)
            gt = jnp.moveaxis(gamma, 2, 0)[..., None]

            def step(s, xg):
                x, g = xg
                s = g * s + (1.0 - g) * x
                return (s, s)
            s0 = jnp.zeros(v.shape[:2] + v.shape[-1:], v.dtype)
            _, out = jax.lax.scan(step, s0, (vt, gt))
            return jnp.moveaxis(out, 0, 2)

        def _forward(hs, Wq, Wk, Wv, Wb, Wdec, Wmix, mix_bias, wq_conv, wk_conv, wv_conv, onorm_w, Wo):
            b, l, d = hs.shape
            h = NUM_HEADS
            q = _causal_dwconv_silu(hs @ Wq.T, wq_conv)
            k = _causal_dwconv_silu(hs @ Wk.T, wk_conv)
            v = _causal_dwconv_silu(hs @ Wv.T, wv_conv)
            dk = q.shape[-1] // h
            dv = v.shape[-1] // h
            q = q.reshape(b, l, h, dk)
            k = k.reshape(b, l, h, dk)
            v = v.reshape(b, l, h, dv)
            beta = jax.nn.sigmoid(hs @ Wb.T)
            qd = jnp.transpose(q, (0, 2, 1, 3))
            kd = jnp.transpose(k, (0, 2, 1, 3))
            vd = jnp.transpose(v, (0, 2, 1, 3))
            bd = jnp.transpose(beta, (0, 2, 1))
            o_d, _S = _delta_rule_chunkwise(qd, kd, vd, bd)
            o_d = jnp.transpose(o_d, (0, 2, 1, 3))
            gamma = jnp.transpose(jax.nn.sigmoid(hs @ Wdec.T), (0, 2, 1))
            ema_out = jnp.transpose(_ema(vd, gamma), (0, 2, 1, 3))
            mix = jax.nn.sigmoid(hs @ Wmix.T + mix_bias)[..., None]
            o = (1.0 - mix) * o_d + mix * ema_out
            o = o * jax.lax.rsqrt(jnp.mean(o * o, -1, keepdims=True) + EPS_RMS) * onorm_w
            return o.reshape(b, l, h * dv) @ Wo.T
        key = jax.random.key(seed)
        ks = jax.random.split(key, 12)
        B, L, D, H, K = (2, 512, 128, 4, 4)
        s = 0.02
        f = jnp.float32
        return {'hidden_states': jax.random.normal(ks[0], (B, L, D), f), 'Wq': jax.random.normal(ks[1], (D, D), f) * s, 'Wk': jax.random.normal(ks[2], (D, D), f) * s, 'Wv': jax.random.normal(ks[3], (D, D), f) * s, 'Wb': jax.random.normal(ks[4], (H, D), f) * s, 'Wdec': jax.random.normal(ks[5], (H, D), f) * s, 'Wmix': jax.random.normal(ks[6], (H, D), f) * s, 'mix_bias': jnp.zeros((H,), f), 'wq_conv': jax.random.normal(ks[7], (D, K), f) * 0.3, 'wk_conv': jax.random.normal(ks[8], (D, K), f) * 0.3, 'wv_conv': jax.random.normal(ks[9], (D, K), f) * 0.3, 'onorm_w': jnp.ones((D // H,), f), 'Wo': jax.random.normal(ks[10], (D, D), f) * s}
    _L1_attn_in = _L1_attn_setup()

    def _L1_ffn_setup():
        import jax, jax.numpy as jnp
        import numpy as np
        DIM = 128
        DEPTH = 2
        HEADS = 8
        DIM_HEAD = 64
        WINDOW = 64
        INNER = HEADS * DIM_HEAD
        HID = int(DIM * 4 * 2 / 3)
        B, N = (2, 1024)
        QK_SCALE = 8.0

        def shift_token(t):
            t1, t2 = jnp.split(t, 2, axis=-1)
            t2 = jnp.pad(t2, ((0, 0), (1, 0), (0, 0)))[:, :-1]
            return jnp.concatenate([t1, t2], axis=-1)

        def l2norm(t):
            return t / jnp.clip(jnp.linalg.norm(t, axis=-1, keepdims=True), 1e-12)

        def rotate_half(x):
            x1, x2 = jnp.split(x, 2, axis=-1)
            return jnp.concatenate([-x2, x1], axis=-1)

        def rotary_xpos(q, k):
            n = q.shape[-2]
            half_idx = jnp.arange(0, DIM_HEAD, 2, dtype=jnp.float32)
            inv_freq = 1.0 / 10000.0 ** (half_idx / DIM_HEAD)
            t = jnp.arange(n, dtype=jnp.float32)
            freqs = t[:, None] * inv_freq[None, :]
            freqs = jnp.concatenate([freqs, freqs], axis=-1)
            base = (half_idx + 0.4 * DIM_HEAD) / (1.4 * DIM_HEAD)
            power = (t - n // 2) / float(WINDOW // 2)
            scale = base[None, :] ** power[:, None]
            scale = jnp.concatenate([scale, scale], axis=-1)
            cos, sin = (jnp.cos(freqs), jnp.sin(freqs))
            q = q * cos * scale + rotate_half(q) * sin * scale
            k = k * cos / scale + rotate_half(k) * sin / scale
            return (q, k)

        def local_attention(q, k, v):
            b, h, n, d = q.shape
            w = n // WINDOW
            bq = q.reshape(b, h, w, WINDOW, d) * QK_SCALE
            bk = k.reshape(b, h, w, WINDOW, d)
            bv = v.reshape(b, h, w, WINDOW, d)

            def look_around(t):
                p = jnp.pad(t, ((0, 0), (0, 0), (1, 0), (0, 0), (0, 0)))
                return jnp.concatenate([p[:, :, :w], p[:, :, 1:]], axis=3)
            bk, bv = (look_around(bk), look_around(bv))
            bt = jnp.arange(n).reshape(w, WINDOW)
            btp = jnp.pad(bt, ((1, 0), (0, 0)), constant_values=-1)
            btk = jnp.concatenate([btp[:w], btp[1:]], axis=1)
            sim = jnp.einsum('bhwid,bhwjd->bhwij', bq, bk)
            i = bt[:, :, None]
            j = btk[:, None, :]
            mask = (i < j) | (i > j + WINDOW) | (j == -1)
            sim = jnp.where(mask, -jnp.finfo(sim.dtype).max, sim)
            attn = jax.nn.softmax(sim, axis=-1)
            out = jnp.einsum('bhwij,bhwjd->bhwid', attn, bv)
            return out.reshape(b, h, n, d)

        def _layer(x, wqkv, qs, ksc, wo, lg, lb, w1, b1, w2, b2):
            b, n, _ = x.shape
            h = shift_token(x)
            qkv = h @ wqkv
            q, k, v = jnp.split(qkv, 3, axis=-1)
            to_heads = lambda t: t.reshape(b, n, HEADS, DIM_HEAD).transpose(0, 2, 1, 3)
            q, k, v = (to_heads(q), to_heads(k), to_heads(v))
            q = l2norm(q) * qs
            k = l2norm(k) * ksc
            q, k = rotary_xpos(q, k)
            o = local_attention(q, k, v)
            o = o.transpose(0, 2, 1, 3).reshape(b, n, INNER)
            x = x + o @ wo
            h = shift_token(x)
            mu = h.mean(-1, keepdims=True)
            var = h.var(-1, keepdims=True)
            h = (h - mu) / jnp.sqrt(var + 1e-05) * lg + lb
            h = h @ w1 + b1
            a, g = jnp.split(h, 2, axis=-1)
            h = a * jax.nn.gelu(g, approximate=False)
            x = x + h @ w2 + b2
            return x
        key = jax.random.key(seed)
        ks = jax.random.split(key, 6)
        return {'x': jax.random.normal(ks[0], (B, N, DIM), jnp.float32), 'wqkv': jax.random.normal(ks[1], (DEPTH, DIM, 3 * INNER), jnp.float32) * 0.02, 'q_scale': jnp.ones((DEPTH, DIM_HEAD), jnp.float32), 'k_scale': jnp.ones((DEPTH, DIM_HEAD), jnp.float32), 'wo': jax.random.normal(ks[2], (DEPTH, INNER, DIM), jnp.float32) * 0.02, 'ln_g': jnp.ones((DEPTH, DIM), jnp.float32), 'ln_b': jnp.zeros((DEPTH, DIM), jnp.float32), 'w1': jax.random.normal(ks[3], (DEPTH, DIM, 2 * HID), jnp.float32) * 0.02, 'b1': jnp.zeros((DEPTH, 2 * HID), jnp.float32), 'w2': jax.random.normal(ks[4], (DEPTH, HID, DIM), jnp.float32) * 0.02, 'b2': jnp.zeros((DEPTH, DIM), jnp.float32)}
    _L1_ffn_in = _L1_ffn_setup()
    _d = {'L0_attn_x': _L0_attn_in['x'], 'L0_attn_Wq': _L0_attn_in['Wq'], 'L0_attn_Wk': _L0_attn_in['Wk'], 'L0_attn_Wv': _L0_attn_in['Wv'], 'L0_attn_Wo': _L0_attn_in['Wo'], 'L0_ffn_w_gate': _L0_ffn_in['w_gate'], 'L0_ffn_c_fc': _L0_ffn_in['c_fc'], 'L0_ffn_c_proj': _L0_ffn_in['c_proj'], 'L1_attn_Wq': _L1_attn_in['Wq'], 'L1_attn_Wk': _L1_attn_in['Wk'], 'L1_attn_Wv': _L1_attn_in['Wv'], 'L1_attn_Wb': _L1_attn_in['Wb'], 'L1_attn_Wdec': _L1_attn_in['Wdec'], 'L1_attn_Wmix': _L1_attn_in['Wmix'], 'L1_attn_mix_bias': _L1_attn_in['mix_bias'], 'L1_attn_wq_conv': _L1_attn_in['wq_conv'], 'L1_attn_wk_conv': _L1_attn_in['wk_conv'], 'L1_attn_wv_conv': _L1_attn_in['wv_conv'], 'L1_attn_onorm_w': _L1_attn_in['onorm_w'], 'L1_attn_Wo': _L1_attn_in['Wo'], 'L1_ffn_wqkv': _L1_ffn_in['wqkv'], 'L1_ffn_q_scale': _L1_ffn_in['q_scale'], 'L1_ffn_k_scale': _L1_ffn_in['k_scale'], 'L1_ffn_wo': _L1_ffn_in['wo'], 'L1_ffn_ln_g': _L1_ffn_in['ln_g'], 'L1_ffn_ln_b': _L1_ffn_in['ln_b'], 'L1_ffn_w1': _L1_ffn_in['w1'], 'L1_ffn_b1': _L1_ffn_in['b1'], 'L1_ffn_w2': _L1_ffn_in['w2'], 'L1_ffn_b2': _L1_ffn_in['b2']}
    _x0 = _d['L0_attn_x']
    _d['L0_attn_x'] = jax.random.normal(jax.random.fold_in(jax.random.key(seed), 1), (8, 512, 128), dtype=_x0.dtype)
    del _x0
    return _d

def reference(L0_attn_x, L0_attn_Wq, L0_attn_Wk, L0_attn_Wv, L0_attn_Wo, L0_ffn_w_gate, L0_ffn_c_fc, L0_ffn_c_proj, L1_attn_Wq, L1_attn_Wk, L1_attn_Wv, L1_attn_Wb, L1_attn_Wdec, L1_attn_Wmix, L1_attn_mix_bias, L1_attn_wq_conv, L1_attn_wk_conv, L1_attn_wv_conv, L1_attn_onorm_w, L1_attn_Wo, L1_ffn_wqkv, L1_ffn_q_scale, L1_ffn_k_scale, L1_ffn_wo, L1_ffn_ln_g, L1_ffn_ln_b, L1_ffn_w1, L1_ffn_b1, L1_ffn_w2, L1_ffn_b2):

    def _L0_attn_ref(x, Wq, Wk, Wv, Wo):
        import jax, jax.numpy as jnp
        import numpy as np
        HEADS, D_MODEL, D_V = (16, 128, 64)
        D_K = D_MODEL // HEADS
        B, T, _ = x.shape
        scale = jnp.asarray(np.sqrt(D_K), x.dtype)
        q = (x @ Wq).reshape(B, T, HEADS, D_K).transpose(0, 2, 1, 3)
        k = (x @ Wk).reshape(B, T, HEADS, D_K).transpose(0, 2, 1, 3)
        v = (x @ Wv).reshape(B, T, HEADS, D_V).transpose(0, 2, 1, 3)
        scores = jnp.einsum('bhqd,bhkd->bhqk', q, k) / scale
        causal = jnp.triu(jnp.ones((T, T), dtype=bool), k=1)
        scores = jnp.where(causal, jnp.asarray(-jnp.inf, scores.dtype), scores)
        attn = jax.nn.softmax(scores, axis=-1)
        ctx = jnp.einsum('bhqk,bhkd->bhqd', attn, v)
        out = ctx.transpose(0, 2, 1, 3).reshape(B, T, HEADS * D_V)
        return out @ Wo

    def _L0_ffn_ref(x, w_gate, c_fc, c_proj):
        import jax, jax.numpy as jnp
        import numpy as np
        N_EMBD = 128
        N_EXP = 8
        TOP_K = 2
        CAPACITY = 512
        D_FF = 3 * N_EMBD
        B, T, d = x.shape
        N = B * T
        xf = x.reshape(N, d)
        scores = jax.nn.softmax(xf @ w_gate, axis=-1)
        weights, idx = jax.lax.top_k(scores, TOP_K)
        flat_e = idx.reshape(-1)
        tok = jnp.repeat(jnp.arange(N), TOP_K)
        oh = jax.nn.one_hot(flat_e, N_EXP, dtype=jnp.int32)
        pos = (jnp.cumsum(oh, axis=0) * oh).sum(-1) - 1
        valid = pos < CAPACITY
        pos_c = jnp.where(valid, pos, 0)
        vmask = valid.astype(x.dtype)[:, None]
        exp_x = jnp.zeros((N_EXP, CAPACITY, d), x.dtype)
        exp_x = exp_x.at[flat_e, pos_c].add(xf[tok] * vmask)
        h = jnp.einsum('ecd,edf->ecf', exp_x, c_fc)
        a, g = jnp.split(h, 2, axis=-1)
        h = jax.nn.silu(a) * g
        exp_out = jnp.einsum('ecf,efd->ecd', h, c_proj)
        gathered = exp_out[flat_e, pos_c]
        w = weights.reshape(-1)[:, None] * vmask
        out = (gathered * w).reshape(N, TOP_K, d).sum(axis=1)
        return out.reshape(B, T, d)

    def _L1_attn_ref(hidden_states, Wq, Wk, Wv, Wb, Wdec, Wmix, mix_bias, wq_conv, wk_conv, wv_conv, onorm_w, Wo):
        import jax, jax.numpy as jnp
        import numpy as np
        CHUNK = 32
        EPS_L2 = 1e-06
        EPS_RMS = 1e-05
        NUM_HEADS = 4

        def _causal_dwconv_silu(x, w):
            k = w.shape[1]
            l = x.shape[1]
            xp = jnp.pad(x, ((0, 0), (k - 1, 0), (0, 0)))
            out = sum((w[:, j] * xp[:, j:j + l, :] for j in range(k)))
            return jax.nn.silu(out)

        def _l2norm(x):
            return x * jax.lax.rsqrt(jnp.sum(x * x, -1, keepdims=True) + EPS_L2)

        def _delta_rule_chunkwise(q, k, v, beta, c=CHUNK):
            b, h, l, dk = q.shape
            dv = v.shape[-1]
            n = l // c
            q = _l2norm(q)
            k = _l2norm(k)
            v = v * beta[..., None]
            kb = k * beta[..., None]
            qc = q.reshape(b, h, n, c, dk)
            kc = k.reshape(b, h, n, c, dk)
            vc = v.reshape(b, h, n, c, dv)
            kbc = kb.reshape(b, h, n, c, dk)
            strict_lower = jnp.tril(jnp.ones((c, c), bool), -1)
            attn = -jnp.einsum('bhnik,bhnjk->bhnij', kbc, kc)
            attn = jnp.where(strict_lower, attn, 0.0)
            for i in range(1, c):
                upd = jnp.einsum('bhnj,bhnjm->bhnm', attn[..., i, :], attn[..., :, :i])
                attn = attn.at[..., i, :i].add(upd)
            attn = attn + jnp.eye(c, dtype=attn.dtype)
            u = attn @ vc
            w = attn @ kbc
            incl_lower = jnp.tril(jnp.ones((c, c), bool))

            def step(S, inp):
                q_i, k_i, u_i, w_i = inp
                a = jnp.where(incl_lower, jnp.einsum('bhik,bhjk->bhij', q_i, k_i), 0.0)
                u_new = u_i - w_i @ S
                o_i = q_i @ S + a @ u_new
                S = S + jnp.einsum('bhck,bhcv->bhkv', k_i, u_new)
                return (S, o_i)
            S0 = jnp.zeros((b, h, dk, dv), q.dtype)
            xs = tuple((jnp.moveaxis(x, 2, 0) for x in (qc, kc, u, w)))
            S, o = jax.lax.scan(step, S0, xs)
            o = jnp.moveaxis(o, 0, 2).reshape(b, h, l, dv)
            return (o, S)

        def _ema(v, gamma):
            vt = jnp.moveaxis(v, 2, 0)
            gt = jnp.moveaxis(gamma, 2, 0)[..., None]

            def step(s, xg):
                x, g = xg
                s = g * s + (1.0 - g) * x
                return (s, s)
            s0 = jnp.zeros(v.shape[:2] + v.shape[-1:], v.dtype)
            _, out = jax.lax.scan(step, s0, (vt, gt))
            return jnp.moveaxis(out, 0, 2)

        def _forward(hs, Wq, Wk, Wv, Wb, Wdec, Wmix, mix_bias, wq_conv, wk_conv, wv_conv, onorm_w, Wo):
            b, l, d = hs.shape
            h = NUM_HEADS
            q = _causal_dwconv_silu(hs @ Wq.T, wq_conv)
            k = _causal_dwconv_silu(hs @ Wk.T, wk_conv)
            v = _causal_dwconv_silu(hs @ Wv.T, wv_conv)
            dk = q.shape[-1] // h
            dv = v.shape[-1] // h
            q = q.reshape(b, l, h, dk)
            k = k.reshape(b, l, h, dk)
            v = v.reshape(b, l, h, dv)
            beta = jax.nn.sigmoid(hs @ Wb.T)
            qd = jnp.transpose(q, (0, 2, 1, 3))
            kd = jnp.transpose(k, (0, 2, 1, 3))
            vd = jnp.transpose(v, (0, 2, 1, 3))
            bd = jnp.transpose(beta, (0, 2, 1))
            o_d, _S = _delta_rule_chunkwise(qd, kd, vd, bd)
            o_d = jnp.transpose(o_d, (0, 2, 1, 3))
            gamma = jnp.transpose(jax.nn.sigmoid(hs @ Wdec.T), (0, 2, 1))
            ema_out = jnp.transpose(_ema(vd, gamma), (0, 2, 1, 3))
            mix = jax.nn.sigmoid(hs @ Wmix.T + mix_bias)[..., None]
            o = (1.0 - mix) * o_d + mix * ema_out
            o = o * jax.lax.rsqrt(jnp.mean(o * o, -1, keepdims=True) + EPS_RMS) * onorm_w
            return o.reshape(b, l, h * dv) @ Wo.T
        return _forward(hidden_states, Wq, Wk, Wv, Wb, Wdec, Wmix, mix_bias, wq_conv, wk_conv, wv_conv, onorm_w, Wo)

    def _L1_ffn_ref(x, wqkv, q_scale, k_scale, wo, ln_g, ln_b, w1, b1, w2, b2):
        import jax, jax.numpy as jnp
        import numpy as np
        DIM = 128
        DEPTH = 2
        HEADS = 8
        DIM_HEAD = 64
        WINDOW = 64
        INNER = HEADS * DIM_HEAD
        HID = int(DIM * 4 * 2 / 3)
        B, N = (2, 1024)
        QK_SCALE = 8.0

        def shift_token(t):
            t1, t2 = jnp.split(t, 2, axis=-1)
            t2 = jnp.pad(t2, ((0, 0), (1, 0), (0, 0)))[:, :-1]
            return jnp.concatenate([t1, t2], axis=-1)

        def l2norm(t):
            return t / jnp.clip(jnp.linalg.norm(t, axis=-1, keepdims=True), 1e-12)

        def rotate_half(x):
            x1, x2 = jnp.split(x, 2, axis=-1)
            return jnp.concatenate([-x2, x1], axis=-1)

        def rotary_xpos(q, k):
            n = q.shape[-2]
            half_idx = jnp.arange(0, DIM_HEAD, 2, dtype=jnp.float32)
            inv_freq = 1.0 / 10000.0 ** (half_idx / DIM_HEAD)
            t = jnp.arange(n, dtype=jnp.float32)
            freqs = t[:, None] * inv_freq[None, :]
            freqs = jnp.concatenate([freqs, freqs], axis=-1)
            base = (half_idx + 0.4 * DIM_HEAD) / (1.4 * DIM_HEAD)
            power = (t - n // 2) / float(WINDOW // 2)
            scale = base[None, :] ** power[:, None]
            scale = jnp.concatenate([scale, scale], axis=-1)
            cos, sin = (jnp.cos(freqs), jnp.sin(freqs))
            q = q * cos * scale + rotate_half(q) * sin * scale
            k = k * cos / scale + rotate_half(k) * sin / scale
            return (q, k)

        def local_attention(q, k, v):
            b, h, n, d = q.shape
            w = n // WINDOW
            bq = q.reshape(b, h, w, WINDOW, d) * QK_SCALE
            bk = k.reshape(b, h, w, WINDOW, d)
            bv = v.reshape(b, h, w, WINDOW, d)

            def look_around(t):
                p = jnp.pad(t, ((0, 0), (0, 0), (1, 0), (0, 0), (0, 0)))
                return jnp.concatenate([p[:, :, :w], p[:, :, 1:]], axis=3)
            bk, bv = (look_around(bk), look_around(bv))
            bt = jnp.arange(n).reshape(w, WINDOW)
            btp = jnp.pad(bt, ((1, 0), (0, 0)), constant_values=-1)
            btk = jnp.concatenate([btp[:w], btp[1:]], axis=1)
            sim = jnp.einsum('bhwid,bhwjd->bhwij', bq, bk)
            i = bt[:, :, None]
            j = btk[:, None, :]
            mask = (i < j) | (i > j + WINDOW) | (j == -1)
            sim = jnp.where(mask, -jnp.finfo(sim.dtype).max, sim)
            attn = jax.nn.softmax(sim, axis=-1)
            out = jnp.einsum('bhwij,bhwjd->bhwid', attn, bv)
            return out.reshape(b, h, n, d)

        def _layer(x, wqkv, qs, ksc, wo, lg, lb, w1, b1, w2, b2):
            b, n, _ = x.shape
            h = shift_token(x)
            qkv = h @ wqkv
            q, k, v = jnp.split(qkv, 3, axis=-1)
            to_heads = lambda t: t.reshape(b, n, HEADS, DIM_HEAD).transpose(0, 2, 1, 3)
            q, k, v = (to_heads(q), to_heads(k), to_heads(v))
            q = l2norm(q) * qs
            k = l2norm(k) * ksc
            q, k = rotary_xpos(q, k)
            o = local_attention(q, k, v)
            o = o.transpose(0, 2, 1, 3).reshape(b, n, INNER)
            x = x + o @ wo
            h = shift_token(x)
            mu = h.mean(-1, keepdims=True)
            var = h.var(-1, keepdims=True)
            h = (h - mu) / jnp.sqrt(var + 1e-05) * lg + lb
            h = h @ w1 + b1
            a, g = jnp.split(h, 2, axis=-1)
            h = a * jax.nn.gelu(g, approximate=False)
            x = x + h @ w2 + b2
            return x
        for l in range(DEPTH):
            x = _layer(x, wqkv[l], q_scale[l], k_scale[l], wo[l], ln_g[l], ln_b[l], w1[l], b1[l], w2[l], b2[l])
        return x
    x = L0_attn_x
    xn = _layernorm(x, axis=-1)
    s = _L0_attn_ref(xn, L0_attn_Wq, L0_attn_Wk, L0_attn_Wv, L0_attn_Wo)
    g = _silu(_L0_ffn_ref(xn, L0_ffn_w_gate, L0_ffn_c_fc, L0_ffn_c_proj))
    x = x + s * g
    xn = _layernorm(x, axis=-1)
    s = _L1_attn_ref(xn, L1_attn_Wq, L1_attn_Wk, L1_attn_Wv, L1_attn_Wb, L1_attn_Wdec, L1_attn_Wmix, L1_attn_mix_bias, L1_attn_wq_conv, L1_attn_wk_conv, L1_attn_wv_conv, L1_attn_onorm_w, L1_attn_Wo)
    g = _silu(_L1_ffn_ref(xn, L1_ffn_wqkv, L1_ffn_q_scale, L1_ffn_k_scale, L1_ffn_wo, L1_ffn_ln_g, L1_ffn_ln_b, L1_ffn_w1, L1_ffn_b1, L1_ffn_w2, L1_ffn_b2))
    x = x + s * g
    return x

_drawn_inputs = setup_inputs


def setup_inputs(seed=0):
    import zlib

    import numpy as np

    out = dict(_drawn_inputs(seed))
    spreads = {'L1_attn_mix_bias': (0.0, 0.8),
     'L1_attn_onorm_w': (1.0, 0.2),
     'L1_ffn_q_scale': (1.0, 0.6),
     'L1_ffn_k_scale': (1.0, 0.6),
     'L1_ffn_ln_g': (1.0, 0.6),
     'L1_ffn_ln_b': (0.0, 0.8),
     'L1_ffn_b1': (0.0, 0.8),
     'L1_ffn_b2': (0.0, 0.372)}
    factors = {'L0_attn_Wq': 8.0,
     'L0_attn_Wk': 8.0,
     'L0_attn_Wv': 8.0,
     'L0_attn_Wo': 8.0,
     'L0_ffn_w_gate': 8.0,
     'L0_ffn_c_fc': 8.0,
     'L0_ffn_c_proj': 8.0,
     'L1_attn_Wb': 4.96,
     'L1_attn_Wdec': 4.259,
     'L1_attn_Wmix': 3.486,
     'L1_ffn_wqkv': 8.0,
     'L1_ffn_wo': 8.0,
     'L1_ffn_w1': 8.0,
     'L1_ffn_w2': 8.0}
    for name, (base, spread) in spreads.items():
        noise = np.random.default_rng([zlib.crc32(name.encode()), seed]).standard_normal(out[name].shape)
        drawn = base * np.exp(spread * noise) if base else spread * noise
        out[name] = jnp.asarray(drawn.astype(out[name].dtype))
    for name, factor in factors.items():
        out[name] = (out[name] * factor).astype(out[name].dtype)
    return out
```

```python
from contextlib import ExitStack

import numpy as np

import concourse.bass as bass
from concourse import mybir

F32 = mybir.dt.float32
BF16 = mybir.dt.bfloat16
U32 = mybir.dt.uint32
ALU = mybir.AluOpType
ACT = mybir.ActivationFunctionType
AX_X = mybir.AxisListType.X

P = 128
B, T = 8, 512
NT = T // P
NTILE = B * NT
BANK = 512
NEG = -1e30

H0, DK0, DV0 = 16, 8, 64
G0 = 4
NE, CAP, HALF = 8, 512, 192
HC = 96
H1, DH1, CH = 4, 32, 32
DEPTH, H2, D2, WIN = 2, 8, 64, 64
HID = int(P * 4 * 2 / 3)
HCH = [(0, 128), (128, 128), (256, HID - 256)]

C_ID, C_USTRICT, C_ONES, C_MEAN = 0, 128, 256, 384
C_BLK32, C_BLK64 = 512, 640
C_CAUSAL, C_CAUSALT = 768, 896
C_BAND, C_BANDT = 1024, 1216
C_DELTA = 1408
C_IOTA = C_DELTA + 320
C_KONE = C_IOTA + 8
C_SEL = C_KONE + 1
C_COS = C_SEL + H2
C_END = C_COS + 4 * T
(D_NEGLO, D_NEGLOT, D_INCLT, D_EYE, D_M1, D_M1T, D_M2T, D_M4T, D_M8T, D_M16T) = range(10)


def constants():
    c = np.zeros((P, C_END), np.float32)
    p = np.arange(P)[:, None]
    f = np.arange(P)[None, :]
    c[:, C_ID:C_ID + P] = p == f
    c[:, C_USTRICT:C_USTRICT + P] = p < f
    c[:, C_ONES:C_ONES + P] = 1.0
    c[:, C_MEAN:C_MEAN + P] = 1.0 / P
    c[:, C_BLK32:C_BLK32 + P] = p // DH1 == f // DH1
    c[:, C_BLK64:C_BLK64 + P] = p // D2 == f // D2
    c[:, C_CAUSAL:C_CAUSAL + P] = np.where(f > p, NEG, 0.0)
    c[:, C_CAUSALT:C_CAUSALT + P] = np.where(p > f, NEG, 0.0)
    w = np.arange(P + WIN)[None, :]
    gap = p - (w - WIN)
    c[:, C_BAND:C_BAND + P + WIN] = np.where((gap < 0) | (gap > WIN), NEG, 0.0)
    gap = w - p
    c[:, C_BANDT:C_BANDT + P + WIN] = np.where((gap < 0) | (gap > WIN), NEG, 0.0)
    i = p % CH
    j = np.arange(CH)[None, :]

    def lower(a, b, s):
        return (a // (2 * s) == b // (2 * s)) & (a % (2 * s) >= s) & (b % (2 * s) < s)

    masks = [-1.0 * (i > j), -1.0 * (i < j), j >= i, i == j, lower(i, j, 1), lower(j, i, 1),
             lower(j, i, 2), lower(j, i, 4), lower(j, i, 8), lower(j, i, 16)]
    for n, m in enumerate(masks):
        c[:, C_DELTA + n * CH:C_DELTA + (n + 1) * CH] = m
    c[:, C_IOTA:C_IOTA + NE] = np.arange(NE)
    c[:, C_KONE] = (np.arange(P) % 32) == DK0
    c[:, C_SEL:C_SEL + H2] = (p % H2 == np.arange(H2)) & (p < 3 * H2)
    half = np.arange(0, D2, 2, dtype=np.float32)
    inv = (np.float32(1.0) / np.float32(10000.0) ** (half / np.float32(D2))).astype(np.float32)
    t = np.arange(T, dtype=np.float32)
    freqs = (t[:, None] * inv[None, :]).astype(np.float32)
    base = ((half + np.float32(0.4 * D2)) / np.float32(1.4 * D2)).astype(np.float32)
    power = ((t - T // 2) / np.float32(WIN // 2)).astype(np.float32)
    scale = (base[None, :] ** power[:, None]).astype(np.float32)
    cos, sin = np.cos(freqs), np.sin(freqs)
    for n, tab in enumerate((cos * scale, sin * scale, cos / scale, sin / scale)):
        first = -tab if n % 2 else tab
        rows = np.concatenate([first, tab, first, tab], axis=1).T
        c[:, C_COS + n * T:C_COS + (n + 1) * T] = rows
    return c


ROUTE = "zeroed loaded cast stats moments variance rstd normed normedT normedT_kept kept logits".split()


def layer_norm_steps(nc, s, dve, x_tile, stats, moments, var_eps, rstd, out):
    for t in range(NT):
        nc.vector.bn_stats(stats[:, 6 * t:6 * t + 6], x_tile(t)).then_inc(s["stats"], 1)
    for t in range(NT):
        dve.wait_ge(s["stats"], t + 1)
        nc.vector.bn_aggr(moments[:, 2 * t:2 * t + 2], stats[:, 6 * t:6 * t + 6]).then_inc(s["moments"], 1)
    dve.wait_ge(s["moments"], NT)
    nc.vector.tensor_scalar(var_eps[:, :], moments[:, 1:2 * NT:2], 1e-5, None, ALU.add).then_inc(s["variance"], 1)
    dve.wait_ge(s["rstd"], 1)
    for t in range(NT):
        nc.vector.tensor_scalar(out(t), x_tile(t), moments[:, 2 * t:2 * t + 1], rstd[:, t:t + 1],
                                ALU.subtract, ALU.mult).then_inc(s["normed"], 1)


def network(nc, ins, out):
    (x_in, w_q0, w_k0, w_v0, w_o0, w_gate, c_fc, c_proj, w_q1, w_k1, w_v1, w_beta, w_decay, w_mix, mix_bias,
     conv_q, conv_k, conv_v, onorm, w_o1, w_qkv, scales, w_oa, ln_g, ln_b, w_1, b_1, w_2, b_2, const_in) = ins

    with ExitStack() as ctx:
        def sb(name, cols, dt=F32, rows=P):
            return ctx.enter_context(nc.sbuf_tensor(name, [rows, cols], dt))

        pool = [ctx.enter_context(nc.semaphore(f"phase_{i}")) for i in range(120)]
        clearable = range(pool[0].num, pool[-1].num + 1)
        scattered = ctx.enter_context(nc.semaphore("scattered"))
        gathered = ctx.enter_context(nc.semaphore("gathered"))

        def phase(names):
            return dict(zip(names, pool))

        def end_phase():
            nc.all_engine_barrier(sems_to_clear=clearable)

        PS = ctx.enter_context(nc.psum_tensor("PS", [P, 8 * BANK], F32))

        def bank(k, a=0, b=BANK):
            return PS[:, BANK * k + a:BANK * k + b]

        slots_in = nc.dram_tensor("slots_in", (NE * CAP, P), F32, kind="Internal").ap()
        slots_out = nc.dram_tensor("slots_out", (NE * CAP, P), F32, kind="Internal").ap()

        cst = sb("cst", C_COS)
        ident = cst[:, C_ID:C_ID + P]
        ones_row = cst[0:1, C_ONES:C_ONES + P]
        causal16 = sb("causal16", P, BF16)
        causalT16 = sb("causalT16", P, BF16)
        band16 = sb("band16", P + WIN, BF16)
        bandT16 = sb("bandT16", P + WIN, BF16)
        ident16 = sb("ident16", P, BF16)

        wq0s = sb("wq0s", G0 * P)
        wk0s = sb("wk0s", G0 * P)
        wv0 = sb("wv0", H0 * DV0)
        wo0 = sb("wo0", H0 * DV0)
        wg = sb("wg", NE)

        x_all = sb("x_all", NTILE * P)
        xnT_all = sb("xnT_all", B * T)
        route_w = sb("route_w", 2 * NTILE)
        slot_from = sb("slot_from", 2 * NTILE, U32)

        stats = sb("stats", 6 * NT)
        moments = sb("moments", 2 * NT)
        var_eps = sb("var_eps", NT)
        rstd = sb("rstd", NT)
        minus_half = sb("minus_half", NT)
        xn_b = sb("xn_b", NT * P)
        xnT_b = sb("xnT_b", T)

        wq1 = sb("wq1", P)
        wk1 = sb("wk1", P)
        wv1 = sb("wv1", P)
        wo1 = sb("wo1", P)
        w_gates = sb("w_gates", 3 * P)
        conv_w = sb("conv_w", 12)
        column = sb("column", 2)
        wqkv = sb("wqkv", DEPTH * 1536)
        w_swap = sb("w_swap", DEPTH * 1024)
        w_oa_sb = sb("w_oa_sb", DEPTH * 4 * P)
        w1_sb = sb("w1_sb", DEPTH * 2 * HID)
        w2_sb = sb("w2_sb", DEPTH * 3 * P)
        b1_sb = sb("b1_sb", DEPTH * 6)
        b2_sb = sb("b2_sb", DEPTH * P, F32, 1)
        ln_sb = sb("ln_sb", 2 * DEPTH)
        tables = sb("tables", DEPTH * 4 * T)
        select16 = sb("select16", H2 * P, BF16, 3 * H2)
        eps = sb("eps", 2)

        before = ctx.enter_context(ExitStack())

        def sb0(name, cols, dt=F32, rows=P):
            return before.enter_context(nc.sbuf_tensor(name, [rows, cols], dt))

        wq0 = sb0("wq0", P)
        wk0 = sb0("wk0", P)
        gates_in = sb0("gates_in", 3 * H1)
        scales_in = sb0("scales_in", 4 * DEPTH)
        rotary = sb0("rotary", 4 * T)
        xn_all = sb0("xn_all", NTILE * P)
        logits_all = sb0("logits_all", NTILE * NE)

        s = phase("loaded zeros cleared cast spread".split())
        with nc.Block() as block:
            zeros = xn_all
            LOADS = [(cst[:, :], const_in[:, 0:C_COS]), (rotary[:, :], const_in[:, C_COS:C_END]),
                     (wq0[:, :], w_q0), (wk0[:, :], w_k0), (wv0[:, :], w_v0), (wg[:, :], w_gate),
                     (wq1[:, :], w_q1), (wk1[:, :], w_k1), (wv1[:, :], w_v1), (wo1[:, :], w_o1),
                     (gates_in[:, 0:H1], w_beta), (gates_in[:, H1:2 * H1], w_decay), (gates_in[:, 2 * H1:3 * H1], w_mix),
                     (conv_w[:, 0:4], conv_q), (conv_w[:, 4:8], conv_k), (conv_w[:, 8:12], conv_v),
                     (column[:, 0:1], mix_bias), (column[:, 1:2], onorm),
                     (scales_in[:, :], scales), (b2_sb[:, :], b_2.rearrange("l (o n) -> o (l n)", o=1)),
                     (ln_sb[:, 0:DEPTH], ln_g), (ln_sb[:, DEPTH:2 * DEPTH], ln_b)]
            for l in range(DEPTH):
                LOADS += [(wqkv[:, l * 1536:(l + 1) * 1536], w_qkv[l]), (w1_sb[:, l * 2 * HID:(l + 1) * 2 * HID], w_1[l]),
                          (w_oa_sb[:, l * 512:(l + 1) * 512].rearrange("p (c n) -> p c n", n=P),
                           w_oa[l].rearrange("(c p) n -> p c n", p=P))]
                for c, (start, n) in enumerate(HCH):
                    k = (l * 3 + c) * P
                    LOADS.append((w2_sb[0:n, k:k + P], w_2[l, start:start + n, :]))
                    for half in range(2):
                        k = (l * 2 + half) * 3 + c
                        a = half * HID + start
                        LOADS.append((b1_sb[0:n, k:k + 1], b_1[l, a:a + n].unsqueeze(1)))

            @block.sync
            def _(sp):
                for dst, src in LOADS:
                    sp.dma_start(dst, src).then_inc(s["loaded"], 16)
                sp.dma_start(wo0[:, :].rearrange("p (c n) -> p c n", n=P),
                             w_o0.rearrange("(c p) n -> p c n", p=P)).then_inc(s["loaded"], 16)
                for q in range(4):
                    sp.dma_start(x_all[:, q * 1024:(q + 1) * 1024].rearrange("p (t f) -> p t f", f=P),
                                 x_in.rearrange("b (t p) f -> p (b t) f", p=P)[:, 8 * q:8 * q + 8, :]
                                 ).then_inc(s["loaded"], 16)
                sp.wait_ge(s["zeros"], 1)
                sp.dma_start(slots_in.rearrange("(p r) f -> p (r f)", p=P), zeros[:, :]).then_inc(s["cleared"], 16)
                sp.wait_ge(s["cleared"], 16)
                sp.wait_ge(s["loaded"], 16 * (len(LOADS) + 5))

            @block.gpsimd
            def _(gp):
                nc.gpsimd.memset(minus_half[:, :], -0.5)

            @block.vector
            def _(dve):
                nc.vector.memset(zeros[:, :], 0.0).then_inc(s["zeros"], 1)
                nc.vector.memset(wq0s[:, :], 0.0).then_inc(s["zeros"], 1)
                nc.vector.memset(wk0s[:, :], 0.0).then_inc(s["zeros"], 1)
                dve.wait_ge(s["loaded"], 16 * (len(LOADS) + 5))
                nc.vector.tensor_copy(causal16[:, :], cst[:, C_CAUSAL:C_CAUSAL + P])
                nc.vector.tensor_copy(causalT16[:, :], cst[:, C_CAUSALT:C_CAUSALT + P])
                nc.vector.tensor_copy(band16[:, :], cst[:, C_BAND:C_BAND + P + WIN])
                nc.vector.tensor_copy(bandT16[:, :], cst[:, C_BANDT:C_BANDT + P + WIN])
                nc.vector.tensor_copy(ident16[:, :], ident)
                dve.wait_ge(s["zeros"], 3)
                for dst, src in ((wq0s, wq0), (wk0s, wk0)):
                    nc.vector.tensor_copy(dst[:, :].rearrange("p (h c) -> p h c", c=32)[:, :, 0:DK0],
                                          src[:, :].rearrange("p (h c) -> p h c", c=DK0))
                nc.vector.tensor_copy(w_gates[:, :].rearrange("p (g d) -> p g d", d=DH1),
                                      gates_in[:, :].unsqueeze(2).to_broadcast([P, 3 * H1, DH1]))
                nc.vector.tensor_copy(select16[:, :].rearrange("p (h d) -> p h d", d=P),
                                      cst[0:3 * H2, C_SEL:C_SEL + H2].unsqueeze(2).to_broadcast([3 * H2, H2, P]))
                for l in range(DEPTH):
                    to = w_swap[:, l * 1024:(l + 1) * 1024].rearrange("p (h r d) -> p h r d", r=2, d=32)
                    src = wqkv[:, l * 1536:l * 1536 + 1024].rearrange("p (h r d) -> p h r d", r=2, d=32)
                    for r in range(2):
                        nc.vector.tensor_copy(to[:, :, r, :], src[:, :, 1 - r, :])
                    for n in range(4):
                        nc.vector.tensor_scalar(tables[:, (4 * l + n) * T:(4 * l + n + 1) * T],
                                                rotary[:, n * T:(n + 1) * T], scales_in[:, 4 * l + n:4 * l + n + 1],
                                                None, ALU.mult)
                nc.vector.memset(eps[:, 0:1], 1e-5)
                nc.vector.memset(eps[:, 1:2], 1e-6)
        end_phase()

        s = phase("stats moments variance rstd normed kept transposed T_copied T_kept logits logits_kept".split())
        with nc.Fori(0, B) as b:
            with nc.Block() as block:
                @block.vector
                def _(dve):
                    layer_norm_steps(nc, s, dve, lambda t: x_all[:, bass.ds(b * T + t * P, P)], stats, moments,
                                     var_eps, rstd, lambda t: xn_b[:, t * P:(t + 1) * P])
                    dve.wait_ge(s["logits"], NT)
                    nc.vector.tensor_copy(logits_all[:, bass.ds(b * NT * NE, NT * NE)],
                                          bank(1, 0, NT * NE)).then_inc(s["logits_kept"], 1)

                @block.gpsimd
                def _(gp):
                    gp.wait_ge(s["variance"], 1)
                    nc.gpsimd.tensor_tensor(rstd[:, :], var_eps[:, :], minus_half[:, :], ALU.pow).then_inc(s["rstd"], 1)
                    gp.wait_ge(s["normed"], NT)
                    nc.gpsimd.tensor_copy(xn_all[:, bass.ds(b * T, T)], xn_b[:, :]).then_inc(s["kept"], 1)
                    gp.wait_ge(s["T_copied"], 1)
                    nc.gpsimd.tensor_copy(xnT_all[:, bass.ds(b * T, T)], xnT_b[:, :]).then_inc(s["T_kept"], 1)

                @block.tensor
                def _(pe):
                    for t in range(NT):
                        pe.wait_ge(s["normed"], t + 1)
                        nc.tensor.transpose(bank(0, t * P, (t + 1) * P), xn_b[:, t * P:(t + 1) * P],
                                            ident).then_inc(s["transposed"], 1)
                    pe.wait_ge(s["T_copied"], 1)
                    for t in range(NT):
                        nc.tensor.matmul(bank(1, t * NE, (t + 1) * NE), xnT_b[:, t * P:(t + 1) * P], wg[:, :],
                                         start=True, stop=True).then_inc(s["logits"], 1)

                @block.scalar
                def _(act):
                    act.wait_ge(s["transposed"], NT)
                    nc.scalar.copy(xnT_b[:, :], bank(0)).then_inc(s["T_copied"], 1)
            end_phase()

        N8 = NTILE * NE
        top = sb0("top", N8)
        top_i = sb0("top_i", N8, U32)
        choice = sb0("choice", 2 * NTILE)
        oh = sb0("oh", 2 * N8)
        both = sb0("both", N8)
        expo = sb0("expo", N8)
        gap2 = sb0("gap2", NTILE)
        wsum = sb0("wsum", NTILE)
        ranked = sb0("ranked", N8)
        tot = sb0("tot", N8)
        cum = sb0("cum", N8)
        prod = sb0("prod", 2 * N8)
        pos = sb0("pos", 2 * NTILE)
        valid = sb0("valid", 2 * NTILE)
        slot_f = sb0("slot_f", 2 * NTILE)
        past = sb0("past", 2 * NTILE)
        slot_to = sb0("slot_to", 2 * NTILE, U32)

        def te(ap):
            return ap.rearrange("p (t e) -> p t e", e=NE)

        s = phase("top index choice onehot both shifted expo wsum inverse weight counts totals cum rank prod pos "
                  "valid slot".split())
        with nc.Block() as block:
            @block.vector
            def _(dve):
                for n in range(NTILE):
                    nc.vector.max(top[:, n * NE:(n + 1) * NE], logits_all[:, n * NE:(n + 1) * NE]).then_inc(s["top"], 1)
                for n in range(NTILE):
                    dve.wait_ge(s["top"], n + 1)
                    nc.vector.max_index(top_i[:, n * NE:(n + 1) * NE], top[:, n * NE:(n + 1) * NE],
                                        logits_all[:, n * NE:(n + 1) * NE]).then_inc(s["index"], 1)
                dve.wait_ge(s["index"], NTILE)
                for k in range(2):
                    nc.vector.tensor_copy(choice[:, k * NTILE:(k + 1) * NTILE],
                                          te(top_i[:, :])[:, :, k]).then_inc(s["choice"], 1)
                dve.wait_ge(s["choice"], 2)
                for k in range(2):
                    nc.vector.tensor_tensor(
                        te(oh[:, k * N8:(k + 1) * N8]),
                        cst[:, C_IOTA:C_IOTA + NE].unsqueeze(1).to_broadcast([P, NTILE, NE]),
                        choice[:, k * NTILE:(k + 1) * NTILE].unsqueeze(2).to_broadcast([P, NTILE, NE]),
                        ALU.is_equal).then_inc(s["onehot"], 1)
                dve.wait_ge(s["onehot"], 2)
                nc.vector.tensor_tensor(both[:, :], oh[:, 0:N8], oh[:, N8:2 * N8], ALU.add).then_inc(s["both"], 1)
                nc.vector.tensor_tensor(te(expo[:, :]), te(logits_all[:, :]),
                                        te(top[:, :])[:, :, 0].unsqueeze(2).to_broadcast([P, NTILE, NE]),
                                        ALU.subtract).then_inc(s["shifted"], 1)
                nc.vector.tensor_tensor(gap2[:, :], te(top[:, :])[:, :, 1], te(top[:, :])[:, :, 0],
                                        ALU.subtract).then_inc(s["shifted"], 1)
                dve.wait_ge(s["expo"], 2)
                nc.vector.reduce_sum(wsum[:, :], te(expo[:, :]), AX_X).then_inc(s["wsum"], 1)
                dve.wait_ge(s["wsum"], 1)
                nc.vector.reciprocal(wsum[:, :], wsum[:, :]).then_inc(s["inverse"], 1)
                dve.wait_ge(s["totals"], 1)
                nc.vector.tensor_copy(tot[:, :], bank(1, 0, N8)).then_inc(s["counts"], 1)
                dve.wait_ge(s["counts"], 1)
                for e in range(NE):
                    nc.vector.tensor_tensor_scan(te(cum[:, :])[:, :, e], cst[:, C_ONES:C_ONES + NTILE],
                                                 te(tot[:, :])[:, :, e], 0.0, ALU.mult, ALU.add).then_inc(s["cum"], 1)
                dve.wait_ge(s["cum"], NE)
                nc.vector.tensor_tensor(ranked[:, :], cum[:, :], tot[:, :], ALU.subtract).then_inc(s["rank"], 1)
                dve.wait_ge(s["rank"], 1)
                nc.vector.tensor_tensor(ranked[:, :], ranked[:, :], bank(0, 0, N8), ALU.add).then_inc(s["rank"], 1)
                dve.wait_ge(s["rank"], 2)
                for k in range(2):
                    nc.vector.tensor_tensor(prod[:, k * N8:(k + 1) * N8], oh[:, k * N8:(k + 1) * N8], ranked[:, :],
                                            ALU.mult).then_inc(s["prod"], 1)
                dve.wait_ge(s["prod"], 2)
                nc.vector.reduce_sum(pos[:, :], te(prod[:, :]), AX_X).then_inc(s["pos"], 1)
                dve.wait_ge(s["pos"], 1)
                nc.vector.tensor_scalar(valid[:, :], pos[:, :], float(CAP), None, ALU.is_lt).then_inc(s["valid"], 1)
                dve.wait_ge(s["valid"], 1)
                weight = route_w[:, :].rearrange("p (t k) -> p t k", k=2)
                nc.vector.tensor_tensor(weight[:, :, 0], wsum[:, :], valid[:, 0:NTILE], ALU.mult)
                nc.vector.tensor_tensor(gap2[:, :], gap2[:, :], wsum[:, :], ALU.mult).then_inc(s["weight"], 1)
                dve.wait_ge(s["weight"], 1)
                nc.vector.tensor_tensor(weight[:, :, 1], gap2[:, :], valid[:, NTILE:2 * NTILE], ALU.mult)
                nc.vector.scalar_tensor_tensor(slot_f[:, :], choice[:, :], float(CAP), pos[:, :],
                                               ALU.mult, ALU.add).then_inc(s["slot"], 1)
                nc.vector.tensor_scalar(past[:, :], valid[:, :], -65536.0, 65536.0, ALU.mult, ALU.add).then_inc(s["slot"], 1)
                dve.wait_ge(s["slot"], 2)
                nc.vector.tensor_tensor(slot_to[:, :], slot_f[:, :], past[:, :], ALU.add).then_inc(s["slot"], 1)
                nc.vector.tensor_tensor(slot_from[:, :].rearrange("p (t k) -> p t k", k=2),
                                        slot_f[:, :].rearrange("p (k t) -> p t k", k=2),
                                        valid[:, :].rearrange("p (k t) -> p t k", k=2), ALU.mult).then_inc(s["slot"], 1)

            @block.scalar
            def _(act):
                act.wait_ge(s["shifted"], 2)
                nc.scalar.activation(expo[:, :], expo[:, :], ACT.Exp).then_inc(s["expo"], 1)
                nc.scalar.activation(gap2[:, :], gap2[:, :], ACT.Exp).then_inc(s["expo"], 1)

            @block.tensor
            def _(pe):
                pe.wait_ge(s["both"], 1)
                nc.tensor.matmul(bank(0, 0, N8), cst[:, C_USTRICT:C_USTRICT + P], both[:, :], start=True, stop=True)
                nc.tensor.matmul(bank(1, 0, N8), cst[:, C_ONES:C_ONES + P], both[:, :],
                                 start=True, stop=True).then_inc(s["totals"], 1)

            @block.gpsimd
            def _(gp):
                gp.wait_ge(s["slot"], 4)
                for n in range(NTILE):
                    for k in range(2):
                        nc.gpsimd.indirect_dma_start(
                            out=slots_in, out_offset=bass.IndirectOffsetOnAxis(
                                ap=slot_to[:, k * NTILE + n:k * NTILE + n + 1], axis=0),
                            in_=xn_all[:, n * P:(n + 1) * P], in_offset=None,
                            bounds_check=NE * CAP - 1, oob_is_err=False).then_inc(scattered, 16)
                gp.wait_ge(scattered, 16 * 2 * NTILE)
        end_phase()

        wfc = sb0("wfc", 4 * HC)
        wpr = sb0("wpr", 2 * P, F32, HC)
        rows = sb0("rows", T)
        rowsT = sb0("rowsT", T)
        silu_a = sb0("silu_a", 2 * T, F32, HC)
        gated = sb0("gated", 2 * T, F32, HC)
        rows_out = sb0("rows_out", T)
        s = phase("loaded transposed T_copied hidden silu gated projected copied stored".split())
        with nc.Fori(0, NE) as e:
            with nc.Block() as block:
                @block.sync
                def _(sp):
                    sp.dma_start(rows[:, :].rearrange("p (t f) -> p t f", f=P),
                                 slots_in[bass.ds(e * CAP, CAP), :].rearrange("(t p) f -> p t f", p=P)
                                 ).then_inc(s["loaded"], 16)
                    sp.dma_start(wfc[:, :], c_fc[bass.ds(e * P, P), :]).then_inc(s["loaded"], 16)
                    sp.dma_start(wpr[:, :].rearrange("p (c n) -> p c n", n=P),
                                 c_proj[bass.ds(e * HALF, HALF), :].rearrange("(c p) n -> p c n", p=HC)
                                 ).then_inc(s["loaded"], 16)
                    sp.wait_ge(s["copied"], 1)
                    sp.dma_start(slots_out[bass.ds(e * CAP, CAP), :].rearrange("(t p) f -> p t f", p=P),
                                 rows_out[:, :].rearrange("p (t f) -> p t f", f=P)).then_inc(s["stored"], 16)
                    sp.wait_ge(s["stored"], 16)

                @block.tensor
                def _(pe):
                    pe.wait_ge(s["loaded"], 48)
                    for t in range(NT):
                        nc.tensor.transpose(bank(0, t * P, (t + 1) * P), rows[:, t * P:(t + 1) * P],
                                            ident).then_inc(s["transposed"], 1)
                    pe.wait_ge(s["T_copied"], 1)
                    for c in (0, 2, 1, 3):
                        nc.tensor.matmul(PS[0:HC, BANK * (1 + c):BANK * (2 + c)], wfc[:, c * HC:(c + 1) * HC],
                                         rowsT[:, :], start=True, stop=True).then_inc(s["hidden"], 1)
                    pe.wait_ge(s["gated"], 2)
                    for t in range(NT):
                        for c in range(2):
                            nc.tensor.matmul(bank(5, t * P, (t + 1) * P), gated[:, c * T + t * P:c * T + (t + 1) * P],
                                             wpr[:, c * P:(c + 1) * P], start=(c == 0), stop=(c == 1)
                                             ).then_inc(s["projected"], 1)

                @block.scalar
                def _(act):
                    for c in range(2):
                        act.wait_ge(s["hidden"], 1 + 2 * c)
                        nc.scalar.activation(silu_a[:, c * T:(c + 1) * T], PS[0:HC, BANK * (1 + c):BANK * (2 + c)],
                                             ACT.Silu).then_inc(s["silu"], 1)

                @block.vector
                def _(dve):
                    dve.wait_ge(s["transposed"], NT)
                    nc.vector.tensor_copy(rowsT[:, :], bank(0)).then_inc(s["T_copied"], 1)
                    for c in range(2):
                        dve.wait_ge(s["silu"], c + 1)
                        dve.wait_ge(s["hidden"], 2 + 2 * c)
                        nc.vector.tensor_tensor(gated[:, c * T:(c + 1) * T], silu_a[:, c * T:(c + 1) * T],
                                                PS[0:HC, BANK * (3 + c):BANK * (4 + c)], ALU.mult
                                                ).then_inc(s["gated"], 1)
                    dve.wait_ge(s["projected"], 2 * NT)
                    nc.vector.tensor_copy(rows_out[:, :], bank(5)).then_inc(s["copied"], 1)
            end_phase()

        before.close()
        x1 = sb("x1", NT * P)

        def sb1(name, cols, dt=F32, rows=P):
            return layer0.enter_context(nc.sbuf_tensor(name, [rows, cols], dt))

        layer0 = ctx.enter_context(ExitStack())
        qS = sb1("qS", G0 * T)
        kS = sb1("kS", G0 * T)
        v_ext = sb1("v_ext", NT * H0 * (DV0 + 1))
        row_max = sb1("row_max", NT * H0)
        max_spread = sb1("max_spread", NT * G0 * P)
        probsT = sb1("probsT", 2 * 1280)
        inv_sum = sb1("inv_sum", 2 * NT)
        ctx0 = sb1("ctx0", NT * H0 * DV0)
        ctx0T = sb1("ctx0T", 8 * T)
        from_b = sb1("from_b", 2 * NT, U32)
        weight_b = sb1("weight_b", 2 * NT)
        picked = sb1("picked", 2 * NT * P)
        moe = sb1("moe", NT * P)
        REGION = {0: 0, 1: 512, 3: 896, 2: 1024}
        QREGION = {3: 0, 2: 512, 0: 896, 1: 1024}

        scale0 = 1.0 / float(np.sqrt(DK0))
        with nc.Fori(0, B) as b:
            s = phase("ones xT_b from_b weight_b qk q_copied k_copied v v_copied_act v_copied_dve scores max max_spread maxT max_added "
                      "scoresT probs context inverse context_kept ctxT ctxT_act ctxT_dve attn moe_half moe silu "
                      "gated x1".split())
            with nc.Block() as block:
                @block.gpsimd
                def _(gp):
                    nc.gpsimd.tensor_copy(from_b[:, :], slot_from[:, bass.ds(b * 2 * NT, 2 * NT)]).then_inc(s["from_b"], 1)
                    gp.wait_ge(s["from_b"], 1)
                    for n in range(2 * NT):
                        nc.gpsimd.indirect_dma_start(
                            out=picked[:, n * P:(n + 1) * P], out_offset=None, in_=slots_out,
                            in_offset=bass.IndirectOffsetOnAxis(ap=from_b[:, n:n + 1], axis=0),
                            bounds_check=NE * CAP - 1, oob_is_err=False).then_inc(gathered, 16)

                @block.tensor
                def _(pe):
                    pe.wait_ge(s["xT_b"], 1)
                    for g in range(G0):
                        nc.tensor.matmul(bank(g), wq0s[:, g * P:(g + 1) * P], xnT_b[:, :], start=True,
                                         stop=True).then_inc(s["qk"], 1)
                        nc.tensor.matmul(bank(4 + g), wk0s[:, g * P:(g + 1) * P], xnT_b[:, :], start=True,
                                         stop=True).then_inc(s["qk"], 1)
                    for t in range(NT):
                        for half in range(2):
                            if half == 0:
                                pe.wait_ge(s["q_copied"], t + 1)
                            else:
                                pe.wait_ge(s["k_copied"], t + 1)
                            nc.tensor.matmul(bank(4 * half + t), xnT_b[:, t * P:(t + 1) * P],
                                             wv0[:, half * 512:(half + 1) * 512], start=True, stop=True
                                             ).then_inc(s["v"], 1)
                    pe.wait_ge(s["v_copied_act"], NT)
                    pe.wait_ge(s["v_copied_dve"], NT)
                    for h in range(H0):
                        g, r = h // 4, 32 * (h % 4)
                        if h >= 2:
                            pe.wait_ge(s["max"], 4 * (h - 1))
                        base = 1536 * (h % 2)
                        for i in (3, 2, 0, 1):
                            a = base + QREGION[i]
                            nc.tensor.matmul(PS[:, a:a + (i + 1) * P], qS[r:r + DK0, g * T + i * P:g * T + (i + 1) * P],
                                             kS[r:r + DK0, g * T:g * T + (i + 1) * P], start=True, stop=False)
                            nc.tensor.matmul(PS[:, a + i * P:a + (i + 1) * P], ident16[:, :], causal16[:, :],
                                             start=False, stop=True).then_inc(s["scores"], 1)
                    pe.wait_ge(s["max_spread"], 1)
                    for g in range(G0):
                        for i in range(NT):
                            nc.tensor.transpose(bank(g, i * P, (i + 1) * P),
                                                max_spread[:, (i * G0 + g) * P:(i * G0 + g + 1) * P],
                                                ident).then_inc(s["maxT"], 1)
                    pe.wait_ge(s["max_added"], G0)

                    def scores_T(h):
                        g, r = h // 4, 32 * (h % 4)
                        base = 1536 * (h % 2)
                        if h >= 2:
                            pe.wait_ge(s["probs"], h - 1)
                        for j in (0, 1, 3, 2):
                            a = base + REGION[j]
                            n = T - j * P
                            nc.tensor.matmul(PS[:, a:a + n], kS[r:r + DK0 + 1, g * T + j * P:g * T + (j + 1) * P],
                                             qS[r:r + DK0 + 1, g * T + j * P:(g + 1) * T], start=True, stop=False)
                            last = nc.tensor.matmul(PS[:, a:a + P], ident16[:, :], causalT16[:, :],
                                                    start=False, stop=True)
                        last.then_inc(s["scoresT"], 1)

                    def context(h):
                        pe.wait_ge(s["probs"], h + 1)
                        if h >= 2:
                            pe.wait_ge(s["context_kept"], h - 1)
                        for i in range(NT):
                            for j in range(i + 1):
                                a = 1280 * (h % 2) + REGION[j] + (i - j) * P
                                c = (j * H0 + h) * (DV0 + 1)
                                last = nc.tensor.matmul(bank(6 + h % 2, i * 65, i * 65 + 65), probsT[:, a:a + P],
                                                        v_ext[:, c:c + DV0 + 1], start=(j == 0), stop=(j == i))
                        last.then_inc(s["context"], 1)

                    for h in range(H0 + 1):
                        if h < H0:
                            scores_T(h)
                        if h >= 1:
                            context(h - 1)
                    pe.wait_ge(s["context_kept"], H0)
                    for c in range(8):
                        for t in range(NT):
                            nc.tensor.transpose(bank(c, t * P, (t + 1) * P),
                                                ctx0[:, t * 1024 + c * P:t * 1024 + (c + 1) * P], ident
                                                ).then_inc(s["ctxT"], 1)
                    pe.wait_ge(s["ctxT_act"], 4)
                    pe.wait_ge(s["ctxT_dve"], 4)
                    for t in range(NT):
                        for c in range(8):
                            last = nc.tensor.matmul(bank(0, t * P, (t + 1) * P), ctx0T[:, c * T + t * P:c * T + (t + 1) * P],
                                                    wo0[:, c * P:(c + 1) * P], start=(c == 0), stop=(c == 7))
                    last.then_inc(s["attn"], 1)

                v_view = v_ext[:, :].rearrange("p (t h d) -> p t h d", t=NT, d=DV0 + 1)

                @block.scalar
                def _(act):
                    nc.scalar.copy(xnT_b[:, :], xnT_all[:, bass.ds(b * T, T)]).then_inc(s["xT_b"], 1)
                    for g in range(G0):
                        act.wait_ge(s["qk"], 2 * g + 1)
                        nc.scalar.copy(qS[:, g * T:(g + 1) * T], bank(g)).then_inc(s["q_copied"], 1)
                    act.wait_ge(s["ones"], 1)
                    for t in range(NT):
                        act.wait_ge(s["v"], 2 * t + 1)
                        nc.scalar.copy(v_view[:, t, 0:8, 0:DV0],
                                       bank(t).rearrange("p (h d) -> p h d", d=DV0)).then_inc(s["v_copied_act"], 1)
                    for h in range(H0):
                        act.wait_ge(s["scoresT"], h + 1)
                        if h >= 2:
                            act.wait_ge(s["context"], h - 1)
                        base = 1536 * (h % 2)
                        nc.scalar.activation(probsT[:, 1280 * (h % 2):1280 * (h % 2 + 1)], PS[:, base:base + 1280],
                                             ACT.Exp, scale=scale0).then_inc(s["probs"], 1)
                    for c in range(0, 8, 2):
                        act.wait_ge(s["ctxT"], NT * (c + 1))
                        nc.scalar.copy(ctx0T[:, c * T:(c + 1) * T], bank(c)).then_inc(s["ctxT_act"], 1)
                    act.wait_ge(s["moe"], NT)
                    nc.scalar.activation(moe[:, :], moe[:, :], ACT.Silu).then_inc(s["silu"], 1)

                @block.vector
                def _(dve):
                    nc.vector.memset(v_ext[:, :], 1.0).then_inc(s["ones"], 1)
                    nc.vector.memset(max_spread[:, :], 0.0).then_inc(s["ones"], 1)
                    nc.vector.tensor_copy(weight_b[:, :], route_w[:, bass.ds(b * 2 * NT, 2 * NT)]).then_inc(s["weight_b"], 1)
                    for g in range(G0):
                        dve.wait_ge(s["qk"], 2 * g + 2)
                        nc.vector.tensor_scalar(kS[:, g * T:(g + 1) * T], bank(4 + g), cst[:, C_KONE:C_KONE + 1], None,
                                                ALU.add).then_inc(s["k_copied"], 1)
                    dve.wait_ge(s["ones"], 2)
                    for t in range(NT):
                        dve.wait_ge(s["v"], 2 * t + 2)
                        nc.vector.tensor_copy(v_view[:, t, 8:16, 0:DV0],
                                              bank(4 + t).rearrange("p (h d) -> p h d", d=DV0)
                                              ).then_inc(s["v_copied_dve"], 1)
                    for h in range(H0):
                        base = 1536 * (h % 2)
                        for n, i in enumerate((3, 2, 0, 1)):
                            dve.wait_ge(s["scores"], 4 * h + (1, 3, 3, 4)[n])
                            a = base + QREGION[i]
                            nc.vector.reduce_max(row_max[:, i * H0 + h:i * H0 + h + 1], PS[:, a:a + (i + 1) * P],
                                                 AX_X).then_inc(s["max"], 1)
                    dve.wait_ge(s["max"], 4 * H0)
                    nc.vector.tensor_scalar(max_spread[:, :].rearrange("p (m c) -> p m c", c=32)[:, :, DK0],
                                            row_max[:, :], -1.0, None, ALU.mult).then_inc(s["max_spread"], 1)
                    for g in range(G0):
                        dve.wait_ge(s["maxT"], NT * (g + 1))
                        nc.vector.tensor_tensor(qS[:, g * T:(g + 1) * T], qS[:, g * T:(g + 1) * T], bank(g),
                                                ALU.add).then_inc(s["max_added"], 1)
                    for h in range(H0):
                        dve.wait_ge(s["context"], h + 1)
                        o = bank(6 + h % 2, 0, NT * 65).rearrange("p (t d) -> p t d", d=65)
                        inv = inv_sum[:, (h % 2) * NT:(h % 2 + 1) * NT]
                        if h >= 2:
                            dve.wait_ge(s["context_kept"], h - 1)
                        nc.vector.reciprocal(inv, o[:, :, DV0]).then_inc(s["inverse"], 1)
                        dve.wait_ge(s["inverse"], h + 1)
                        nc.vector.tensor_tensor(
                            ctx0[:, :].rearrange("p (t h d) -> p t h d", t=NT, d=DV0)[:, :, h, :], o[:, :, 0:DV0],
                            inv.unsqueeze(2).to_broadcast([P, NT, DV0]), ALU.mult).then_inc(s["context_kept"], 1)
                    for c in range(1, 8, 2):
                        dve.wait_ge(s["ctxT"], NT * (c + 1))
                        nc.vector.tensor_copy(ctx0T[:, c * T:(c + 1) * T], bank(c)).then_inc(s["ctxT_dve"], 1)
                    dve.wait_ge(s["weight_b"], 1)
                    dve.wait_ge(gathered, b * (16 * 2 * NT) + 16 * 2 * NT)
                    for t in range(NT):
                        nc.vector.tensor_scalar(moe[:, t * P:(t + 1) * P], picked[:, 2 * t * P:(2 * t + 1) * P],
                                                weight_b[:, 2 * t:2 * t + 1], None, ALU.mult).then_inc(s["moe_half"], 1)
                    for t in range(NT):
                        dve.wait_ge(s["moe_half"], t + 1)
                        nc.vector.scalar_tensor_tensor(moe[:, t * P:(t + 1) * P], picked[:, (2 * t + 1) * P:(2 * t + 2) * P],
                                                       weight_b[:, 2 * t + 1:2 * t + 2], moe[:, t * P:(t + 1) * P],
                                                       ALU.mult, ALU.add).then_inc(s["moe"], 1)
                    dve.wait_ge(s["silu"], 1)
                    dve.wait_ge(s["attn"], 1)
                    nc.vector.tensor_tensor(x1[:, :], bank(0), moe[:, :], ALU.mult).then_inc(s["gated"], 1)
                    dve.wait_ge(s["gated"], 1)
                    nc.vector.tensor_tensor(x1[:, :], x1[:, :], x_all[:, bass.ds(b * T, T)], ALU.add).then_inc(s["x1"], 1)
            end_phase()
            layer0.close()

            layer1 = ctx.enter_context(ExitStack())

            def sb2(name, cols, dt=F32, rows=P):
                return layer1.enter_context(nc.sbuf_tensor(name, [rows, cols], dt))

            s1 = sb2("s1", T)

            s = phase("stats moments variance rstd normed transposed T_copied".split())
            with nc.Block() as block:
                @block.vector
                def _(dve):
                    layer_norm_steps(nc, s, dve, lambda t: x1[:, t * P:(t + 1) * P], stats, moments,
                                     var_eps, rstd, lambda t: xn_b[:, t * P:(t + 1) * P])

                @block.gpsimd
                def _(gp):
                    gp.wait_ge(s["variance"], 1)
                    nc.gpsimd.tensor_tensor(rstd[:, :], var_eps[:, :], minus_half[:, :], ALU.pow).then_inc(s["rstd"], 1)

                @block.tensor
                def _(pe):
                    for t in range(NT):
                        pe.wait_ge(s["normed"], t + 1)
                        nc.tensor.transpose(bank(0, t * P, (t + 1) * P), xn_b[:, t * P:(t + 1) * P],
                                            ident).then_inc(s["transposed"], 1)

                @block.scalar
                def _(act):
                    act.wait_ge(s["transposed"], NT)
                    nc.scalar.copy(xnT_b[:, :], bank(0)).then_inc(s["T_copied"], 1)
            end_phase()

            delta = ctx.enter_context(ExitStack())

            def sb3(name, cols, dt=F32, rows=P):
                return delta.enter_context(nc.sbuf_tensor(name, [rows, cols], dt))

            padded = sb3("padded", 3 * (T + 4))
            conv = sb3("conv", 3 * T)
            beta = sb3("beta", T)
            decay = sb3("decay", T)
            keep_in = sb3("keep_in", T)
            mix = sb3("mix", T)
            squares = sb3("squares", 2 * T)
            norm = sb3("norm", 2 * T)
            qk_n = sb3("qk_n", 2 * T)
            scaled = sb3("scaled", 2 * T)
            ema_in = sb3("ema_in", T)
            ema = sb3("ema", T)
            rows3 = sb3("rows3", 3 * T)
            low = sb3("low", 3 * T)
            inv_t = sb3("inv_t", 2 * T)
            level = sb3("level", T)
            product = sb3("product", T)
            uw = sb3("uw", 2 * T)
            u_new = sb3("u_new", P)
            state = sb3("state", 2 * P)
            out1 = sb3("out1", T)
            diff = sb3("diff", T)
            NCH = T // CH

            def mask(n):
                a = C_DELTA + n * CH
                return cst[:, a:a + CH].unsqueeze(1).to_broadcast([P, NCH, CH])

            def g32(ap):
                return ap.rearrange("p (n j) -> p n j", j=CH)

            def chunks():
                for n in range(NCH):
                    t, c = divmod(n, 4)
                    for h in range(H1):
                        yield slice(32 * c, 32 * c + 32), (t * H1 + h) * CH, slice(32 * h, 32 * h + 32), n * CH, \
                            t * P + h * DH1

            s = phase("pads qkv pad_copied conv silu gates sigmoid squares sumsq root inverse qk_n scaled ema_in ema "
                      "rowsT rows_act rows_dve kk low inv level product product_copied updated added uw_mm uw_act uw_dve "
                      "w_state u_new s_updated s_copied out_mm diff mixed out1 o_sq o_ms o_root o_inverse o_final "
                      "s1_mm s1".split())
            with nc.Block() as block:
                @block.tensor
                def _(pe):
                    for n, w in enumerate((wq1, wk1, wv1)):
                        nc.tensor.matmul(bank(n), w[:, :], xnT_b[:, :], start=True, stop=True).then_inc(s["qkv"], 1)
                    for n in range(3):
                        pe.wait_ge(s["pad_copied"], n + 1)
                        nc.tensor.matmul(bank(n), w_gates[:, n * P:(n + 1) * P], xnT_b[:, :], start=True,
                                         stop=True).then_inc(s["gates"], 1)
                    for n in range(2):
                        pe.wait_ge(s["squares"], n + 1)
                        pe.wait_ge(s["sigmoid"], 4)
                        nc.tensor.matmul(bank(n), cst[:, C_BLK32:C_BLK32 + P], squares[:, n * T:(n + 1) * T],
                                         start=True, stop=True).then_inc(s["sumsq"], 1)
                    pe.wait_ge(s["root"], 2)
                    for n in range(3):
                        src = (qk_n[:, T:2 * T], scaled[:, 0:T], scaled[:, T:2 * T])[n]
                        if n == 0:
                            pe.wait_ge(s["qk_n"], 2)
                        else:
                            pe.wait_ge(s["scaled"], n)
                        for t in range(NT):
                            nc.tensor.transpose(bank(n, t * P, (t + 1) * P), src[:, t * P:(t + 1) * P],
                                                ident).then_inc(s["rowsT"], 1)
                    pe.wait_ge(s["rows_act"], 2)
                    pe.wait_ge(s["rows_dve"], 1)
                    pairs = ((scaled, 0, qk_n, T), (qk_n, T, scaled, 0), (qk_n, T, qk_n, 0))
                    for n, (a, ao, b_, bo) in enumerate(pairs):
                        for rc, blk, rh, tok, _ in chunks():
                            o = BANK * (rh.start // 32) + n * P + tok // P * CH
                            last = nc.tensor.matmul(PS[rc, o:o + CH],
                                                    a[rh, ao + tok:ao + tok + CH], b_[rh, bo + tok:bo + tok + CH],
                                                    start=True, stop=True, tile_position=(rh.start, rc.start))
                        last.then_inc(s["kk"], 1)
                    for l in range(4):
                        pe.wait_ge(s["level"], l + 1)
                        pe.wait_ge(s["added"], 2 * l + 2)
                        for rc, blk, _, _, _ in chunks():
                            last = nc.tensor.matmul(PS[rc, blk:blk + CH], level[rc, blk:blk + CH],
                                                    inv_t[rc, blk:blk + CH], start=True, stop=True,
                                                    tile_position=(rc.start, rc.start))
                        last.then_inc(s["product"], 1)
                        pe.wait_ge(s["product_copied"], l + 1)
                        for n in ((1, 2) if l < 3 else (2,)):
                            for rc, blk, _, _, _ in chunks():
                                a = inv_t[rc, T + blk:T + blk + CH] if n == 1 else product[rc, blk:blk + CH]
                                r = product[rc, blk:blk + CH] if n == 1 else inv_t[rc, T + blk:T + blk + CH]
                                last = nc.tensor.matmul(PS[rc, BANK * n + blk:BANK * n + blk + CH], a, r,
                                                        start=True, stop=True, tile_position=(rc.start, rc.start))
                            last.then_inc(s["updated"], 1)
                    pe.wait_ge(s["added"], 9)
                    for rc, blk, _, _, feat in chunks():
                        last = nc.tensor.matmul(PS[rc, blk:blk + CH], inv_t[rc, T + blk:T + blk + CH],
                                                rows3[rc, 2 * T + feat:2 * T + feat + CH], start=True, stop=True,
                                                tile_position=(rc.start, rc.start))
                    last.then_inc(s["uw_mm"], 1)
                    for rc, blk, rh, tok, feat in chunks():
                        o = BANK * (1 + rc.start // 32) + tok // P * CH
                        last = nc.tensor.matmul(PS[rh, o:o + CH], rows3[rc, T + feat:T + feat + CH],
                                                inv_t[rc, T + blk:T + blk + CH], start=True, stop=True,
                                                tile_position=(rc.start, rh.start))
                    last.then_inc(s["uw_mm"], 1)
                    pe.wait_ge(s["uw_act"], 1)
                    pe.wait_ge(s["uw_dve"], 4)
                    todo = list(chunks())
                    for n in range(NCH):
                        mine = todo[n * H1:(n + 1) * H1]
                        rc, tok = mine[0][0], mine[0][3]
                        st = state[:, (n % 2) * P:(n % 2 + 1) * P]
                        if n:
                            pe.wait_ge(s["s_copied"], n)
                            nc.tensor.matmul(PS[rc, 0:P], uw[:, T + tok:T + tok + CH], st, start=True, stop=True,
                                             tile_position=(0, rc.start)).then_inc(s["w_state"], 1)
                        pe.wait_ge(s["u_new"], n + 1)
                        t = n // 4
                        nc.tensor.matmul(bank(1, 0, P), rows3[rc, t * P:(t + 1) * P], u_new[rc, :], start=(n == 0),
                                         stop=True, tile_position=(rc.start, 0),
                                         skip_group_check=True).then_inc(s["s_updated"], 1)
                        if n:
                            nc.tensor.matmul(bank(2, tok, tok + CH), st, qk_n[:, tok:tok + CH], start=True, stop=True)
                        for h, (rc, blk, rh, tok, feat) in enumerate(mine):
                            last = nc.tensor.matmul(PS[rh, 3 * BANK + tok:3 * BANK + tok + CH],
                                                    u_new[rc, h * DH1:(h + 1) * DH1],
                                                    low[rc, 2 * T + blk:2 * T + blk + CH], start=True, stop=True,
                                                    tile_position=(rc.start, rh.start))
                        last.then_inc(s["out_mm"], 1)
                    pe.wait_ge(s["o_sq"], 1)
                    nc.tensor.matmul(bank(0), cst[:, C_BLK32:C_BLK32 + P], squares[:, 0:T], start=True,
                                     stop=True).then_inc(s["o_ms"], 1)
                    pe.wait_ge(s["o_final"], 1)
                    for t in range(NT):
                        last = nc.tensor.matmul(bank(1, t * P, (t + 1) * P), out1[:, t * P:(t + 1) * P], wo1[:, :],
                                                start=True, stop=True)
                    last.then_inc(s["s1_mm"], 1)

                @block.scalar
                def _(act):
                    act.wait_ge(s["pads"], 1)
                    for n in range(3):
                        act.wait_ge(s["qkv"], n + 1)
                        a = n * (T + 4) + 3
                        nc.scalar.copy(padded[:, a:a + T], bank(n)).then_inc(s["pad_copied"], 1)
                    act.wait_ge(s["gates"], 3)
                    nc.scalar.activation(beta[:, :], bank(0), ACT.Sigmoid).then_inc(s["sigmoid"], 1)
                    nc.scalar.activation(decay[:, :], bank(1), ACT.Sigmoid).then_inc(s["sigmoid"], 1)
                    nc.scalar.activation(keep_in[:, :], bank(1), ACT.Sigmoid, scale=-1.0).then_inc(s["sigmoid"], 1)
                    nc.scalar.activation(mix[:, :], bank(2), ACT.Sigmoid, bias=column[:, 0:1]).then_inc(s["sigmoid"], 1)
                    for n in range(3):
                        act.wait_ge(s["conv"], 4 * (n + 1))
                        nc.scalar.activation(conv[:, n * T:(n + 1) * T], conv[:, n * T:(n + 1) * T],
                                             ACT.Silu).then_inc(s["silu"], 1)
                    act.wait_ge(s["silu"], 3)
                    for n in range(2):
                        nc.scalar.square(squares[:, n * T:(n + 1) * T], conv[:, n * T:(n + 1) * T]
                                         ).then_inc(s["squares"], 1)
                    for n in range(2):
                        act.wait_ge(s["sumsq"], n + 1)
                        nc.scalar.activation(norm[:, n * T:(n + 1) * T], bank(n), ACT.Sqrt,
                                             bias=eps[:, 1:2]).then_inc(s["root"], 1)
                    for n in (0, 2):
                        act.wait_ge(s["rowsT"], NT * (n + 1))
                        nc.scalar.copy(rows3[:, n * T:(n + 1) * T], bank(n)).then_inc(s["rows_act"], 1)
                    for l in range(4):
                        act.wait_ge(s["product"], l + 1)
                        nc.scalar.copy(product[:, :], bank(0)).then_inc(s["product_copied"], 1)
                    act.wait_ge(s["uw_mm"], 1)
                    nc.scalar.copy(uw[:, 0:T], bank(0)).then_inc(s["uw_act"], 1)
                    act.wait_ge(s["mixed"], 2)
                    nc.scalar.square(squares[:, 0:T], out1[:, :]).then_inc(s["o_sq"], 1)
                    act.wait_ge(s["o_ms"], 1)
                    nc.scalar.activation(norm[:, 0:T], bank(0), ACT.Sqrt, bias=eps[:, 0:1],
                                         scale=1.0 / DH1).then_inc(s["o_root"], 1)
                    act.wait_ge(s["s1_mm"], 1)
                    nc.scalar.copy(s1[:, :], bank(1)).then_inc(s["s1"], 1)

                @block.gpsimd
                def _(gp):
                    gp.wait_ge(s["silu"], 3)
                    gp.wait_ge(s["sigmoid"], 4)
                    nc.gpsimd.tensor_tensor(ema_in[:, :], conv[:, 2 * T:3 * T], keep_in[:, :], ALU.mult
                                            ).then_inc(s["ema_in"], 1)

                @block.vector
                def _(dve):
                    nc.vector.memset(padded[:, :], 0.0).then_inc(s["pads"], 1)
                    for n in range(3):
                        a = n * (T + 4)
                        to = conv[:, n * T:(n + 1) * T]
                        dve.wait_ge(s["pad_copied"], n + 1)
                        nc.vector.tensor_scalar(to, padded[:, a:a + T], conv_w[:, 4 * n:4 * n + 1], None,
                                                ALU.mult).then_inc(s["conv"], 1)
                        for j in range(1, 4):
                            dve.wait_ge(s["conv"], 4 * n + j)
                            nc.vector.scalar_tensor_tensor(to, padded[:, a + j:a + j + T],
                                                           conv_w[:, 4 * n + j:4 * n + j + 1], to,
                                                           ALU.mult, ALU.add).then_inc(s["conv"], 1)
                    for n in range(2):
                        dve.wait_ge(s["root"], n + 1)
                        nc.vector.reciprocal(norm[:, n * T:(n + 1) * T], norm[:, n * T:(n + 1) * T]
                                             ).then_inc(s["inverse"], 1)
                        dve.wait_ge(s["inverse"], n + 1)
                        nc.vector.tensor_tensor(qk_n[:, n * T:(n + 1) * T], conv[:, n * T:(n + 1) * T],
                                                norm[:, n * T:(n + 1) * T], ALU.mult).then_inc(s["qk_n"], 1)
                    dve.wait_ge(s["qk_n"], 2)
                    nc.vector.tensor_tensor(scaled[:, 0:T], qk_n[:, T:2 * T], beta[:, :], ALU.mult
                                            ).then_inc(s["scaled"], 1)
                    nc.vector.tensor_tensor(scaled[:, T:2 * T], conv[:, 2 * T:3 * T], beta[:, :], ALU.mult
                                            ).then_inc(s["scaled"], 1)
                    dve.wait_ge(s["ema_in"], 1)
                    nc.vector.tensor_tensor_scan(ema[:, :], decay[:, :], ema_in[:, :], 0.0, ALU.mult, ALU.add
                                                 ).then_inc(s["ema"], 1)
                    dve.wait_ge(s["rowsT"], 2 * NT)
                    nc.vector.tensor_copy(rows3[:, T:2 * T], bank(1)).then_inc(s["rows_dve"], 1)
                    for n in range(3):
                        dve.wait_ge(s["kk"], 3)
                        m = C_DELTA + (D_NEGLO, D_NEGLOT, D_INCLT)[n] * CH
                        for h in range(H1):
                            nc.vector.tensor_tensor(
                                low[:, n * T:(n + 1) * T].rearrange("p (t h j) -> p t h j", h=H1, j=CH)[:, :, h, :],
                                g32(bank(h, n * P, (n + 1) * P)),
                                cst[:, m:m + CH].unsqueeze(1).to_broadcast([P, NT, CH]), ALU.mult
                            ).then_inc(s["low"], 1)
                    dve.wait_ge(s["low"], 8)
                    for n in range(2):
                        nc.vector.tensor_tensor(g32(inv_t[:, n * T:(n + 1) * T]), g32(low[:, n * T:(n + 1) * T]),
                                                mask(D_M1 + n), ALU.mult).then_inc(s["inv"], 1)
                    for n in range(2):
                        dve.wait_ge(s["inv"], n + 1)
                        nc.vector.tensor_tensor(g32(inv_t[:, n * T:(n + 1) * T]), g32(inv_t[:, n * T:(n + 1) * T]),
                                                mask(D_EYE), ALU.add).then_inc(s["added"], 1)
                    for l in range(4):
                        if l:
                            dve.wait_ge(s["product"], l)
                        nc.vector.tensor_tensor(g32(level[:, :]), g32(low[:, T:2 * T]), mask(D_M2T + l), ALU.mult
                                                ).then_inc(s["level"], 1)
                        for n in ((0, 1) if l < 3 else (1,)):
                            dve.wait_ge(s["updated"], 2 * l + n + 1 if l < 3 else 7)
                            if n == 0:
                                dve.wait_ge(s["added"], 2 * l + 2)
                            nc.vector.tensor_tensor(inv_t[:, n * T:(n + 1) * T], inv_t[:, n * T:(n + 1) * T],
                                                    bank(n + 1), ALU.add).then_inc(s["added"], 1)
                    dve.wait_ge(s["uw_mm"], 2)
                    for c in range(4):
                        nc.vector.tensor_copy(
                            uw[:, T:2 * T].rearrange("p (t c j) -> p t c j", c=4, j=CH)[:, :, c, :],
                            g32(bank(1 + c, 0, P))).then_inc(s["uw_dve"], 1)
                    block_mask = cst[:, C_BLK32:C_BLK32 + P]
                    for n in range(NCH):
                        t, c = divmod(n, 4)
                        rc = slice(32 * c, 32 * c + 32)
                        if n == 0:
                            dve.wait_ge(s["uw_act"], 1)
                            nc.vector.tensor_copy(u_new[rc, :], uw[rc, 0:P]).then_inc(s["u_new"], 1)
                        else:
                            dve.wait_ge(s["w_state"], n)
                            if n >= 4:
                                dve.wait_ge(s["out_mm"], n - 3)
                            nc.vector.tensor_tensor(u_new[rc, :], uw[rc, t * P:(t + 1) * P], PS[rc, 0:P],
                                                    ALU.subtract).then_inc(s["u_new"], 1)
                        if n < NCH - 1:
                            dve.wait_ge(s["s_updated"], n + 1)
                            if n:
                                dve.wait_ge(s["out_mm"], n)
                            a = ((n + 1) % 2) * P
                            nc.vector.tensor_tensor(state[:, a:a + P], bank(1, 0, P), block_mask, ALU.mult
                                                    ).then_inc(s["s_copied"], 1)
                    dve.wait_ge(s["out_mm"], NCH)
                    dve.wait_ge(s["ema"], 1)
                    nc.vector.tensor_copy(out1[:, :], bank(3)).then_inc(s["diff"], 1)
                    dve.wait_ge(s["diff"], 1)
                    nc.vector.tensor_tensor(out1[:, CH:T], out1[:, CH:T], bank(2, CH, T), ALU.add
                                            ).then_inc(s["diff"], 1)
                    dve.wait_ge(s["diff"], 2)
                    nc.vector.tensor_tensor(diff[:, :], ema[:, :], out1[:, :], ALU.subtract).then_inc(s["diff"], 1)
                    dve.wait_ge(s["diff"], 3)
                    nc.vector.tensor_tensor(diff[:, :], diff[:, :], mix[:, :], ALU.mult).then_inc(s["mixed"], 1)
                    dve.wait_ge(s["mixed"], 1)
                    nc.vector.tensor_tensor(out1[:, :], diff[:, :], out1[:, :], ALU.add).then_inc(s["mixed"], 1)
                    dve.wait_ge(s["o_root"], 1)
                    nc.vector.reciprocal(norm[:, 0:T], norm[:, 0:T]).then_inc(s["o_inverse"], 1)
                    dve.wait_ge(s["o_inverse"], 1)
                    nc.vector.scalar_tensor_tensor(out1[:, :], out1[:, :], column[:, 1:2], norm[:, 0:T],
                                                   ALU.mult, ALU.mult).then_inc(s["o_final"], 1)
            end_phase()
            delta.close()

            KX = P + WIN
            y = sb2("y", NT * P)
            hT = sb2("hT", T)
            v2 = sb2("v2", NT * H2 * (D2 + 1))
            f_sq = sb2("f_sq", 2 * T)
            f_norm = sb2("f_norm", 2 * T)
            f_cos = sb2("f_cos", 2 * T)
            f_sin = sb2("f_sin", 2 * T)
            f_sum = sb2("f_sum", 2 * T)
            qk2 = sb2("qk2", 8 * T)
            max2 = sb2("max2", NT * H2)
            max_rest = sb2("max_rest", NT * H2)
            max_part = sb2("max_part", NT * H2, BF16)
            max_parts = sb2("max_parts", NT * 3 * H2)
            maxT16 = sb2("maxT16", T, BF16, 3 * H2)
            probs2 = sb2("probs2", 2 * 704)
            inv2 = sb2("inv2", 2 * NT)
            ctx2 = sb2("ctx2", NT * 512)
            ctx2T = sb2("ctx2T", 4 * T)
            gelu = sb2("gelu", 2 * T)
            glu = sb2("glu", 3 * T)
            final = sb2("final", NT * P)
            Q_AT, Q_KEYS = (0, 128, 320, 512), (P, KX, KX, KX)
            K_AT, K_QUERIES = (0, 192, 512, 384), (KX, KX, KX, P)

            for l in range(DEPTH):
                s = phase("y yT shift_low shift_high ones v v_act v_dve a_mm b_mm sq ss root clip inverse cos sin sum "
                          "qk2 scores max max_neg part parts maxT maxT_copied scoresT probs context inverse2 ctx ctxT "
                          "ctxT_act ctxT_dve wo y_new yT2 shift2_low shift2_high mean dev dev_sq var root2 inverse3 "
                          "normed hidden gelu glu w2_mm y_out".split())
                with nc.Block() as block:
                    @block.gpsimd
                    def _(gp):
                        for m in range(8):
                            if m >= 2:
                                gp.wait_ge(s["qk2"], m - 1)
                            gp.wait_ge(s["sin"], m + 1)
                            k = (m % 2) * T
                            nc.gpsimd.tensor_tensor(f_sum[:, k:k + T], f_cos[:, k:k + T], f_sin[:, k:k + T],
                                                    ALU.add).then_inc(s["sum"], 1)

                    @block.tensor
                    def _(pe):
                        if l:
                            for t in range(NT):
                                nc.tensor.transpose(bank(0, t * P, (t + 1) * P), y[:, t * P:(t + 1) * P],
                                                    ident).then_inc(s["yT"], 1)
                        pe.wait_ge(s["shift_high"], 2)
                        pe.wait_ge(s["shift_low"], 1)
                        for t in range(NT):
                            nc.tensor.matmul(bank(4 + t), hT[:, t * P:(t + 1) * P],
                                             wqkv[:, l * 1536 + 1024:(l + 1) * 1536], start=True, stop=True
                                             ).then_inc(s["v"], 1)
                        for m in range(9):
                            if m < 8:
                                if m >= 2:
                                    pe.wait_ge(s["sq"], m - 1)
                                    pe.wait_ge(s["sin"], m - 1)
                                nc.tensor.matmul(bank(m % 2), wqkv[:, l * 1536 + m * P:l * 1536 + (m + 1) * P],
                                                 hT[:, :], start=True, stop=True).then_inc(s["a_mm"], 1)
                                nc.tensor.matmul(bank(2 + m % 2), w_swap[:, l * 1024 + m * P:l * 1024 + (m + 1) * P],
                                                 hT[:, :], start=True, stop=True).then_inc(s["b_mm"], 1)
                            if m == 1:
                                pe.wait_ge(s["v_act"], 2)
                                pe.wait_ge(s["v_dve"], 2)
                            if m:
                                pe.wait_ge(s["sq"], m)
                                if m >= 3:
                                    pe.wait_ge(s["root"], m - 2)
                                k = ((m - 1) % 2) * T
                                nc.tensor.matmul(bank(4 + (m - 1) % 2), cst[:, C_BLK64:C_BLK64 + P], f_sq[:, k:k + T],
                                                 start=True, stop=True).then_inc(s["ss"], 1)
                        pe.wait_ge(s["qk2"], 8)
                        for h in range(H2):
                            r = 64 * (h % 2)
                            q0, k0 = (h // 2) * T, (4 + h // 2) * T
                            base = 2 * BANK * (h % 2)
                            if h >= 2:
                                pe.wait_ge(s["max"], 3 * (h - 1))
                            for i in range(NT):
                                a, n = base + Q_AT[i], Q_KEYS[i]
                                nc.tensor.matmul(PS[:, a:a + n], qk2[r:r + D2, q0 + i * P:q0 + (i + 1) * P],
                                                 qk2[r:r + D2, k0 + (i + 1) * P - n:k0 + (i + 1) * P],
                                                 start=True, stop=False)
                                last = nc.tensor.matmul(PS[:, a:a + n], ident16[:, :], band16[:, KX - n:KX],
                                                        start=False, stop=True)
                            last.then_inc(s["scores"], 1)
                        pe.wait_ge(s["parts"], 3)
                        for i in range(NT):
                            nc.tensor.transpose(PS[0:3 * H2, 4 * BANK + i * P:4 * BANK + (i + 1) * P],
                                                max_parts[:, i * 24:(i + 1) * 24], ident).then_inc(s["maxT"], 1)
                        pe.wait_ge(s["maxT_copied"], 1)

                        def scores_T(h):
                            r = 64 * (h % 2)
                            q0, k0 = (h // 2) * T, (4 + h // 2) * T
                            base = 2 * BANK * (h % 2)
                            if h >= 2:
                                pe.wait_ge(s["probs"], h - 1)
                            for j in range(NT):
                                a, n = base + K_AT[j], K_QUERIES[j]
                                nc.tensor.matmul(PS[:, a:a + n], qk2[r:r + D2, k0 + j * P:k0 + (j + 1) * P],
                                                 qk2[r:r + D2, q0 + j * P:q0 + j * P + n], start=True, stop=False)
                                nc.tensor.matmul(PS[:, a:a + n], select16[:, h * P:(h + 1) * P],
                                                 maxT16[:, j * P:j * P + n], start=False, stop=False)
                                last = nc.tensor.matmul(PS[:, a:a + n], ident16[:, :], bandT16[:, 0:n],
                                                        start=False, stop=True)
                            last.then_inc(s["scoresT"], 1)

                        def context(h):
                            pe.wait_ge(s["probs"], h + 1)
                            if h >= 2:
                                pe.wait_ge(s["ctx"], h - 1)
                            base = 704 * (h % 2)
                            for i in range(NT):
                                o = (6 + h % 2) * BANK + i * 65
                                a = base + K_AT[i]
                                c = (i * H2 + h) * (D2 + 1)
                                last = nc.tensor.matmul(PS[:, o:o + 65], probs2[:, a:a + P], v2[:, c:c + D2 + 1],
                                                        start=True, stop=True)
                                if i:
                                    a = base + K_AT[i - 1] + P
                                    c = ((i - 1) * H2 + h) * (D2 + 1)
                                    last = nc.tensor.matmul(PS[0:WIN, o:o + 65], probs2[:, a:a + WIN],
                                                            v2[:, c:c + D2 + 1], start=False, stop=True,
                                                            skip_group_check=True)
                            last.then_inc(s["context"], 1)

                        for h in range(H2 + 1):
                            if h < H2:
                                scores_T(h)
                            if h:
                                context(h - 1)
                        pe.wait_ge(s["ctx"], H2)
                        for c in range(4):
                            for t in range(NT):
                                nc.tensor.transpose(bank(c, t * P, (t + 1) * P),
                                                    ctx2[:, t * 512 + c * P:t * 512 + (c + 1) * P], ident
                                                    ).then_inc(s["ctxT"], 1)
                        pe.wait_ge(s["ctxT_act"], 2)
                        pe.wait_ge(s["ctxT_dve"], 2)
                        for t in range(NT):
                            for c in range(4):
                                k = (l * 4 + c) * P
                                last = nc.tensor.matmul(bank(4, t * P, (t + 1) * P),
                                                        ctx2T[:, c * T + t * P:c * T + (t + 1) * P],
                                                        w_oa_sb[:, k:k + P], start=(c == 0), stop=(c == 3))
                        last.then_inc(s["wo"], 1)
                        pe.wait_ge(s["y_new"], 1)
                        for t in range(NT):
                            nc.tensor.transpose(bank(0, t * P, (t + 1) * P), y[:, t * P:(t + 1) * P],
                                                ident).then_inc(s["yT2"], 1)
                        pe.wait_ge(s["shift2_high"], 1)
                        pe.wait_ge(s["shift2_low"], 1)
                        nc.tensor.matmul(bank(1), cst[:, C_MEAN:C_MEAN + P], hT[:, :], start=True,
                                         stop=True).then_inc(s["mean"], 1)
                        pe.wait_ge(s["dev_sq"], 1)
                        nc.tensor.matmul(bank(2), cst[:, C_MEAN:C_MEAN + P], f_sq[:, 0:T], start=True,
                                         stop=True).then_inc(s["var"], 1)
                        pe.wait_ge(s["normed"], 2)
                        for c, (start, n) in enumerate(HCH):
                            for half in (1, 0):
                                w = l * 2 * HID + half * HID + start
                                k = BANK * (2 * c + half)
                                nc.tensor.matmul(PS[0:n, k:k + T], w1_sb[:, w:w + n], hT[:, :], start=True,
                                                 stop=True).then_inc(s["hidden"], 1)
                        pe.wait_ge(s["glu"], 3)
                        for t in range(NT):
                            nc.tensor.matmul(bank(6, t * P, (t + 1) * P), ones_row, b2_sb[:, l * P:(l + 1) * P],
                                             start=True, stop=False)
                            for c, (start, n) in enumerate(HCH):
                                k = (l * 3 + c) * P
                                last = nc.tensor.matmul(bank(6, t * P, (t + 1) * P),
                                                        glu[0:n, c * T + t * P:c * T + (t + 1) * P],
                                                        w2_sb[0:n, k:k + P], start=False, stop=(c == 2))
                        last.then_inc(s["w2_mm"], 1)

                    v2_view = v2[:, :].rearrange("p (t h d) -> p t h d", t=NT, d=D2 + 1)

                    @block.scalar
                    def _(act):
                        src = xnT_b[:, :] if l == 0 else bank(0)
                        if l:
                            act.wait_ge(s["yT"], NT)
                        nc.scalar.copy(hT[0:64, :], src[0:64, :]).then_inc(s["shift_low"], 1)
                        nc.scalar.copy(hT[64:P, 1:T], src[64:P, 0:T - 1]).then_inc(s["shift_high"], 1)
                        act.wait_ge(s["ones"], 1)
                        for t in (0, 2):
                            act.wait_ge(s["v"], t + 1)
                            nc.scalar.copy(v2_view[:, t, :, 0:D2],
                                           bank(4 + t).rearrange("p (h d) -> p h d", d=D2)).then_inc(s["v_act"], 1)
                        for m in range(9):
                            if m < 8:
                                act.wait_ge(s["a_mm"], m + 1)
                                if m >= 2:
                                    act.wait_ge(s["ss"], m - 1)
                                k = (m % 2) * T
                                nc.scalar.square(f_sq[:, k:k + T], bank(m % 2)).then_inc(s["sq"], 1)
                            if m:
                                act.wait_ge(s["ss"], m)
                                if m >= 3:
                                    act.wait_ge(s["qk2"], m - 2)
                                k = ((m - 1) % 2) * T
                                nc.scalar.activation(f_norm[:, k:k + T], bank(4 + (m - 1) % 2), ACT.Sqrt
                                                     ).then_inc(s["root"], 1)
                        act.wait_ge(s["maxT"], NT)
                        nc.scalar.copy(maxT16[:, :], PS[0:3 * H2, 4 * BANK:5 * BANK]).then_inc(s["maxT_copied"], 1)
                        for h in range(H2):
                            act.wait_ge(s["scoresT"], h + 1)
                            if h >= 2:
                                act.wait_ge(s["context"], h - 1)
                            base = 2 * BANK * (h % 2)
                            nc.scalar.activation(probs2[:, 704 * (h % 2):704 * (h % 2 + 1)], PS[:, base:base + 704],
                                                 ACT.Exp, scale=8.0).then_inc(s["probs"], 1)
                        for c in (0, 2):
                            act.wait_ge(s["ctxT"], NT * (c + 1))
                            nc.scalar.copy(ctx2T[:, c * T:(c + 1) * T], bank(c)).then_inc(s["ctxT_act"], 1)
                        act.wait_ge(s["yT2"], NT)
                        nc.scalar.copy(hT[0:64, :], bank(0)[0:64, :]).then_inc(s["shift2_low"], 1)
                        nc.scalar.copy(hT[64:P, 1:T], bank(0)[64:P, 0:T - 1]).then_inc(s["shift2_high"], 1)
                        act.wait_ge(s["dev"], 1)
                        nc.scalar.square(f_sq[:, 0:T], f_cos[:, 0:T]).then_inc(s["dev_sq"], 1)
                        act.wait_ge(s["var"], 1)
                        nc.scalar.activation(f_norm[:, 0:T], bank(2), ACT.Sqrt, bias=eps[:, 0:1]).then_inc(s["root2"], 1)
                        for c, (start, n) in enumerate(HCH):
                            act.wait_ge(s["hidden"], 2 * c + 1)
                            if c == 2:
                                act.wait_ge(s["glu"], 1)
                            k = (c % 2) * T
                            u = (l * 2 + 1) * 3 + c
                            nc.scalar.activation(gelu[0:n, k:k + T], PS[0:n, BANK * (2 * c + 1):BANK * (2 * c + 2)],
                                                 ACT.Gelu, bias=b1_sb[0:n, u:u + 1]).then_inc(s["gelu"], 1)

                    @block.vector
                    def _(dve):
                        nc.vector.memset(hT[64:P, 0:1], 0.0).then_inc(s["shift_high"], 1)
                        nc.vector.memset(v2[:, :], 1.0).then_inc(s["ones"], 1)
                        if l == 0:
                            nc.vector.tensor_copy(y[:, :], xn_b[:, :]).then_inc(s["y"], 1)
                        dve.wait_ge(s["ones"], 1)
                        for t in (1, 3):
                            dve.wait_ge(s["v"], t + 1)
                            nc.vector.tensor_copy(v2_view[:, t, :, 0:D2],
                                                  bank(4 + t).rearrange("p (h d) -> p h d", d=D2)
                                                  ).then_inc(s["v_dve"], 1)
                        for m in range(8):
                            k = (m % 2) * T
                            tab = (4 * l + (0 if m < 4 else 2)) * T
                            dve.wait_ge(s["a_mm"], m + 1)
                            dve.wait_ge(s["sq"], m + 1)
                            if m >= 2:
                                dve.wait_ge(s["sum"], m - 1)
                            nc.vector.tensor_tensor(f_cos[:, k:k + T], bank(m % 2), tables[:, tab:tab + T],
                                                    ALU.mult).then_inc(s["cos"], 1)
                            dve.wait_ge(s["b_mm"], m + 1)
                            nc.vector.tensor_tensor(f_sin[:, k:k + T], bank(2 + m % 2), tables[:, tab + T:tab + 2 * T],
                                                    ALU.mult).then_inc(s["sin"], 1)
                            dve.wait_ge(s["root"], m + 1)
                            nc.vector.tensor_scalar(f_norm[:, k:k + T], f_norm[:, k:k + T], 1e-12, None, ALU.max
                                                    ).then_inc(s["clip"], 1)
                            dve.wait_ge(s["clip"], m + 1)
                            nc.vector.reciprocal(f_norm[:, k:k + T], f_norm[:, k:k + T]).then_inc(s["inverse"], 1)
                            dve.wait_ge(s["inverse"], m + 1)
                            dve.wait_ge(s["sum"], m + 1)
                            nc.vector.tensor_tensor(qk2[:, m * T:(m + 1) * T], f_sum[:, k:k + T], f_norm[:, k:k + T],
                                                    ALU.mult).then_inc(s["qk2"], 1)
                        for h in range(H2):
                            base = 2 * BANK * (h % 2)
                            dve.wait_ge(s["scores"], h + 1)
                            nc.vector.reduce_max(max2[:, h:h + 1], PS[:, base:base + P], AX_X).then_inc(s["max"], 1)
                            nc.vector.reduce_max(max2[:, H2 + h:3 * H2 + h:H2],
                                                 PS[:, base + P:base + 512].rearrange("p (i k) -> p i k", k=KX),
                                                 AX_X).then_inc(s["max"], 1)
                            nc.vector.reduce_max(max2[:, 3 * H2 + h:3 * H2 + h + 1], PS[:, base + 512:base + 704], AX_X
                                                 ).then_inc(s["max"], 1)
                        dve.wait_ge(s["max"], 3 * H2)
                        nc.vector.tensor_scalar(max_rest[:, :], max2[:, :], -1.0, None, ALU.mult
                                                ).then_inc(s["max_neg"], 1)
                        for n in range(3):
                            dve.wait_ge(s["max_neg"], n + 1)
                            if n:
                                dve.wait_ge(s["parts"], n)
                            nc.vector.tensor_copy(max_part[:, :], max_rest[:, :]).then_inc(s["part"], 1)
                            dve.wait_ge(s["part"], n + 1)
                            nc.vector.tensor_copy(
                                max_parts[:, :].rearrange("p (i r h) -> p i r h", r=3, h=H2)[:, :, n, :],
                                max_part[:, :].rearrange("p (i h) -> p i h", h=H2)).then_inc(s["parts"], 1)
                            if n < 2:
                                nc.vector.tensor_tensor(max_rest[:, :], max_rest[:, :], max_part[:, :], ALU.subtract
                                                        ).then_inc(s["max_neg"], 1)
                        for h in range(H2):
                            dve.wait_ge(s["context"], h + 1)
                            o = bank(6 + h % 2, 0, NT * 65).rearrange("p (t d) -> p t d", d=65)
                            inv = inv2[:, (h % 2) * NT:(h % 2 + 1) * NT]
                            if h >= 2:
                                dve.wait_ge(s["ctx"], h - 1)
                            nc.vector.reciprocal(inv, o[:, :, D2]).then_inc(s["inverse2"], 1)
                            dve.wait_ge(s["inverse2"], h + 1)
                            nc.vector.tensor_tensor(
                                ctx2[:, :].rearrange("p (t h d) -> p t h d", t=NT, d=D2)[:, :, h, :], o[:, :, 0:D2],
                                inv.unsqueeze(2).to_broadcast([P, NT, D2]), ALU.mult).then_inc(s["ctx"], 1)
                        for c in (1, 3):
                            dve.wait_ge(s["ctxT"], NT * (c + 1))
                            nc.vector.tensor_copy(ctx2T[:, c * T:(c + 1) * T], bank(c)).then_inc(s["ctxT_dve"], 1)
                        dve.wait_ge(s["wo"], 1)
                        if l == 0:
                            dve.wait_ge(s["y"], 1)
                        nc.vector.tensor_tensor(y[:, :], y[:, :], bank(4), ALU.add).then_inc(s["y_new"], 1)
                        dve.wait_ge(s["mean"], 1)
                        nc.vector.tensor_tensor(f_cos[:, 0:T], hT[:, :], bank(1), ALU.subtract).then_inc(s["dev"], 1)
                        dve.wait_ge(s["root2"], 1)
                        nc.vector.reciprocal(f_norm[:, 0:T], f_norm[:, 0:T]).then_inc(s["inverse3"], 1)
                        dve.wait_ge(s["inverse3"], 1)
                        nc.vector.scalar_tensor_tensor(f_sin[:, 0:T], f_cos[:, 0:T], ln_sb[:, l:l + 1], f_norm[:, 0:T],
                                                       ALU.mult, ALU.mult).then_inc(s["normed"], 1)
                        dve.wait_ge(s["normed"], 1)
                        nc.vector.tensor_scalar(hT[:, :], f_sin[:, 0:T], ln_sb[:, DEPTH + l:DEPTH + l + 1], None,
                                                ALU.add).then_inc(s["normed"], 1)
                        for c, (start, n) in enumerate(HCH):
                            dve.wait_ge(s["gelu"], c + 1)
                            dve.wait_ge(s["hidden"], 2 * c + 2)
                            u = l * 6 + c
                            nc.vector.scalar_tensor_tensor(glu[0:n, c * T:(c + 1) * T],
                                                           PS[0:n, BANK * 2 * c:BANK * (2 * c + 1)], b1_sb[0:n, u:u + 1],
                                                           gelu[0:n, (c % 2) * T:(c % 2 + 1) * T], ALU.add, ALU.mult
                                                           ).then_inc(s["glu"], 1)
                        dve.wait_ge(s["w2_mm"], 1)
                        nc.vector.tensor_tensor(y[:, :], y[:, :], bank(6), ALU.add).then_inc(s["y_out"], 1)
                end_phase()

            s = phase("silu product sum stored".split())
            with nc.Block() as block:
                @block.scalar
                def _(act):
                    nc.scalar.activation(final[:, :], y[:, :], ACT.Silu).then_inc(s["silu"], 1)

                @block.vector
                def _(dve):
                    dve.wait_ge(s["silu"], 1)
                    nc.vector.tensor_tensor(final[:, :], final[:, :], s1[:, :], ALU.mult).then_inc(s["product"], 1)
                    dve.wait_ge(s["product"], 1)
                    nc.vector.tensor_tensor(final[:, :], final[:, :], x1[:, :], ALU.add).then_inc(s["sum"], 1)

                @block.sync
                def _(sp):
                    sp.wait_ge(s["sum"], 1)
                    sp.dma_start(out[bass.ds(b, 1)].rearrange("o (t p) f -> p (o t) f", p=P),
                                 final[:, :].rearrange("p (t f) -> p t f", f=P)).then_inc(s["stored"], 16)
                    sp.wait_ge(s["stored"], 16)
            end_phase()


_INS = ['L0_attn_x', 'L0_attn_Wq', 'L0_attn_Wk', 'L0_attn_Wv', 'L0_attn_Wo', 'L0_ffn_w_gate', 'L0_ffn_c_fc',
        'L0_ffn_c_proj', 'L1_attn_Wq', 'L1_attn_Wk', 'L1_attn_Wv', 'L1_attn_Wb', 'L1_attn_Wdec', 'L1_attn_Wmix',
        'L1_attn_mix_bias', 'L1_attn_wq_conv', 'L1_attn_wk_conv', 'L1_attn_wv_conv', 'L1_attn_onorm_w', 'L1_attn_Wo',
        'L1_ffn_wqkv', 'scales', 'L1_ffn_wo', 'L1_ffn_ln_g', 'L1_ffn_ln_b', 'L1_ffn_w1',
        'L1_ffn_b1', 'L1_ffn_w2', 'L1_ffn_b2', 'constants']
_TRANSPOSED = {'L1_attn_Wq', 'L1_attn_Wk', 'L1_attn_Wv', 'L1_attn_Wb', 'L1_attn_Wdec', 'L1_attn_Wmix', 'L1_attn_Wo', 'L1_ffn_ln_g',
               'L1_ffn_ln_b'}
_FLAT = {'L0_ffn_c_fc', 'L0_ffn_c_proj'}


def laid_out(name, inputs):
    if name == 'constants':
        return constants()
    if name == 'scales':
        both = []
        for layer in range(DEPTH):
            for n in ('L1_ffn_q_scale', 'L1_ffn_k_scale'):
                a = np.asarray(inputs[n])[layer]
                both += [np.tile(a, 2), np.tile(np.roll(a, D2 // 2), 2)]
        return np.ascontiguousarray(np.stack(both, axis=1))
    a = np.asarray(inputs[name])
    if name == 'L1_attn_mix_bias':
        a = np.repeat(a, DH1)[:, None]
    if name == 'L1_attn_onorm_w':
        a = np.tile(a, H1)[:, None]
    if name in _TRANSPOSED:
        a = a.T
    if name in _FLAT:
        a = a.reshape(-1, a.shape[-1])
    return np.ascontiguousarray(a)


def kernel(**inputs):
    import concourse.bacc as _bacc
    from concourse import mybir as _mybir
    from concourse.bass_utils import run_bass_kernel_spmd as _run

    nc = _bacc.Bacc("TRN2", target_bir_lowering=False, num_devices=1)
    arrays, args = {}, []
    for name in _INS:
        a = laid_out(name, inputs)
        arrays[f"in_{name}_dram"] = a
        args.append(nc.dram_tensor(f"in_{name}_dram", a.shape, _mybir.dt.from_np(a.dtype), kind="ExternalInput").ap())
    out = nc.dram_tensor("out_0_dram", (B, T, P), _mybir.dt.float32, kind="ExternalOutput").ap()
    network(nc, args, out)
    r = _run(nc, [arrays], core_ids=[0])
    return r.results[0]["out_0_dram"]
```

```python
from contextlib import ExitStack

import numpy as np

import concourse.bass as bass
from concourse import mybir

F32 = mybir.dt.float32
BF16 = mybir.dt.bfloat16
U32 = mybir.dt.uint32
ALU = mybir.AluOpType
ACT = mybir.ActivationFunctionType
AX_X = mybir.AxisListType.X

P = 128
B, T = 8, 512
NT = T // P
NTILE = B * NT
BANK = 512
NEG = -1e30

H0, DK0, DV0 = 16, 8, 64
G0 = 8
Q_PART, K_PART = (0, 0, 1, 0, 2, 1, 1), (0, 1, 0, 2, 0, 1, 2)
LSE_ROW = 8 * len(Q_PART)
NE, CAP, HALF = 8, 512, 192
HC = 96
H1, DH1, CH = 4, 32, 32
DEPTH, H2, D2, WIN = 2, 8, 64, 64
HID = int(P * 4 * 2 / 3)
HCH = [(0, 128), (128, 128), (256, HID - 256)]

C_ID, C_USTRICT, C_ONES, C_STEP = 0, 128, 256, 384
C_BLK32, C_CORNER = 512, 640
C_CAUSAL, C_CAUSALT = 768, 896
C_BAND, C_BANDT = 1024, 1216
C_DELTA = 1408
C_IOTA = C_DELTA + 320
C_KONE = C_IOTA + 8
C_SEL = C_KONE + 1
C_COS = C_SEL + H2
C_STACK = C_COS + 4 * NT * D2
C_STACKG = C_STACK + 6 * P
C_SHIFT = C_STACKG + 8
C_SHIFTG = C_SHIFT + P
C_END = C_SHIFTG + 8
(D_NEGLO, D_NEGLOT, D_INCLT, D_EYE, D_M1, D_M1T, D_M2T, D_M4T, D_M8T, D_M16T) = range(10)


def constants():
    c = np.zeros((P, C_END), np.float32)
    p = np.arange(P)[:, None]
    f = np.arange(P)[None, :]
    c[:, C_ID:C_ID + P] = p == f
    c[:, C_USTRICT:C_USTRICT + P] = p < f
    c[:, C_ONES:C_ONES + P] = 1.0
    c[:, C_STEP:C_STEP + P] = p == f - 1
    c[:, C_BLK32:C_BLK32 + P] = p // DH1 == f // DH1
    c[:, C_CORNER:C_CORNER + P] = (p == P - 1) & (f == 0)
    c[:, C_CAUSAL:C_CAUSAL + P] = np.where(f > p, NEG, 0.0)
    c[:, C_CAUSALT:C_CAUSALT + P] = np.where(p > f, NEG, 0.0)
    w = np.arange(P + WIN)[None, :]
    gap = p - (w - WIN)
    c[:, C_BAND:C_BAND + P + WIN] = np.where((gap < 0) | (gap > WIN), NEG, 0.0)
    gap = w - p
    c[:, C_BANDT:C_BANDT + P + WIN] = np.where((gap < 0) | (gap > WIN), NEG, 0.0)
    i = p % CH
    j = np.arange(CH)[None, :]

    def lower(a, b, s):
        return (a // (2 * s) == b // (2 * s)) & (a % (2 * s) >= s) & (b % (2 * s) < s)

    masks = [-1.0 * (i > j), -1.0 * (i < j), j >= i, i == j, lower(i, j, 1), lower(j, i, 1),
             lower(j, i, 2), lower(j, i, 4), lower(j, i, 8), lower(j, i, 16)]
    for n, m in enumerate(masks):
        c[:, C_DELTA + n * CH:C_DELTA + (n + 1) * CH] = m
    c[:, C_IOTA:C_IOTA + NE] = np.arange(NE)
    c[:, C_KONE] = (np.arange(P) % 64 >= LSE_ROW) & (np.arange(P) % 64 < LSE_ROW + 3)
    c[:, C_SEL:C_SEL + H2 // 2] = (p % (H2 // 2) == np.arange(H2 // 2)) & (p < 3 * H2 // 2)
    r = f % 64 // DK0
    mine = (p % 16 // DK0 == f // 64) & (p % DK0 == f % DK0)
    for n, part in enumerate((Q_PART, K_PART)):
        of = np.array(list(part) + [-1])[r]
        for k in range(3):
            a = C_STACK + (3 * n + k) * P
            c[:, a:a + P] = mine & (of == k)
    c[:, C_STACKG:C_STACKG + G0] = p // 16 == np.arange(G0)
    c[:, C_SHIFT:C_SHIFT + P] = (p < 3 * H0) & (f % 64 == LSE_ROW + p // H0) & (p % 2 == f // 64)
    c[:, C_SHIFTG:C_SHIFTG + G0] = p % H0 // 2 == np.arange(G0)
    half = np.arange(0, D2, 2, dtype=np.float32)
    inv = (np.float32(1.0) / np.float32(10000.0) ** (half / np.float32(D2))).astype(np.float32)
    t = np.arange(T, dtype=np.float32)
    freqs = (t[:, None] * inv[None, :]).astype(np.float32)
    base = ((half + np.float32(0.4 * D2)) / np.float32(1.4 * D2)).astype(np.float32)
    power = ((t - T // 2) / np.float32(WIN // 2)).astype(np.float32)
    scale = (base[None, :] ** power[:, None]).astype(np.float32)
    cos, sin = np.cos(freqs), np.sin(freqs)
    for n, tab in enumerate((cos * scale, sin * scale, cos / scale, sin / scale)):
        first = -tab if n % 2 else tab
        rows = np.concatenate([first, tab], axis=1)
        c[:, C_COS + n * NT * D2:C_COS + (n + 1) * NT * D2] = rows.reshape(NT, P, D2).transpose(1, 0, 2).reshape(P, -1)
    return c


ROUTE = "zeroed loaded cast stats moments variance rstd normed normedT normedT_kept kept logits".split()


def layer_norm_steps(nc, s, dve, x_tile, stats, moments, var_eps, rstd, out):
    for t in range(NT):
        nc.vector.bn_stats(stats[:, 6 * t:6 * t + 6], x_tile(t)).then_inc(s["stats"], 1)
    for t in range(NT):
        dve.wait_ge(s["stats"], t + 1)
        nc.vector.bn_aggr(moments[:, 2 * t:2 * t + 2], stats[:, 6 * t:6 * t + 6]).then_inc(s["moments"], 1)
    dve.wait_ge(s["moments"], NT)
    nc.vector.tensor_scalar(var_eps[:, :], moments[:, 1:2 * NT:2], 1e-5, None, ALU.add).then_inc(s["variance"], 1)
    dve.wait_ge(s["rstd"], 1)
    for t in range(NT):
        nc.vector.tensor_scalar(out(t), x_tile(t), moments[:, 2 * t:2 * t + 1], rstd[:, t:t + 1],
                                ALU.subtract, ALU.mult).then_inc(s["normed"], 1)


def split_steps(nc, dve, s, rest, part, parts, heads, half):
    for n in range(3):
        dve.wait_ge(s["shift_rest"], 3 * half + n + 1)
        if n:
            dve.wait_ge(s["shift_parts"], 3 * half + n)
        nc.vector.tensor_copy(part, rest).then_inc(s["shift_part"], 1)
        dve.wait_ge(s["shift_part"], 3 * half + n + 1)
        nc.vector.tensor_copy(parts.rearrange("p (i r h) -> p i r h", r=3, h=heads)[:, :, n, :],
                              part.rearrange("p (i h) -> p i h", h=heads)).then_inc(s["shift_parts"], 1)
        if n < 2:
            nc.vector.tensor_tensor(rest, rest, part, ALU.subtract).then_inc(s["shift_rest"], 1)


def network(nc, ins, out):
    (x_in, w_q0, w_k0, w_v0, w_o0, w_gate, c_fc, c_proj, w_q1, w_k1, w_v1, w_beta, w_decay, w_mix, mix_bias,
     conv_q, conv_k, conv_v, onorm, w_o1, w_qkv, scales, w_oa, ln_g, ln_b, w_1, b_1, w_2, b_2, const_in) = ins

    with ExitStack() as ctx:
        def sb(name, cols, dt=F32, rows=P):
            return ctx.enter_context(nc.sbuf_tensor(name, [rows, cols], dt))

        pool = [ctx.enter_context(nc.semaphore(f"phase_{i}")) for i in range(120)]
        clearable = range(pool[0].num, pool[-1].num + 1)
        scattered = ctx.enter_context(nc.semaphore("scattered"))
        gathered = ctx.enter_context(nc.semaphore("gathered"))

        def phase(names):
            return dict(zip(names, pool))

        def end_phase():
            nc.all_engine_barrier(sems_to_clear=clearable)

        PS = ctx.enter_context(nc.psum_tensor("PS", [P, 8 * BANK], F32))

        def bank(k, a=0, b=BANK):
            return PS[:, BANK * k + a:BANK * k + b]

        slots_in = nc.dram_tensor("slots_in", (NE * CAP, P), F32, kind="Internal").ap()
        slots_out = nc.dram_tensor("slots_out", (NE * CAP, P), F32, kind="Internal").ap()

        cst = sb("cst", C_COS)
        ident = cst[:, C_ID:C_ID + P]
        ones_row = cst[0:1, C_ONES:C_ONES + P]
        causal16 = sb("causal16", P, BF16)
        causalT16 = sb("causalT16", P, BF16)
        band16 = sb("band16", P + WIN, BF16)
        bandT16 = sb("bandT16", P + WIN, BF16)
        ident16 = sb("ident16", P, BF16)

        wq0 = sb("wq0", P)
        wk0 = sb("wk0", P)
        stack16 = sb("stack16", G0 * 6 * P, BF16)
        shift16 = sb("shift16", G0 * P, BF16, 3 * H0)
        kz = sb("kz", H0 * T, BF16)
        wv0 = sb("wv0", H0 * DV0)
        wo0 = sb("wo0", H0 * DV0)
        wg = sb("wg", NE)

        x_all = sb("x_all", NTILE * P)
        xnT_all = sb("xnT_all", B * T)
        route_w = sb("route_w", 2 * NTILE)
        slot_from = sb("slot_from", 2 * NTILE, U32)

        stats = sb("stats", 6 * NT)
        moments = sb("moments", 2 * NT)
        var_eps = sb("var_eps", NT)
        rstd = sb("rstd", NT)
        minus_half = sb("minus_half", NT)
        xn_b = sb("xn_b", NT * P)
        xnT_b = sb("xnT_b", T)

        wq1 = sb("wq1", P)
        wk1 = sb("wk1", P)
        wv1 = sb("wv1", P)
        wo1 = sb("wo1", P)
        w_gates = sb("w_gates", 3 * P)
        conv_w = sb("conv_w", 12)
        column = sb("column", 2)
        wqkv = sb("wqkv", DEPTH * 1536)
        w_oa_sb = sb("w_oa_sb", DEPTH * 4 * P)
        w1_sb = sb("w1_sb", DEPTH * 2 * HID)
        w2_sb = sb("w2_sb", DEPTH * 3 * P)
        b1_sb = sb("b1_sb", DEPTH * 6)
        b2_sb = sb("b2_sb", DEPTH * P, F32, 1)
        ln_sb = sb("ln_sb", 2 * DEPTH)
        tables = sb("tables", DEPTH * 4 * NT * D2)
        kz2 = sb("kz2", H2 * T)
        select16 = sb("select16", H2 // 2 * P, BF16, 3 * H2 // 2)
        eps = sb("eps", 2)

        before = ctx.enter_context(ExitStack())

        def sb0(name, cols, dt=F32, rows=P):
            return before.enter_context(nc.sbuf_tensor(name, [rows, cols], dt))

        gates_in = sb0("gates_in", 3 * H1)
        scales_in = sb0("scales_in", 4 * DEPTH * D2)
        rotary = sb0("rotary", C_END - C_COS)
        xn_all = sb0("xn_all", NTILE * P)
        logits_all = sb0("logits_all", NTILE * NE)

        s = phase("loaded zeros cleared cast spread".split())
        with nc.Block() as block:
            zeros = xn_all
            LOADS = [(cst[:, :], const_in[:, 0:C_COS]), (rotary[:, :], const_in[:, C_COS:C_END]),
                     (wq0[:, :], w_q0), (wk0[:, :], w_k0), (wv0[:, :], w_v0), (wg[:, :], w_gate),
                     (wq1[:, :], w_q1), (wk1[:, :], w_k1), (wv1[:, :], w_v1), (wo1[:, :], w_o1),
                     (gates_in[:, 0:H1], w_beta), (gates_in[:, H1:2 * H1], w_decay), (gates_in[:, 2 * H1:3 * H1], w_mix),
                     (conv_w[:, 0:4], conv_q), (conv_w[:, 4:8], conv_k), (conv_w[:, 8:12], conv_v),
                     (column[:, 0:1], mix_bias), (column[:, 1:2], onorm),
                     (scales_in[:, :], scales), (b2_sb[:, :], b_2.rearrange("l (o n) -> o (l n)", o=1)),
                     (ln_sb[:, 0:DEPTH], ln_g), (ln_sb[:, DEPTH:2 * DEPTH], ln_b)]
            for l in range(DEPTH):
                LOADS += [(wqkv[:, l * 1536:(l + 1) * 1536], w_qkv[l]), (w1_sb[:, l * 2 * HID:(l + 1) * 2 * HID], w_1[l]),
                          (w_oa_sb[:, l * 512:(l + 1) * 512].rearrange("p (c n) -> p c n", n=P),
                           w_oa[l].rearrange("(c p) n -> p c n", p=P))]
                for c, (start, n) in enumerate(HCH):
                    k = (l * 3 + c) * P
                    LOADS.append((w2_sb[0:n, k:k + P], w_2[l, start:start + n, :]))
                    for half in range(2):
                        k = (l * 2 + half) * 3 + c
                        a = half * HID + start
                        LOADS.append((b1_sb[0:n, k:k + 1], b_1[l, a:a + n].unsqueeze(1)))

            @block.sync
            def _(sp):
                for dst, src in LOADS:
                    sp.dma_start(dst, src).then_inc(s["loaded"], 16)
                sp.dma_start(wo0[:, :].rearrange("p (c n) -> p c n", n=P),
                             w_o0.rearrange("(c p) n -> p c n", p=P)).then_inc(s["loaded"], 16)
                for q in range(4):
                    sp.dma_start(x_all[:, q * 1024:(q + 1) * 1024].rearrange("p (t f) -> p t f", f=P),
                                 x_in.rearrange("b (t p) f -> p (b t) f", p=P)[:, 8 * q:8 * q + 8, :]
                                 ).then_inc(s["loaded"], 16)
                sp.wait_ge(s["zeros"], 1)
                sp.dma_start(slots_in.rearrange("(p r) f -> p (r f)", p=P), zeros[:, :]).then_inc(s["cleared"], 16)
                sp.wait_ge(s["cleared"], 16)
                sp.wait_ge(s["loaded"], 16 * (len(LOADS) + 5))

            @block.gpsimd
            def _(gp):
                nc.gpsimd.memset(minus_half[:, :], -0.5)

            @block.vector
            def _(dve):
                nc.vector.memset(zeros[:, :], 0.0).then_inc(s["zeros"], 1)
                nc.vector.memset(kz[:, :], 0.0)
                nc.vector.memset(kz2[:, :], 0.0)
                dve.wait_ge(s["loaded"], 16 * (len(LOADS) + 5))
                nc.vector.tensor_copy(causal16[:, :], cst[:, C_CAUSAL:C_CAUSAL + P])
                nc.vector.tensor_copy(causalT16[:, :], cst[:, C_CAUSALT:C_CAUSALT + P])
                nc.vector.tensor_copy(band16[:, :], cst[:, C_BAND:C_BAND + P + WIN])
                nc.vector.tensor_copy(bandT16[:, :], cst[:, C_BANDT:C_BANDT + P + WIN])
                nc.vector.tensor_copy(ident16[:, :], ident)
                at = C_STACK - C_COS
                for g in range(G0):
                    nc.vector.tensor_scalar(stack16[:, g * 6 * P:(g + 1) * 6 * P], rotary[:, at:at + 6 * P],
                                            rotary[:, C_STACKG - C_COS + g:C_STACKG - C_COS + g + 1], None, ALU.mult)
                    nc.vector.tensor_scalar(shift16[:, g * P:(g + 1) * P],
                                            rotary[0:3 * H0, C_SHIFT - C_COS:C_SHIFT - C_COS + P],
                                            rotary[0:3 * H0, C_SHIFTG - C_COS + g:C_SHIFTG - C_COS + g + 1], None,
                                            ALU.mult)
                nc.vector.tensor_copy(w_gates[:, :].rearrange("p (g d) -> p g d", d=DH1),
                                      gates_in[:, :].unsqueeze(2).to_broadcast([P, 3 * H1, DH1]))
                nc.vector.tensor_copy(select16[:, :].rearrange("p (h d) -> p h d", d=P),
                                      cst[0:3 * H2 // 2, C_SEL:C_SEL + H2 // 2].unsqueeze(2).to_broadcast(
                                          [3 * H2 // 2, H2 // 2, P]))
                for l in range(DEPTH):
                    for n in range(4):
                        nc.vector.tensor_tensor(
                            tables[:, (4 * l + n) * NT * D2:(4 * l + n + 1) * NT * D2].rearrange("p (t d) -> p t d", d=D2),
                            rotary[:, n * NT * D2:(n + 1) * NT * D2].rearrange("p (t d) -> p t d", d=D2),
                            scales_in[:, (4 * l + n) * D2:(4 * l + n + 1) * D2].unsqueeze(1).to_broadcast([P, NT, D2]),
                            ALU.mult)
                nc.vector.memset(eps[:, 0:1], 1e-5)
                nc.vector.memset(eps[:, 1:2], 1e-6)
        end_phase()

        s = phase("stats moments variance rstd normed kept transposed T_copied T_kept logits logits_kept".split())
        with nc.Fori(0, B) as b:
            with nc.Block() as block:
                @block.vector
                def _(dve):
                    layer_norm_steps(nc, s, dve, lambda t: x_all[:, bass.ds(b * T + t * P, P)], stats, moments,
                                     var_eps, rstd, lambda t: xn_b[:, t * P:(t + 1) * P])
                    dve.wait_ge(s["logits"], NT)
                    nc.vector.tensor_copy(logits_all[:, bass.ds(b * NT * NE, NT * NE)],
                                          bank(1, 0, NT * NE)).then_inc(s["logits_kept"], 1)

                @block.gpsimd
                def _(gp):
                    gp.wait_ge(s["variance"], 1)
                    nc.gpsimd.tensor_tensor(rstd[:, :], var_eps[:, :], minus_half[:, :], ALU.pow).then_inc(s["rstd"], 1)
                    gp.wait_ge(s["normed"], NT)
                    nc.gpsimd.tensor_copy(xn_all[:, bass.ds(b * T, T)], xn_b[:, :]).then_inc(s["kept"], 1)
                    gp.wait_ge(s["T_copied"], 1)
                    nc.gpsimd.tensor_copy(xnT_all[:, bass.ds(b * T, T)], xnT_b[:, :]).then_inc(s["T_kept"], 1)

                @block.tensor
                def _(pe):
                    for t in range(NT):
                        pe.wait_ge(s["normed"], t + 1)
                        nc.tensor.transpose(bank(0, t * P, (t + 1) * P), xn_b[:, t * P:(t + 1) * P],
                                            ident).then_inc(s["transposed"], 1)
                    pe.wait_ge(s["T_copied"], 1)
                    for t in range(NT):
                        nc.tensor.matmul(bank(1, t * NE, (t + 1) * NE), xnT_b[:, t * P:(t + 1) * P], wg[:, :],
                                         start=True, stop=True).then_inc(s["logits"], 1)

                @block.scalar
                def _(act):
                    act.wait_ge(s["transposed"], NT)
                    nc.scalar.copy(xnT_b[:, :], bank(0)).then_inc(s["T_copied"], 1)
            end_phase()

        N8 = NTILE * NE
        top = sb0("top", N8)
        top_i = sb0("top_i", N8, U32)
        choice = sb0("choice", 2 * NTILE)
        oh = sb0("oh", 2 * N8)
        both = sb0("both", N8)
        expo = sb0("expo", N8)
        gap2 = sb0("gap2", NTILE)
        wsum = sb0("wsum", NTILE)
        ranked = sb0("ranked", N8)
        tot = sb0("tot", N8)
        cum = sb0("cum", N8)
        prod = sb0("prod", 2 * N8)
        pos = sb0("pos", 2 * NTILE)
        valid = sb0("valid", 2 * NTILE)
        slot_f = sb0("slot_f", 2 * NTILE)
        past = sb0("past", 2 * NTILE)
        slot_to = sb0("slot_to", 2 * NTILE, U32)

        def te(ap):
            return ap.rearrange("p (t e) -> p t e", e=NE)

        s = phase("top index choice onehot both shifted expo wsum inverse weight counts totals cum rank prod pos "
                  "valid slot".split())
        with nc.Block() as block:
            @block.vector
            def _(dve):
                for n in range(NTILE):
                    nc.vector.max(top[:, n * NE:(n + 1) * NE], logits_all[:, n * NE:(n + 1) * NE]).then_inc(s["top"], 1)
                for n in range(NTILE):
                    dve.wait_ge(s["top"], n + 1)
                    nc.vector.max_index(top_i[:, n * NE:(n + 1) * NE], top[:, n * NE:(n + 1) * NE],
                                        logits_all[:, n * NE:(n + 1) * NE]).then_inc(s["index"], 1)
                dve.wait_ge(s["index"], NTILE)
                for k in range(2):
                    nc.vector.tensor_copy(choice[:, k * NTILE:(k + 1) * NTILE],
                                          te(top_i[:, :])[:, :, k]).then_inc(s["choice"], 1)
                dve.wait_ge(s["choice"], 2)
                for k in range(2):
                    nc.vector.tensor_tensor(
                        te(oh[:, k * N8:(k + 1) * N8]),
                        cst[:, C_IOTA:C_IOTA + NE].unsqueeze(1).to_broadcast([P, NTILE, NE]),
                        choice[:, k * NTILE:(k + 1) * NTILE].unsqueeze(2).to_broadcast([P, NTILE, NE]),
                        ALU.is_equal).then_inc(s["onehot"], 1)
                dve.wait_ge(s["onehot"], 2)
                nc.vector.tensor_tensor(both[:, :], oh[:, 0:N8], oh[:, N8:2 * N8], ALU.add).then_inc(s["both"], 1)
                nc.vector.tensor_tensor(te(expo[:, :]), te(logits_all[:, :]),
                                        te(top[:, :])[:, :, 0].unsqueeze(2).to_broadcast([P, NTILE, NE]),
                                        ALU.subtract).then_inc(s["shifted"], 1)
                nc.vector.tensor_tensor(gap2[:, :], te(top[:, :])[:, :, 1], te(top[:, :])[:, :, 0],
                                        ALU.subtract).then_inc(s["shifted"], 1)
                dve.wait_ge(s["expo"], 2)
                nc.vector.reduce_sum(wsum[:, :], te(expo[:, :]), AX_X).then_inc(s["wsum"], 1)
                dve.wait_ge(s["wsum"], 1)
                nc.vector.reciprocal(wsum[:, :], wsum[:, :]).then_inc(s["inverse"], 1)
                dve.wait_ge(s["totals"], 1)
                nc.vector.tensor_copy(tot[:, :], bank(1, 0, N8)).then_inc(s["counts"], 1)
                dve.wait_ge(s["counts"], 1)
                for e in range(NE):
                    nc.vector.tensor_tensor_scan(te(cum[:, :])[:, :, e], cst[:, C_ONES:C_ONES + NTILE],
                                                 te(tot[:, :])[:, :, e], 0.0, ALU.mult, ALU.add).then_inc(s["cum"], 1)
                dve.wait_ge(s["cum"], NE)
                nc.vector.tensor_tensor(ranked[:, :], cum[:, :], tot[:, :], ALU.subtract).then_inc(s["rank"], 1)
                dve.wait_ge(s["rank"], 1)
                nc.vector.tensor_tensor(ranked[:, :], ranked[:, :], bank(0, 0, N8), ALU.add).then_inc(s["rank"], 1)
                dve.wait_ge(s["rank"], 2)
                for k in range(2):
                    nc.vector.tensor_tensor(prod[:, k * N8:(k + 1) * N8], oh[:, k * N8:(k + 1) * N8], ranked[:, :],
                                            ALU.mult).then_inc(s["prod"], 1)
                dve.wait_ge(s["prod"], 2)
                nc.vector.reduce_sum(pos[:, :], te(prod[:, :]), AX_X).then_inc(s["pos"], 1)
                dve.wait_ge(s["pos"], 1)
                nc.vector.tensor_scalar(valid[:, :], pos[:, :], float(CAP), None, ALU.is_lt).then_inc(s["valid"], 1)
                dve.wait_ge(s["valid"], 1)
                weight = route_w[:, :].rearrange("p (t k) -> p t k", k=2)
                nc.vector.tensor_tensor(weight[:, :, 0], wsum[:, :], valid[:, 0:NTILE], ALU.mult)
                nc.vector.tensor_tensor(gap2[:, :], gap2[:, :], wsum[:, :], ALU.mult).then_inc(s["weight"], 1)
                dve.wait_ge(s["weight"], 1)
                nc.vector.tensor_tensor(weight[:, :, 1], gap2[:, :], valid[:, NTILE:2 * NTILE], ALU.mult)
                nc.vector.scalar_tensor_tensor(slot_f[:, :], choice[:, :], float(CAP), pos[:, :],
                                               ALU.mult, ALU.add).then_inc(s["slot"], 1)
                nc.vector.tensor_scalar(past[:, :], valid[:, :], -65536.0, 65536.0, ALU.mult, ALU.add).then_inc(s["slot"], 1)
                dve.wait_ge(s["slot"], 2)
                nc.vector.tensor_tensor(slot_to[:, :], slot_f[:, :], past[:, :], ALU.add).then_inc(s["slot"], 1)
                nc.vector.tensor_tensor(slot_from[:, :].rearrange("p (t k) -> p t k", k=2),
                                        slot_f[:, :].rearrange("p (k t) -> p t k", k=2),
                                        valid[:, :].rearrange("p (k t) -> p t k", k=2), ALU.mult).then_inc(s["slot"], 1)

            @block.scalar
            def _(act):
                act.wait_ge(s["shifted"], 2)
                nc.scalar.activation(expo[:, :], expo[:, :], ACT.Exp).then_inc(s["expo"], 1)
                nc.scalar.activation(gap2[:, :], gap2[:, :], ACT.Exp).then_inc(s["expo"], 1)

            @block.tensor
            def _(pe):
                pe.wait_ge(s["both"], 1)
                nc.tensor.matmul(bank(0, 0, N8), cst[:, C_USTRICT:C_USTRICT + P], both[:, :], start=True, stop=True)
                nc.tensor.matmul(bank(1, 0, N8), cst[:, C_ONES:C_ONES + P], both[:, :],
                                 start=True, stop=True).then_inc(s["totals"], 1)

            @block.gpsimd
            def _(gp):
                gp.wait_ge(s["slot"], 4)
                for n in range(NTILE):
                    for k in range(2):
                        nc.gpsimd.indirect_dma_start(
                            out=slots_in, out_offset=bass.IndirectOffsetOnAxis(
                                ap=slot_to[:, k * NTILE + n:k * NTILE + n + 1], axis=0),
                            in_=xn_all[:, n * P:(n + 1) * P], in_offset=None,
                            bounds_check=NE * CAP - 1, oob_is_err=False).then_inc(scattered, 16)
                gp.wait_ge(scattered, 16 * 2 * NTILE)
        end_phase()

        wfc = sb0("wfc", 4 * HC)
        wpr = sb0("wpr", 2 * P, F32, HC)
        rows = sb0("rows", T)
        rowsT = sb0("rowsT", T)
        silu_a = sb0("silu_a", 2 * T, F32, HC)
        gated = sb0("gated", 2 * T, F32, HC)
        rows_out = sb0("rows_out", T)
        s = phase("loaded transposed T_copied hidden silu gated projected copied stored".split())
        with nc.Fori(0, NE) as e:
            with nc.Block() as block:
                @block.sync
                def _(sp):
                    sp.dma_start(rows[:, :].rearrange("p (t f) -> p t f", f=P),
                                 slots_in[bass.ds(e * CAP, CAP), :].rearrange("(t p) f -> p t f", p=P)
                                 ).then_inc(s["loaded"], 16)
                    sp.dma_start(wfc[:, :], c_fc[bass.ds(e * P, P), :]).then_inc(s["loaded"], 16)
                    sp.dma_start(wpr[:, :].rearrange("p (c n) -> p c n", n=P),
                                 c_proj[bass.ds(e * HALF, HALF), :].rearrange("(c p) n -> p c n", p=HC)
                                 ).then_inc(s["loaded"], 16)
                    sp.wait_ge(s["copied"], 1)
                    sp.dma_start(slots_out[bass.ds(e * CAP, CAP), :].rearrange("(t p) f -> p t f", p=P),
                                 rows_out[:, :].rearrange("p (t f) -> p t f", f=P)).then_inc(s["stored"], 16)
                    sp.wait_ge(s["stored"], 16)

                @block.tensor
                def _(pe):
                    pe.wait_ge(s["loaded"], 48)
                    for t in range(NT):
                        nc.tensor.transpose(bank(0, t * P, (t + 1) * P), rows[:, t * P:(t + 1) * P],
                                            ident).then_inc(s["transposed"], 1)
                    pe.wait_ge(s["T_copied"], 1)
                    for c in (0, 2, 1, 3):
                        nc.tensor.matmul(PS[0:HC, BANK * (1 + c):BANK * (2 + c)], wfc[:, c * HC:(c + 1) * HC],
                                         rowsT[:, :], start=True, stop=True).then_inc(s["hidden"], 1)
                    pe.wait_ge(s["gated"], 2)
                    for t in range(NT):
                        for c in range(2):
                            nc.tensor.matmul(bank(5, t * P, (t + 1) * P), gated[:, c * T + t * P:c * T + (t + 1) * P],
                                             wpr[:, c * P:(c + 1) * P], start=(c == 0), stop=(c == 1)
                                             ).then_inc(s["projected"], 1)

                @block.scalar
                def _(act):
                    for c in range(2):
                        act.wait_ge(s["hidden"], 1 + 2 * c)
                        nc.scalar.activation(silu_a[:, c * T:(c + 1) * T], PS[0:HC, BANK * (1 + c):BANK * (2 + c)],
                                             ACT.Silu).then_inc(s["silu"], 1)

                @block.vector
                def _(dve):
                    dve.wait_ge(s["transposed"], NT)
                    nc.vector.tensor_copy(rowsT[:, :], bank(0)).then_inc(s["T_copied"], 1)
                    for c in range(2):
                        dve.wait_ge(s["silu"], c + 1)
                        dve.wait_ge(s["hidden"], 2 + 2 * c)
                        nc.vector.tensor_tensor(gated[:, c * T:(c + 1) * T], silu_a[:, c * T:(c + 1) * T],
                                                PS[0:HC, BANK * (3 + c):BANK * (4 + c)], ALU.mult
                                                ).then_inc(s["gated"], 1)
                    dve.wait_ge(s["projected"], 2 * NT)
                    nc.vector.tensor_copy(rows_out[:, :], bank(5)).then_inc(s["copied"], 1)
            end_phase()

        before.close()
        x1 = sb("x1", NT * P)

        def sb1(name, cols, dt=F32, rows=P):
            return layer0.enter_context(nc.sbuf_tensor(name, [rows, cols], dt))

        layer0 = ctx.enter_context(ExitStack())
        q_parts = sb1("q_parts", 3 * T, BF16)
        k_parts = sb1("k_parts", 3 * T, BF16)
        rest = sb1("rest", 2 * T)
        qS = sb1("qS", G0 * T, BF16)
        v0 = sb1("v0", NT * H0 * DV0)
        row_max = sb1("row_max", H0 * NT)
        bias0 = sb1("bias0", H0 * NT)
        sums0 = sb1("sums0", H0 * NT)
        log_sums = sb1("log_sums", H0 * NT)
        shift_rest = sb1("shift_rest", NT * H0)
        shift_part = sb1("shift_part", NT * H0, BF16)
        shift_parts = sb1("shift_parts", NT * 3 * H0)
        shiftT16 = sb1("shiftT16", T, BF16, 3 * H0)
        probsT = sb1("probsT", 2 * 1280)
        ctx0T = sb1("ctx0T", G0 * T)
        from_b = sb1("from_b", 2 * NT, U32)
        weight_b = sb1("weight_b", 2 * NT)
        picked = ctx0T[:, 0:2 * NT * P]
        moe = rest[:, 0:NT * P]
        REGION = {0: 0, 1: 512, 3: 896, 2: 1024}
        QREGION = {3: 0, 2: 512, 0: 896, 1: 1024}

        scale0 = 1.0 / float(np.sqrt(DK0))
        with nc.Fori(0, B) as b:
            s = phase("xT_b from_b weight_b qk part rest v v_act v_dve stack stacked scores max bias sum "
                      "log shift_rest shift_part shift_parts shiftT shiftT_copied shift_mm shifted scoresT probs "
                      "context ctxT attn moe_half moe silu gated x1".split())
            with nc.Block() as block:
                @block.gpsimd
                def _(gp):
                    nc.gpsimd.tensor_copy(from_b[:, :], slot_from[:, bass.ds(b * 2 * NT, 2 * NT)]).then_inc(s["from_b"], 1)
                    gp.wait_ge(s["from_b"], 1)
                    for n in range(2 * NT):
                        nc.gpsimd.indirect_dma_start(
                            out=picked[:, n * P:(n + 1) * P], out_offset=None, in_=slots_out,
                            in_offset=bass.IndirectOffsetOnAxis(ap=from_b[:, n:n + 1], axis=0),
                            bounds_check=NE * CAP - 1, oob_is_err=False).then_inc(gathered, 16)

                @block.tensor
                def _(pe):
                    pe.wait_ge(s["xT_b"], 1)
                    nc.tensor.matmul(bank(0), wq0[:, :], xnT_b[:, :], start=True, stop=True).then_inc(s["qk"], 1)
                    nc.tensor.matmul(bank(1), wk0[:, :], xnT_b[:, :], start=True, stop=True).then_inc(s["qk"], 1)
                    for n in range(2 * NT):
                        t, half = divmod(n, 2)
                        if n == 6:
                            pe.wait_ge(s["v_act"], 1)
                        if n == 7:
                            pe.wait_ge(s["v_dve"], 1)
                        nc.tensor.matmul(bank(2 + n % 6), xnT_b[:, t * P:(t + 1) * P],
                                         wv0[:, half * 512:(half + 1) * 512], start=True, stop=True
                                         ).then_inc(s["v"], 1)

                    def stack(g):
                        if g:
                            pe.wait_ge(s["stacked"], 3 * g)
                        for n, parts in ((1, k_parts), (0, q_parts)):
                            for k in range(3):
                                a = (g * 6 + 3 * n + k) * P
                                last = nc.tensor.matmul(bank(7 - n), stack16[:, a:a + P], parts[:, k * T:(k + 1) * T],
                                                        start=(k == 0), stop=(k == 2))
                            last.then_inc(s["stack"], 1)

                    def scores(h):
                        g = h // 2
                        if h >= 2:
                            pe.wait_ge(s["sum"], 4 * (h - 1))
                        base = 1536 * (h % 2)
                        for i in (3, 2, 0, 1):
                            a = base + QREGION[i]
                            nc.tensor.matmul(PS[:, a:a + (i + 1) * P], qS[:, g * T + i * P:g * T + (i + 1) * P],
                                             kz[:, h * T:h * T + (i + 1) * P], start=True, stop=False)
                            nc.tensor.matmul(PS[:, a + i * P:a + (i + 1) * P], ident16[:, :], causal16[:, :],
                                             start=False, stop=True).then_inc(s["scores"], 1)

                    pe.wait_ge(s["part"], 6)
                    pe.wait_ge(s["v_act"], NT)
                    pe.wait_ge(s["v_dve"], NT)
                    stack(0)
                    for g in range(G0):
                        if g < G0 - 1:
                            stack(g + 1)
                        pe.wait_ge(s["stacked"], 3 * g + 3)
                        scores(2 * g)
                        scores(2 * g + 1)
                    pe.wait_ge(s["shift_parts"], 3)
                    pe.wait_ge(s["log"], 1)
                    for i in range(NT):
                        nc.tensor.transpose(PS[0:3 * H0, i * P:(i + 1) * P],
                                            shift_parts[:, i * 3 * H0:(i + 1) * 3 * H0], ident
                                            ).then_inc(s["shiftT"], 1)
                    pe.wait_ge(s["shiftT_copied"], 1)
                    for g in range(G0):
                        nc.tensor.matmul(bank(g), shift16[:, g * P:(g + 1) * P], shiftT16[:, :], start=True, stop=True
                                         ).then_inc(s["shift_mm"], 1)

                    def scores_T(h):
                        g = h // 2
                        base = 1536 * (h % 2)
                        if h < 2:
                            pe.wait_ge(s["shifted"], 3 * (h + 1))
                        else:
                            pe.wait_ge(s["probs"], h - 1)
                        for j in (0, 1, 3, 2):
                            a = base + REGION[j]
                            n = T - j * P
                            nc.tensor.matmul(PS[:, a:a + n], kz[:, h * T + j * P:h * T + (j + 1) * P],
                                             qS[:, g * T + j * P:(g + 1) * T], start=True, stop=False)
                            last = nc.tensor.matmul(PS[:, a:a + P], ident16[:, :], causalT16[:, :],
                                                    start=False, stop=True)
                        last.then_inc(s["scoresT"], 1)

                    def context(h):
                        g, r = h // 2, 64 * (h % 2)
                        pe.wait_ge(s["probs"], h + 1)
                        if h == 0:
                            pe.wait_ge(s["shifted"], G0)
                        if h >= 4:
                            pe.wait_ge(s["ctxT"], g - 1)
                        for j in range(NT):
                            a = 1280 * (h % 2) + REGION[j]
                            n = T - j * P
                            last = nc.tensor.matmul(PS[r:r + DV0, (6 + g % 2) * BANK + j * P:(7 + g % 2) * BANK],
                                                    v0[:, (j * H0 + h) * DV0:(j * H0 + h + 1) * DV0],
                                                    probsT[:, a:a + n], start=(j == 0), stop=(j == NT - 1),
                                                    tile_position=(0, r))
                        last.then_inc(s["context"], 1)

                    for h in range(H0 + 1):
                        if h < H0:
                            scores_T(h)
                        if h >= 1:
                            context(h - 1)
                    pe.wait_ge(s["ctxT"], G0)
                    for t in range(NT):
                        for c in range(G0):
                            last = nc.tensor.matmul(bank(0, t * P, (t + 1) * P), ctx0T[:, c * T + t * P:c * T + (t + 1) * P],
                                                    wo0[:, c * P:(c + 1) * P], start=(c == 0), stop=(c == G0 - 1))
                    last.then_inc(s["attn"], 1)

                def v_copy(t, half):
                    return v0[:, (2 * t + half) * T:(2 * t + half + 1) * T], bank(2 + (2 * t + half) % 6)

                @block.scalar
                def _(act):
                    nc.scalar.copy(xnT_b[:, :], xnT_all[:, bass.ds(b * T, T)]).then_inc(s["xT_b"], 1)
                    for k in range(3):
                        for n, parts in enumerate((q_parts, k_parts)):
                            if k == 0:
                                act.wait_ge(s["qk"], n + 1)
                                src = bank(n)
                            else:
                                act.wait_ge(s["rest"], 2 * (k - 1) + n + 1)
                                src = rest[:, n * T:(n + 1) * T]
                            nc.scalar.copy(parts[:, k * T:(k + 1) * T], src).then_inc(s["part"], 1)
                        act.wait_ge(s["v"], 2 * k + 1)
                        nc.scalar.copy(*v_copy(k, 0)).then_inc(s["v_act"], 1)
                    act.wait_ge(s["v"], 7)
                    nc.scalar.copy(*v_copy(3, 0)).then_inc(s["v_act"], 1)

                    def stacks(g):
                        for e in range(2):
                            rows = slice(64 * e, 64 * e + 64)
                            act.wait_ge(s["stack"], 2 * g + 1)
                            nc.scalar.activation(kz[rows, (2 * g + e) * T:(2 * g + e + 1) * T], bank(6)[rows, :],
                                                 ACT.Identity, bias=cst[rows, C_KONE:C_KONE + 1]
                                                 ).then_inc(s["stacked"], 1)
                        act.wait_ge(s["stack"], 2 * g + 2)
                        nc.scalar.copy(qS[:, g * T:(g + 1) * T], bank(7)).then_inc(s["stacked"], 1)

                    stacks(0)
                    for h in range(H0):
                        if h % 2 == 0 and h < H0 - 2:
                            stacks(h // 2 + 1)
                        act.wait_ge(s["bias"], h + 1)
                        base = 1536 * (h % 2)
                        for n, i in enumerate((3, 2, 0, 1)):
                            if 4 * h + n >= 2:
                                act.wait_ge(s["sum"], 4 * h + n - 1)
                            a = base + QREGION[i]
                            nc.scalar.activation(rest[:, n % 2 * T:n % 2 * T + (i + 1) * P], PS[:, a:a + (i + 1) * P], ACT.Exp,
                                                 bias=bias0[:, h * NT + i:h * NT + i + 1], scale=scale0,
                                                 accum_out=sums0[:, h * NT + i:h * NT + i + 1]).then_inc(s["sum"], 1)
                    act.wait_ge(s["sum"], 4 * H0)
                    nc.scalar.activation(log_sums[:, :], sums0[:, :], ACT.Ln).then_inc(s["log"], 1)
                    act.wait_ge(s["shiftT"], NT)
                    nc.scalar.copy(shiftT16[:, :], PS[0:3 * H0, 0:T]).then_inc(s["shiftT_copied"], 1)
                    for h in range(H0):
                        act.wait_ge(s["scoresT"], h + 1)
                        if h >= 2:
                            act.wait_ge(s["context"], h - 1)
                        base = 1536 * (h % 2)
                        nc.scalar.activation(probsT[:, 1280 * (h % 2):1280 * (h % 2 + 1)], PS[:, base:base + 1280],
                                             ACT.Exp, scale=scale0).then_inc(s["probs"], 1)
                    act.wait_ge(s["moe"], NT)
                    nc.scalar.activation(moe[:, :], moe[:, :], ACT.Silu).then_inc(s["silu"], 1)

                @block.vector
                def _(dve):
                    nc.vector.tensor_copy(weight_b[:, :], route_w[:, bass.ds(b * 2 * NT, 2 * NT)]).then_inc(s["weight_b"], 1)
                    for k in range(2):
                        for n, parts in enumerate((q_parts, k_parts)):
                            dve.wait_ge(s["part"], 2 * k + n + 1)
                            src = bank(n) if k == 0 else rest[:, n * T:(n + 1) * T]
                            nc.vector.tensor_tensor(rest[:, n * T:(n + 1) * T], src, parts[:, k * T:(k + 1) * T],
                                                    ALU.subtract).then_inc(s["rest"], 1)
                        dve.wait_ge(s["v"], 2 * k + 2)
                        nc.vector.tensor_copy(*v_copy(k, 1)).then_inc(s["v_dve"], 1)
                    for k in (2, 3):
                        dve.wait_ge(s["v"], 2 * k + 2)
                        nc.vector.tensor_copy(*v_copy(k, 1)).then_inc(s["v_dve"], 1)

                    for h in range(H0):
                        base = 1536 * (h % 2)
                        for n, i in enumerate((3, 2, 0, 1)):
                            dve.wait_ge(s["scores"], 4 * h + (1, 3, 3, 4)[n])
                            a = base + QREGION[i]
                            nc.vector.reduce_max(row_max[:, h * NT + i:h * NT + i + 1], PS[:, a:a + (i + 1) * P],
                                                 AX_X).then_inc(s["max"], 1)
                        dve.wait_ge(s["max"], 4 * h + 4)
                        nc.vector.tensor_scalar(bias0[:, h * NT:(h + 1) * NT], row_max[:, h * NT:(h + 1) * NT], -scale0,
                                                None, ALU.mult).then_inc(s["bias"], 1)
                    dve.wait_ge(s["log"], 1)
                    nc.vector.scalar_tensor_tensor(shift_rest[:, :].rearrange("p (i h) -> p h i", h=H0),
                                                   log_sums[:, :].rearrange("p (h i) -> p h i", i=NT), -1.0 / scale0,
                                                   row_max[:, :].rearrange("p (h i) -> p h i", i=NT),
                                                   ALU.mult, ALU.subtract).then_inc(s["shift_rest"], 1)
                    split_steps(nc, dve, s, shift_rest[:, :], shift_part[:, :], shift_parts[:, :], H0, 0)
                    for g in range(G0):
                        dve.wait_ge(s["shift_mm"], g + 1)
                        nc.vector.tensor_tensor(qS[:, g * T:(g + 1) * T], qS[:, g * T:(g + 1) * T], bank(g),
                                                ALU.add).then_inc(s["shifted"], 1)
                    dve.wait_ge(s["weight_b"], 1)
                    dve.wait_ge(gathered, b * (16 * 2 * NT) + 16 * 2 * NT)
                    for t in range(NT):
                        nc.vector.tensor_scalar(moe[:, t * P:(t + 1) * P], picked[:, 2 * t * P:(2 * t + 1) * P],
                                                weight_b[:, 2 * t:2 * t + 1], None, ALU.mult).then_inc(s["moe_half"], 1)
                    for t in range(NT):
                        dve.wait_ge(s["moe_half"], t + 1)
                        nc.vector.scalar_tensor_tensor(moe[:, t * P:(t + 1) * P], picked[:, (2 * t + 1) * P:(2 * t + 2) * P],
                                                       weight_b[:, 2 * t + 1:2 * t + 2], moe[:, t * P:(t + 1) * P],
                                                       ALU.mult, ALU.add).then_inc(s["moe"], 1)
                    dve.wait_ge(s["moe"], NT)
                    for g in range(G0):
                        dve.wait_ge(s["context"], 2 * g + 2)
                        nc.vector.tensor_copy(ctx0T[:, g * T:(g + 1) * T], bank(6 + g % 2)).then_inc(s["ctxT"], 1)
                    dve.wait_ge(s["silu"], 1)
                    dve.wait_ge(s["attn"], 1)
                    nc.vector.tensor_tensor(x1[:, :], bank(0), moe[:, :], ALU.mult).then_inc(s["gated"], 1)
                    dve.wait_ge(s["gated"], 1)
                    nc.vector.tensor_tensor(x1[:, :], x1[:, :], x_all[:, bass.ds(b * T, T)], ALU.add).then_inc(s["x1"], 1)
            end_phase()
            layer0.close()

            layer1 = ctx.enter_context(ExitStack())

            def sb2(name, cols, dt=F32, rows=P):
                return layer1.enter_context(nc.sbuf_tensor(name, [rows, cols], dt))

            s1 = sb2("s1", T)

            delta = ctx.enter_context(ExitStack())

            def sb3(name, cols, dt=F32, rows=P):
                return delta.enter_context(nc.sbuf_tensor(name, [rows, cols], dt))

            padded = sb3("padded", 3 * (T + 4))
            conv = sb3("conv", 3 * T)
            beta = sb3("beta", T)
            decay = sb3("decay", T)
            keep_in = sb3("keep_in", T)
            mix = sb3("mix", T)
            squares = sb3("squares", 2 * T)
            norm = sb3("norm", 2 * T)
            qk_n = sb3("qk_n", 2 * T)
            scaled = sb3("scaled", 2 * T)
            ema_in = sb3("ema_in", T)
            ema = sb3("ema", T)
            rows3 = sb3("rows3", 3 * T)
            low = sb3("low", 3 * T)
            inv_t = sb3("inv_t", 2 * T)
            level = squares[:, T:2 * T]
            product = norm[:, T:2 * T]
            uw = sb3("uw", 2 * T)
            u_new = sb3("u_new", P)
            state = sb3("state", 2 * P)
            out1 = sb3("out1", T)
            diff = scaled[:, 0:T]
            NCH = T // CH

            def mask(n):
                a = C_DELTA + n * CH
                return cst[:, a:a + CH].unsqueeze(1).to_broadcast([P, NCH, CH])

            def g32(ap):
                return ap.rearrange("p (n j) -> p n j", j=CH)

            def chunks():
                for n in range(NCH):
                    t, c = divmod(n, 4)
                    for h in range(H1):
                        yield slice(32 * c, 32 * c + 32), (t * H1 + h) * CH, slice(32 * h, 32 * h + 32), n * CH, \
                            t * P + h * DH1

            s = phase("stats moments variance rstd normed transposed T_copied pads qkv pad_copied conv silu gates sigmoid squares sumsq root inverse qk_n scaled ema_in ema "
                      "rowsT rows_act rows_dve kk low flipped inv level product product_copied updated added uw_mm uw_act uw_dve "
                      "w_state u_new s_updated s_copied out_mm diff mixed out1 o_sq o_ms o_root o_inverse o_final "
                      "s1_mm s1".split())
            with nc.Block() as block:
                @block.tensor
                def _(pe):
                    for t in range(NT):
                        pe.wait_ge(s["normed"], t + 1)
                        nc.tensor.transpose(bank(7, t * P, (t + 1) * P), xn_b[:, t * P:(t + 1) * P],
                                            ident).then_inc(s["transposed"], 1)
                    pe.wait_ge(s["T_copied"], 1)
                    for n, w in enumerate((wq1, wk1, wv1)):
                        nc.tensor.matmul(bank(n), w[:, :], xnT_b[:, :], start=True, stop=True).then_inc(s["qkv"], 1)
                    for n in range(3):
                        pe.wait_ge(s["pad_copied"], n + 1)
                        nc.tensor.matmul(bank(n), w_gates[:, n * P:(n + 1) * P], xnT_b[:, :], start=True,
                                         stop=True).then_inc(s["gates"], 1)
                    for n in range(2):
                        pe.wait_ge(s["squares"], n + 1)
                        pe.wait_ge(s["sigmoid"], 4)
                        nc.tensor.matmul(bank(n), cst[:, C_BLK32:C_BLK32 + P], squares[:, n * T:(n + 1) * T],
                                         start=True, stop=True).then_inc(s["sumsq"], 1)
                    pe.wait_ge(s["root"], 2)
                    for n in range(3):
                        src = (qk_n[:, T:2 * T], scaled[:, 0:T], scaled[:, T:2 * T])[n]
                        if n == 0:
                            pe.wait_ge(s["qk_n"], 2)
                        else:
                            pe.wait_ge(s["scaled"], n)
                        for t in range(NT):
                            nc.tensor.transpose(bank(n, t * P, (t + 1) * P), src[:, t * P:(t + 1) * P],
                                                ident).then_inc(s["rowsT"], 1)
                    pe.wait_ge(s["rows_act"], 2)
                    pe.wait_ge(s["rows_dve"], 1)
                    pairs = ((scaled, 0, qk_n, T), (qk_n, T, qk_n, 0))
                    for n, (a, ao, b_, bo) in enumerate(pairs):
                        for rc, blk, rh, tok, _ in chunks():
                            o = BANK * (rh.start // 32) + n * P + tok // P * CH
                            last = nc.tensor.matmul(PS[rc, o:o + CH],
                                                    a[rh, ao + tok:ao + tok + CH], b_[rh, bo + tok:bo + tok + CH],
                                                    start=True, stop=True, tile_position=(rh.start, rc.start))
                        last.then_inc(s["kk"], 1)
                    for l in range(4):
                        pe.wait_ge(s["level"], l + 1)
                        pe.wait_ge(s["added"], l + 1)
                        for rc, blk, _, _, _ in chunks():
                            last = nc.tensor.matmul(PS[rc, blk:blk + CH], level[rc, blk:blk + CH],
                                                    inv_t[rc, blk:blk + CH], start=True, stop=True,
                                                    tile_position=(rc.start, rc.start))
                        last.then_inc(s["product"], 1)
                        pe.wait_ge(s["product_copied"], l + 1)
                        pe.wait_ge(s["flipped"], l + 2)
                        for rc, blk, _, _, _ in chunks():
                            last = nc.tensor.matmul(PS[rc, BANK + blk:BANK + blk + CH],
                                                    inv_t[rc, T + blk:T + blk + CH], product[rc, blk:blk + CH],
                                                    start=True, stop=True, tile_position=(rc.start, rc.start))
                        last.then_inc(s["updated"], 1)
                    pe.wait_ge(s["flipped"], 6)
                    for rc, blk, _, _, feat in chunks():
                        last = nc.tensor.matmul(PS[rc, blk:blk + CH], inv_t[rc, T + blk:T + blk + CH],
                                                rows3[rc, 2 * T + feat:2 * T + feat + CH], start=True, stop=True,
                                                tile_position=(rc.start, rc.start))
                    last.then_inc(s["uw_mm"], 1)
                    for rc, blk, rh, tok, feat in chunks():
                        o = BANK * (1 + rc.start // 32) + tok // P * CH
                        last = nc.tensor.matmul(PS[rh, o:o + CH], rows3[rc, T + feat:T + feat + CH],
                                                inv_t[rc, T + blk:T + blk + CH], start=True, stop=True,
                                                tile_position=(rc.start, rh.start))
                    last.then_inc(s["uw_mm"], 1)
                    pe.wait_ge(s["uw_act"], 1)
                    pe.wait_ge(s["uw_dve"], 4)
                    todo = list(chunks())
                    for n in range(NCH):
                        mine = todo[n * H1:(n + 1) * H1]
                        rc, tok = mine[0][0], mine[0][3]
                        st = state[:, (n % 2) * P:(n % 2 + 1) * P]
                        if n:
                            pe.wait_ge(s["s_copied"], n)
                            nc.tensor.matmul(PS[rc, 0:P], uw[:, T + tok:T + tok + CH], st, start=True, stop=True,
                                             tile_position=(0, rc.start)).then_inc(s["w_state"], 1)
                        pe.wait_ge(s["u_new"], n + 1)
                        t = n // 4
                        nc.tensor.matmul(bank(1, 0, P), rows3[rc, t * P:(t + 1) * P], u_new[rc, :], start=(n == 0),
                                         stop=True, tile_position=(rc.start, 0),
                                         skip_group_check=True).then_inc(s["s_updated"], 1)
                        if n:
                            nc.tensor.matmul(bank(2, tok, tok + CH), st, qk_n[:, tok:tok + CH], start=True, stop=True)
                        for h, (rc, blk, rh, tok, feat) in enumerate(mine):
                            last = nc.tensor.matmul(PS[rh, 3 * BANK + tok:3 * BANK + tok + CH],
                                                    u_new[rc, h * DH1:(h + 1) * DH1],
                                                    low[rc, 2 * T + blk:2 * T + blk + CH], start=True, stop=True,
                                                    tile_position=(rc.start, rh.start))
                        last.then_inc(s["out_mm"], 1)
                    pe.wait_ge(s["o_sq"], 1)
                    nc.tensor.matmul(bank(0), cst[:, C_BLK32:C_BLK32 + P], squares[:, 0:T], start=True,
                                     stop=True).then_inc(s["o_ms"], 1)
                    pe.wait_ge(s["o_final"], 1)
                    for t in range(NT):
                        last = nc.tensor.matmul(bank(1, t * P, (t + 1) * P), out1[:, t * P:(t + 1) * P], wo1[:, :],
                                                start=True, stop=True)
                    last.then_inc(s["s1_mm"], 1)

                @block.scalar
                def _(act):
                    act.wait_ge(s["transposed"], NT)
                    nc.scalar.copy(xnT_b[:, :], bank(7)).then_inc(s["T_copied"], 1)
                    act.wait_ge(s["pads"], 1)
                    for n in range(3):
                        act.wait_ge(s["qkv"], n + 1)
                        a = n * (T + 4) + 3
                        nc.scalar.copy(padded[:, a:a + T], bank(n)).then_inc(s["pad_copied"], 1)
                    act.wait_ge(s["gates"], 3)
                    nc.scalar.activation(beta[:, :], bank(0), ACT.Sigmoid).then_inc(s["sigmoid"], 1)
                    nc.scalar.activation(decay[:, :], bank(1), ACT.Sigmoid).then_inc(s["sigmoid"], 1)
                    nc.scalar.activation(keep_in[:, :], bank(1), ACT.Sigmoid, scale=-1.0).then_inc(s["sigmoid"], 1)
                    nc.scalar.activation(mix[:, :], bank(2), ACT.Sigmoid, bias=column[:, 0:1]).then_inc(s["sigmoid"], 1)
                    for n in range(3):
                        act.wait_ge(s["conv"], 4 * (n + 1))
                        nc.scalar.activation(conv[:, n * T:(n + 1) * T], conv[:, n * T:(n + 1) * T],
                                             ACT.Silu).then_inc(s["silu"], 1)
                    act.wait_ge(s["silu"], 3)
                    for n in range(2):
                        nc.scalar.square(squares[:, n * T:(n + 1) * T], conv[:, n * T:(n + 1) * T]
                                         ).then_inc(s["squares"], 1)
                    for n in range(2):
                        act.wait_ge(s["sumsq"], n + 1)
                        nc.scalar.activation(norm[:, n * T:(n + 1) * T], bank(n), ACT.Sqrt,
                                             bias=eps[:, 1:2]).then_inc(s["root"], 1)
                    for n in (0, 2):
                        act.wait_ge(s["rowsT"], NT * (n + 1))
                        nc.scalar.copy(rows3[:, n * T:(n + 1) * T], bank(n)).then_inc(s["rows_act"], 1)
                    for l in range(4):
                        act.wait_ge(s["product"], l + 1)
                        nc.scalar.copy(product[:, :], bank(0)).then_inc(s["product_copied"], 1)
                    act.wait_ge(s["uw_mm"], 1)
                    nc.scalar.copy(uw[:, 0:T], bank(0)).then_inc(s["uw_act"], 1)
                    act.wait_ge(s["mixed"], 2)
                    nc.scalar.square(squares[:, 0:T], out1[:, :]).then_inc(s["o_sq"], 1)
                    act.wait_ge(s["o_ms"], 1)
                    nc.scalar.activation(norm[:, 0:T], bank(0), ACT.Sqrt, bias=eps[:, 0:1],
                                         scale=1.0 / DH1).then_inc(s["o_root"], 1)
                    act.wait_ge(s["s1_mm"], 1)
                    nc.scalar.copy(s1[:, :], bank(1)).then_inc(s["s1"], 1)

                @block.gpsimd
                def _(gp):
                    gp.wait_ge(s["variance"], 1)
                    nc.gpsimd.tensor_tensor(rstd[:, :], var_eps[:, :], minus_half[:, :], ALU.pow).then_inc(s["rstd"], 1)
                    gp.wait_ge(s["silu"], 3)
                    gp.wait_ge(s["sigmoid"], 4)
                    nc.gpsimd.tensor_tensor(ema_in[:, :], conv[:, 2 * T:3 * T], keep_in[:, :], ALU.mult
                                            ).then_inc(s["ema_in"], 1)

                @block.vector
                def _(dve):
                    layer_norm_steps(nc, s, dve, lambda t: x1[:, t * P:(t + 1) * P], stats, moments,
                                     var_eps, rstd, lambda t: xn_b[:, t * P:(t + 1) * P])
                    nc.vector.memset(padded[:, :].rearrange("p (n c) -> p n c", n=3)[:, :, 0:3], 0.0
                                     ).then_inc(s["pads"], 1)
                    for n in range(3):
                        a = n * (T + 4)
                        to = conv[:, n * T:(n + 1) * T]
                        dve.wait_ge(s["pad_copied"], n + 1)
                        nc.vector.tensor_scalar(to, padded[:, a:a + T], conv_w[:, 4 * n:4 * n + 1], None,
                                                ALU.mult).then_inc(s["conv"], 1)
                        for j in range(1, 4):
                            dve.wait_ge(s["conv"], 4 * n + j)
                            nc.vector.scalar_tensor_tensor(to, padded[:, a + j:a + j + T],
                                                           conv_w[:, 4 * n + j:4 * n + j + 1], to,
                                                           ALU.mult, ALU.add).then_inc(s["conv"], 1)
                    for n in range(2):
                        dve.wait_ge(s["root"], n + 1)
                        nc.vector.reciprocal(norm[:, n * T:(n + 1) * T], norm[:, n * T:(n + 1) * T]
                                             ).then_inc(s["inverse"], 1)
                        dve.wait_ge(s["inverse"], n + 1)
                        nc.vector.tensor_tensor(qk_n[:, n * T:(n + 1) * T], conv[:, n * T:(n + 1) * T],
                                                norm[:, n * T:(n + 1) * T], ALU.mult).then_inc(s["qk_n"], 1)
                    dve.wait_ge(s["qk_n"], 2)
                    nc.vector.tensor_tensor(scaled[:, 0:T], qk_n[:, T:2 * T], beta[:, :], ALU.mult
                                            ).then_inc(s["scaled"], 1)
                    nc.vector.tensor_tensor(scaled[:, T:2 * T], conv[:, 2 * T:3 * T], beta[:, :], ALU.mult
                                            ).then_inc(s["scaled"], 1)
                    dve.wait_ge(s["ema_in"], 1)
                    nc.vector.tensor_tensor_scan(ema[:, :], decay[:, :], ema_in[:, :], 0.0, ALU.mult, ALU.add
                                                 ).then_inc(s["ema"], 1)
                    dve.wait_ge(s["rowsT"], 2 * NT)
                    nc.vector.tensor_copy(rows3[:, T:2 * T], bank(1)).then_inc(s["rows_dve"], 1)
                    dve.wait_ge(s["kk"], 2)
                    for n in range(2):
                        m = C_DELTA + (D_NEGLO, D_INCLT)[n] * CH
                        for h in range(H1):
                            nc.vector.tensor_tensor(
                                low[:, 2 * n * T:(2 * n + 1) * T].rearrange("p (t h j) -> p t h j", h=H1, j=CH)[:, :, h, :],
                                g32(bank(h, n * P, (n + 1) * P)),
                                cst[:, m:m + CH].unsqueeze(1).to_broadcast([P, NT, CH]), ALU.mult
                            ).then_inc(s["low"], 1)
                    dve.wait_ge(s["low"], 8)
                    nc.vector.transpose(low[:, T:2 * T], low[:, 0:T]).then_inc(s["flipped"], 1)
                    nc.vector.tensor_tensor(g32(inv_t[:, 0:T]), g32(low[:, 0:T]), mask(D_M1), ALU.mult
                                            ).then_inc(s["inv"], 1)
                    dve.wait_ge(s["inv"], 1)
                    nc.vector.tensor_tensor(g32(inv_t[:, 0:T]), g32(inv_t[:, 0:T]), mask(D_EYE), ALU.add
                                            ).then_inc(s["added"], 1)
                    for l in range(4):
                        if l:
                            dve.wait_ge(s["product"], l)
                        else:
                            dve.wait_ge(s["flipped"], 1)
                        nc.vector.tensor_tensor(g32(level[:, :]), g32(low[:, T:2 * T]), mask(D_M2T + l), ALU.mult
                                                ).then_inc(s["level"], 1)
                        dve.wait_ge(s["added"], l + 1)
                        if l:
                            dve.wait_ge(s["updated"], l)
                        nc.vector.transpose(inv_t[:, T:2 * T], inv_t[:, 0:T]).then_inc(s["flipped"], 1)
                        dve.wait_ge(s["updated"], l + 1)
                        dve.wait_ge(s["flipped"], l + 2)
                        nc.vector.tensor_tensor(inv_t[:, 0:T], inv_t[:, 0:T], bank(1), ALU.add
                                                ).then_inc(s["added"], 1)
                    dve.wait_ge(s["added"], 5)
                    nc.vector.transpose(inv_t[:, T:2 * T], inv_t[:, 0:T]).then_inc(s["flipped"], 1)
                    dve.wait_ge(s["uw_mm"], 2)
                    for c in range(4):
                        nc.vector.tensor_copy(
                            uw[:, T:2 * T].rearrange("p (t c j) -> p t c j", c=4, j=CH)[:, :, c, :],
                            g32(bank(1 + c, 0, P))).then_inc(s["uw_dve"], 1)
                    block_mask = cst[:, C_BLK32:C_BLK32 + P]
                    for n in range(NCH):
                        t, c = divmod(n, 4)
                        rc = slice(32 * c, 32 * c + 32)
                        if n == 0:
                            dve.wait_ge(s["uw_act"], 1)
                            nc.vector.tensor_copy(u_new[rc, :], uw[rc, 0:P]).then_inc(s["u_new"], 1)
                        else:
                            dve.wait_ge(s["w_state"], n)
                            if n >= 4:
                                dve.wait_ge(s["out_mm"], n - 3)
                            nc.vector.tensor_tensor(u_new[rc, :], uw[rc, t * P:(t + 1) * P], PS[rc, 0:P],
                                                    ALU.subtract).then_inc(s["u_new"], 1)
                        if n < NCH - 1:
                            dve.wait_ge(s["s_updated"], n + 1)
                            if n:
                                dve.wait_ge(s["out_mm"], n)
                            a = ((n + 1) % 2) * P
                            nc.vector.tensor_tensor(state[:, a:a + P], bank(1, 0, P), block_mask, ALU.mult
                                                    ).then_inc(s["s_copied"], 1)
                    dve.wait_ge(s["out_mm"], NCH)
                    dve.wait_ge(s["ema"], 1)
                    nc.vector.tensor_copy(out1[:, :], bank(3)).then_inc(s["diff"], 1)
                    dve.wait_ge(s["diff"], 1)
                    nc.vector.tensor_tensor(out1[:, CH:T], out1[:, CH:T], bank(2, CH, T), ALU.add
                                            ).then_inc(s["diff"], 1)
                    dve.wait_ge(s["diff"], 2)
                    nc.vector.tensor_tensor(diff[:, :], ema[:, :], out1[:, :], ALU.subtract).then_inc(s["diff"], 1)
                    dve.wait_ge(s["diff"], 3)
                    nc.vector.tensor_tensor(diff[:, :], diff[:, :], mix[:, :], ALU.mult).then_inc(s["mixed"], 1)
                    dve.wait_ge(s["mixed"], 1)
                    nc.vector.tensor_tensor(out1[:, :], diff[:, :], out1[:, :], ALU.add).then_inc(s["mixed"], 1)
                    dve.wait_ge(s["o_root"], 1)
                    nc.vector.reciprocal(norm[:, 0:T], norm[:, 0:T]).then_inc(s["o_inverse"], 1)
                    dve.wait_ge(s["o_inverse"], 1)
                    nc.vector.scalar_tensor_tensor(out1[:, :], out1[:, :], column[:, 1:2], norm[:, 0:T],
                                                   ALU.mult, ALU.mult).then_inc(s["o_final"], 1)
            end_phase()
            delta.close()

            KX = P + WIN
            HH = H2 // 2
            QK = 2 * H2 * D2
            y = sb2("y", NT * P)
            hT = sb2("hT", T)
            hs = sb2("hs", NT * P)
            v2 = sb2("v2", NT * H2 * D2)
            squares2 = sb2("squares2", 2 * QK)
            normed2 = sb2("normed2", 2 * QK)
            rot = sb2("rot", 2 * QK)
            rot_sin = sb2("rot_sin", 2 * QK)
            norm2 = sb2("norm2", NT * 2 * H2)
            clip2 = sb2("clip2", NT * 2 * H2)
            inv2 = sb2("inv2", NT * 2 * H2)
            q2 = sb2("q2", 4 * T)
            row_max2 = sb2("row_max2", H2 * NT)
            bias2 = sb2("bias2", H2 * NT)
            sums2 = sb2("sums2", H2 * NT)
            log_sums2 = sb2("log_sums2", H2 * NT)
            shift_rest2 = sb2("shift_rest2", NT * H2)
            shift_part2 = sb2("shift_part2", NT * H2, BF16)
            shift_parts2 = sb2("shift_parts2", NT * 3 * H2)
            shiftT2 = sb2("shiftT2", 2 * T, BF16, 3 * HH)
            probs2 = sb2("probs2", 2 * 704)
            ctx2T = rot
            gelu = rot_sin
            glu = normed2
            final = v2[:, 0:T]
            Q_AT, Q_KEYS = (0, 128, 320, 512), (P, KX, KX, KX)
            K_AT, K_QUERIES = (0, 192, 512, 384), (KX, KX, KX, P)

            for l in range(DEPTH):
                s = phase("yT shift_low shift_high qk_mm v v_copied sq ss root clip inverse normed_qk cos sin rotated "
                          "turn_mm turned scores max bias sum log shift_rest shift_part shift_parts shiftT "
                          "shiftT_copied scoresT probs context ctxT wo y_new step_mm low high stats moments variance "
                          "rstd normed h_mm h_ready hidden gelu glu w2_mm y_out silu product final stored".split())
                before_y = xn_b if l == 0 else y
                with nc.Block() as block:
                    def halves(buf, t):
                        return buf[:, (t % 2) * QK:(t % 2 + 1) * QK].rearrange("p (n h r d) -> p n h r d", n=2, h=H2, r=2)

                    def heads(buf, t):
                        return buf[:, (t % 2) * QK:(t % 2 + 1) * QK].rearrange("p (n h d) -> p n h d", n=2, h=H2)

                    def table(n, t):
                        a = ((l * 4 + n) * NT + t) * D2
                        return tables[:, a:a + D2]

                    @block.tensor
                    def _(pe):
                        if l:
                            for t in range(NT):
                                nc.tensor.transpose(bank(0, t * P, (t + 1) * P), y[:, t * P:(t + 1) * P],
                                                    ident).then_inc(s["yT"], 1)
                        pe.wait_ge(s["shift_high"], 2)
                        pe.wait_ge(s["shift_low"], 1)

                        def project(t):
                            if t >= 2:
                                pe.wait_ge(s["normed_qk"], t - 1)
                                pe.wait_ge(s["v_copied"], t - 1)
                            for n in range(3):
                                a = l * 1536 + n * 512
                                k = 2 * (t % 2) + n if n < 2 else 4 + t % 2
                                last = nc.tensor.matmul(bank(k), hT[:, t * P:(t + 1) * P], wqkv[:, a:a + 512],
                                                        start=True, stop=True)
                                if n == 1:
                                    last.then_inc(s["qk_mm"], 1)
                            last.then_inc(s["v"], 1)

                        def turn(t):
                            pe.wait_ge(s["rotated"], t + 1)
                            if t:
                                pe.wait_ge(s["turned"], 3 * t)
                            for c in range(8):
                                a = (t % 2) * QK + c * P
                                last = nc.tensor.transpose(bank(6 + c // 4, c % 4 * P, (c % 4 + 1) * P), rot[:, a:a + P],
                                                           ident)
                            last.then_inc(s["turn_mm"], 1)

                        project(0)
                        for t in range(1, NT):
                            project(t)
                            if t >= 2:
                                turn(t - 2)
                        turn(NT - 2)
                        turn(NT - 1)
                        pe.wait_ge(s["turned"], 3 * NT)
                        def shifts_T(half):
                            pe.wait_ge(s["shift_parts"], 3 * half + 3)
                            for i in range(NT):
                                a = (half * NT + i) * 3 * HH
                                last = nc.tensor.transpose(PS[0:3 * HH, (6 + half) * BANK + i * P:(6 + half) * BANK + (i + 1) * P],
                                                           shift_parts2[:, a:a + 3 * HH], ident)
                            last.then_inc(s["shiftT"], 1)

                        for h in range(H2):
                            q0, base = (h // 2) * T, 2 * BANK * (h % 3)
                            if h >= 3:
                                pe.wait_ge(s["sum"], NT * (h - 2))
                            for i in range(NT):
                                a, n = base + Q_AT[i], Q_KEYS[i]
                                nc.tensor.matmul(PS[:, a:a + n], q2[:, q0 + i * P:q0 + (i + 1) * P],
                                                 kz2[:, h * T + (i + 1) * P - n:h * T + (i + 1) * P],
                                                 start=True, stop=False)
                                last = nc.tensor.matmul(PS[:, a:a + n], ident16[:, :], band16[:, KX - n:KX],
                                                        start=False, stop=True)
                            last.then_inc(s["scores"], 1)
                            if h == H2 - 2:
                                shifts_T(0)

                        def scores_T(h):
                            q0, base = (h // 2) * T, 2 * BANK * ((H2 + h) % 3)
                            if h < 3:
                                pe.wait_ge(s["sum"], NT * (H2 + h - 2))
                            else:
                                pe.wait_ge(s["probs"], h - 2)
                            if h % HH == 0:
                                pe.wait_ge(s["shiftT_copied"], h // HH + 1)
                            for j in range(NT):
                                a, n = base + K_AT[j], K_QUERIES[j]
                                nc.tensor.matmul(PS[:, a:a + n], kz2[:, h * T + j * P:h * T + (j + 1) * P],
                                                 q2[:, q0 + j * P:q0 + j * P + n], start=True, stop=False)
                                nc.tensor.matmul(PS[:, a:a + n], select16[:, (h % HH) * P:(h % HH + 1) * P],
                                                 shiftT2[:, h // HH * T + j * P:h // HH * T + j * P + n],
                                                 start=False, stop=False)
                                last = nc.tensor.matmul(PS[:, a:a + n], ident16[:, :], bandT16[:, 0:n],
                                                        start=False, stop=True)
                            last.then_inc(s["scoresT"], 1)

                        def context(h):
                            g, r = h // 2, 64 * (h % 2)
                            pe.wait_ge(s["probs"], h + 1)
                            if h >= 4:
                                pe.wait_ge(s["ctxT"], g - 1)
                            o = (6 + g % 2) * BANK
                            for j in range(NT):
                                a, n = 704 * (h % 2) + K_AT[j], K_QUERIES[j]
                                v = (j * H2 + h) * D2
                                last = nc.tensor.matmul(PS[r:r + D2, o + j * P:o + j * P + n], v2[:, v:v + D2],
                                                        probs2[:, a:a + n], start=(j == 0), stop=(j == NT - 1),
                                                        tile_position=(0, r), skip_group_check=True)
                            last.then_inc(s["context"], 1)

                        for h in range(H2 + 2):
                            if h == HH - 1:
                                shifts_T(1)
                            if h < H2:
                                scores_T(h)
                            if h >= 2:
                                context(h - 2)
                        pe.wait_ge(s["ctxT"], 4)
                        for t in range(NT):
                            for c in range(4):
                                k = l * 512 + c * P
                                last = nc.tensor.matmul(bank(0, t * P, (t + 1) * P),
                                                        ctx2T[:, c * T + t * P:c * T + (t + 1) * P],
                                                        w_oa_sb[:, k:k + P], start=(c == 0), stop=(c == 3))
                        last.then_inc(s["wo"], 1)
                        pe.wait_ge(s["y_new"], 1)
                        upper = y[:, :].rearrange("p (t r d) -> p t r d", r=2, d=64)[:, :, 1, :]
                        nc.tensor.matmul(bank(1, 0, 256), cst[:, C_STEP:C_STEP + P], upper, start=True, stop=True)
                        nc.tensor.matmul(bank(1, 64, 256), cst[:, C_CORNER:C_CORNER + P], upper[:, 0:3, :],
                                         start=False, stop=True, skip_group_check=True).then_inc(s["step_mm"], 1)
                        for t in range(NT):
                            pe.wait_ge(s["normed"], t + 1)
                            last = nc.tensor.transpose(bank(2, t * P, (t + 1) * P), hs[:, t * P:(t + 1) * P], ident)
                        last.then_inc(s["h_mm"], 1)
                        pe.wait_ge(s["h_ready"], 1)
                        for c, (start, n) in enumerate(HCH):
                            for half in range(2):
                                k = l * 2 * HID + half * HID + start
                                u = (3 + 2 * c + half) % 8
                                nc.tensor.matmul(PS[0:n, BANK * u:BANK * (u + 1)], w1_sb[:, k:k + n], hT[:, :],
                                                 start=True, stop=True).then_inc(s["hidden"], 1)
                        for c, (start, n) in enumerate(HCH):
                            pe.wait_ge(s["glu"], c + 1)
                            for t in range(NT):
                                o = bank(1, t * P, (t + 1) * P)
                                if c == 0:
                                    nc.tensor.matmul(o, ones_row, b2_sb[:, l * P:(l + 1) * P], start=(t == 0),
                                                     stop=(t == 0), skip_group_check=True)
                                k = (l * 3 + c) * P
                                last = nc.tensor.matmul(o, glu[0:n, c * T + t * P:c * T + (t + 1) * P],
                                                        w2_sb[0:n, k:k + P], start=False, stop=True,
                                                        skip_group_check=True)
                        last.then_inc(s["w2_mm"], 1)

                    @block.gpsimd
                    def _(gp):
                        for t in range(NT):
                            gp.wait_ge(s["normed_qk"], t + 1)
                            if t >= 2:
                                gp.wait_ge(s["rotated"], t - 1)
                            src, to = halves(normed2, t), halves(rot_sin, t)
                            for n in range(2):
                                for r in range(2):
                                    nc.gpsimd.tensor_tensor(
                                        to[:, n, :, r, :], src[:, n, :, 1 - r, :],
                                        table(2 * n + 1, t)[:, 32 * r:32 * r + 32].unsqueeze(1).to_broadcast([P, H2, 32]),
                                        ALU.mult).then_inc(s["sin"], 1)
                        gp.wait_ge(s["variance"], 1)
                        nc.gpsimd.tensor_tensor(rstd[:, :], var_eps[:, :], minus_half[:, :], ALU.pow).then_inc(s["rstd"], 1)

                    @block.scalar
                    def _(act):
                        src = xnT_b[:, :] if l == 0 else bank(0)
                        if l:
                            act.wait_ge(s["yT"], NT)
                        nc.scalar.copy(hT[0:64, :], src[0:64, :]).then_inc(s["shift_low"], 1)
                        nc.scalar.copy(hT[64:P, 1:T], src[64:P, 0:T - 1]).then_inc(s["shift_high"], 1)

                        def turned(t):
                            act.wait_ge(s["turn_mm"], t + 1)
                            nc.scalar.copy(q2[:, :].rearrange("p (g c) -> p g c", c=T)[:, :, t * P:(t + 1) * P],
                                           bank(6).rearrange("p (g c) -> p g c", c=P)).then_inc(s["turned"], 1)
                            for e in range(2):
                                rows = slice(64 * e, 64 * e + 64)
                                nc.scalar.copy(
                                    kz2[rows, :].rearrange("p (g e c) -> p g e c", e=2, c=T)[:, :, e, t * P:(t + 1) * P],
                                    bank(7)[rows, :].rearrange("p (g c) -> p g c", c=P)).then_inc(s["turned"], 1)

                        for t in range(NT):
                            act.wait_ge(s["qk_mm"], t + 1)
                            if t >= 2:
                                act.wait_ge(s["ss"], t - 1)
                            k = t % 2
                            nc.scalar.square(squares2[:, k * QK:(k + 1) * QK], PS[:, k * QK:(k + 1) * QK]
                                             ).then_inc(s["sq"], 1)
                            act.wait_ge(s["v"], t + 1)
                            nc.scalar.copy(v2[:, t * 512:(t + 1) * 512], bank(4 + k)).then_inc(s["v_copied"], 1)
                            act.wait_ge(s["ss"], t + 1)
                            nc.scalar.activation(norm2[:, t * 16:(t + 1) * 16], clip2[:, t * 16:(t + 1) * 16], ACT.Sqrt
                                                 ).then_inc(s["root"], 1)
                            if t >= 2:
                                turned(t - 2)
                        turned(NT - 2)
                        turned(NT - 1)
                        def shift_logs(half):
                            act.wait_ge(s["sum"], NT * HH * (half + 1))
                            at = slice(half * NT * HH, (half + 1) * NT * HH)
                            nc.scalar.activation(log_sums2[:, at], sums2[:, at], ACT.Ln).then_inc(s["log"], 1)

                        def shifts_copied(half):
                            act.wait_ge(s["shiftT"], half + 1)
                            nc.scalar.copy(shiftT2[:, half * T:(half + 1) * T],
                                           bank(6 + half)[0:3 * HH, :]).then_inc(s["shiftT_copied"], 1)

                        for h in range(H2):
                            base = 2 * BANK * (h % 3)
                            act.wait_ge(s["bias"], h + 1)
                            for i in range(NT):
                                m = NT * h + i
                                if m >= 4:
                                    act.wait_ge(s["sum"], m - 3)
                                a, n = base + Q_AT[i], Q_KEYS[i]
                                nc.scalar.activation(squares2[:, i * T:i * T + n], PS[:, a:a + n], ACT.Exp,
                                                     bias=bias2[:, m:m + 1], scale=8.0,
                                                     accum_out=sums2[:, m:m + 1]).then_inc(s["sum"], 1)
                            if h == HH - 1:
                                shift_logs(0)
                            if h == H2 - 2:
                                shifts_copied(0)
                        shift_logs(1)
                        for h in range(H2):
                            act.wait_ge(s["scoresT"], h + 1)
                            if h >= 2:
                                act.wait_ge(s["context"], h - 1)
                            base = 2 * BANK * ((H2 + h) % 3)
                            nc.scalar.activation(probs2[:, 704 * (h % 2):704 * (h % 2 + 1)], PS[:, base:base + 704],
                                                 ACT.Exp, scale=8.0).then_inc(s["probs"], 1)
                            if h == HH - 2:
                                shifts_copied(1)
                        act.wait_ge(s["y_new"], 1)
                        nc.scalar.copy(hs[:, :].rearrange("p (t r d) -> p t r d", r=2, d=64)[:, :, 0, :],
                                       y[:, :].rearrange("p (t r d) -> p t r d", r=2, d=64)[:, :, 0, :]
                                       ).then_inc(s["low"], 1)
                        act.wait_ge(s["h_mm"], 1)
                        nc.scalar.activation(hT[:, :], bank(2), ACT.Identity, bias=ln_sb[:, DEPTH + l:DEPTH + l + 1],
                                             scale=ln_sb[:, l:l + 1]).then_inc(s["h_ready"], 1)
                        for c, (start, n) in enumerate(HCH):
                            act.wait_ge(s["hidden"], 2 * c + 2)
                            if c == 2:
                                act.wait_ge(s["glu"], 1)
                            k = (c % 2) * T
                            u = (4 + 2 * c) % 8
                            b1 = (l * 2 + 1) * 3 + c
                            nc.scalar.activation(gelu[0:n, k:k + T], PS[0:n, BANK * u:BANK * (u + 1)],
                                                 ACT.Gelu, bias=b1_sb[0:n, b1:b1 + 1]).then_inc(s["gelu"], 1)
                        if l == DEPTH - 1:
                            act.wait_ge(s["y_out"], 1)
                            nc.scalar.activation(final, y[:, :], ACT.Silu).then_inc(s["silu"], 1)

                    @block.vector
                    def _(dve):
                        nc.vector.memset(hT[64:P, 0:1], 0.0).then_inc(s["shift_high"], 1)

                        def add_rotated(t):
                            dve.wait_ge(s["sin"], 4 * (t + 1))
                            dve.wait_ge(s["cos"], 2 * (t + 1))
                            k = (t % 2) * QK
                            nc.vector.tensor_tensor(rot[:, k:k + QK], rot[:, k:k + QK], rot_sin[:, k:k + QK], ALU.add
                                                    ).then_inc(s["rotated"], 1)

                        for t in range(NT):
                            k = t % 2
                            at = slice(t * 16, (t + 1) * 16)
                            dve.wait_ge(s["sq"], t + 1)
                            nc.vector.reduce_sum(clip2[:, at], heads(squares2, t).rearrange("p n h d -> p (n h) d"),
                                                 AX_X).then_inc(s["ss"], 1)
                            if t:
                                add_rotated(t - 1)
                            dve.wait_ge(s["root"], t + 1)
                            nc.vector.tensor_scalar(norm2[:, at], norm2[:, at], 1e-12, None, ALU.max
                                                    ).then_inc(s["clip"], 1)
                            dve.wait_ge(s["clip"], t + 1)
                            nc.vector.reciprocal(inv2[:, at], norm2[:, at]).then_inc(s["inverse"], 1)
                            dve.wait_ge(s["inverse"], t + 1)
                            if t >= 2:
                                dve.wait_ge(s["sin"], 4 * (t - 1))
                                dve.wait_ge(s["cos"], 2 * (t - 1))
                            nc.vector.tensor_tensor(
                                heads(normed2, t).rearrange("p n h d -> p (n h) d"),
                                PS[:, k * QK:(k + 1) * QK].rearrange("p (g d) -> p g d", d=D2),
                                inv2[:, at].unsqueeze(2).to_broadcast([P, 2 * H2, D2]), ALU.mult
                            ).then_inc(s["normed_qk"], 1)
                            dve.wait_ge(s["normed_qk"], t + 1)
                            if t >= 2:
                                dve.wait_ge(s["turn_mm"], t - 1)
                            for n in range(2):
                                nc.vector.tensor_tensor(
                                    heads(rot, t)[:, n], heads(normed2, t)[:, n],
                                    table(2 * n, t).unsqueeze(1).to_broadcast([P, H2, D2]), ALU.mult
                                ).then_inc(s["cos"], 1)
                        add_rotated(NT - 1)
                        def shifts(half):
                            at = slice(half * NT * HH, (half + 1) * NT * HH)
                            dve.wait_ge(s["log"], half + 1)
                            nc.vector.scalar_tensor_tensor(
                                shift_rest2[:, at].rearrange("p (i h) -> p h i", h=HH),
                                log_sums2[:, at].rearrange("p (h i) -> p h i", i=NT), -0.125,
                                row_max2[:, at].rearrange("p (h i) -> p h i", i=NT),
                                ALU.mult, ALU.subtract).then_inc(s["shift_rest"], 1)
                            split_steps(nc, dve, s, shift_rest2[:, at], shift_part2[:, at],
                                        shift_parts2[:, half * NT * 3 * HH:(half + 1) * NT * 3 * HH], HH, half)

                        for h in range(H2):
                            base = 2 * BANK * (h % 3)
                            m = NT * h
                            dve.wait_ge(s["scores"], h + 1)
                            nc.vector.reduce_max(row_max2[:, m:m + 1], PS[:, base:base + P], AX_X).then_inc(s["max"], 1)
                            nc.vector.reduce_max(row_max2[:, m + 1:m + 3],
                                                 PS[:, base + P:base + 512].rearrange("p (i k) -> p i k", k=KX),
                                                 AX_X).then_inc(s["max"], 1)
                            nc.vector.reduce_max(row_max2[:, m + 3:m + 4], PS[:, base + 512:base + 704], AX_X
                                                 ).then_inc(s["max"], 1)
                            dve.wait_ge(s["max"], 3 * (h + 1))
                            nc.vector.tensor_scalar(bias2[:, m:m + NT], row_max2[:, m:m + NT], -8.0, None, ALU.mult
                                                    ).then_inc(s["bias"], 1)
                            if h == HH:
                                shifts(0)
                        shifts(1)
                        for g in range(4):
                            dve.wait_ge(s["context"], 2 * g + 2)
                            nc.vector.tensor_copy(ctx2T[:, g * T:(g + 1) * T], bank(6 + g % 2)).then_inc(s["ctxT"], 1)
                        dve.wait_ge(s["wo"], 1)
                        nc.vector.tensor_tensor(y[:, :], before_y[:, :], bank(0), ALU.add).then_inc(s["y_new"], 1)
                        dve.wait_ge(s["step_mm"], 1)
                        nc.vector.tensor_copy(hs[:, :].rearrange("p (t r d) -> p t r d", r=2, d=64)[:, :, 1, :],
                                              bank(1, 0, 256).rearrange("p (t d) -> p t d", d=64)).then_inc(s["high"], 1)
                        dve.wait_ge(s["low"], 1)
                        dve.wait_ge(s["high"], 1)
                        layer_norm_steps(nc, s, dve, lambda t: hs[:, t * P:(t + 1) * P], stats, moments,
                                         var_eps, rstd, lambda t: hs[:, t * P:(t + 1) * P])
                        for c, (start, n) in enumerate(HCH):
                            dve.wait_ge(s["gelu"], c + 1)
                            u = (3 + 2 * c) % 8
                            b1 = l * 6 + c
                            nc.vector.scalar_tensor_tensor(glu[0:n, c * T:(c + 1) * T],
                                                           PS[0:n, BANK * u:BANK * (u + 1)], b1_sb[0:n, b1:b1 + 1],
                                                           gelu[0:n, (c % 2) * T:(c % 2 + 1) * T], ALU.add, ALU.mult
                                                           ).then_inc(s["glu"], 1)
                        dve.wait_ge(s["w2_mm"], 1)
                        nc.vector.tensor_tensor(y[:, :], y[:, :], bank(1), ALU.add).then_inc(s["y_out"], 1)
                        if l == DEPTH - 1:
                            dve.wait_ge(s["silu"], 1)
                            nc.vector.tensor_tensor(final, final, s1[:, :], ALU.mult).then_inc(s["product"], 1)
                            dve.wait_ge(s["product"], 1)
                            nc.vector.tensor_tensor(final, final, x1[:, :], ALU.add).then_inc(s["final"], 1)

                    @block.sync
                    def _(sp):
                        if l == DEPTH - 1:
                            sp.wait_ge(s["final"], 1)
                            sp.dma_start(out[bass.ds(b, 1)].rearrange("o (t p) f -> p (o t) f", p=P),
                                         final.rearrange("p (t f) -> p t f", f=P)).then_inc(s["stored"], 16)
                            sp.wait_ge(s["stored"], 16)
                end_phase()




_INS = ['L0_attn_x', 'L0_attn_Wq', 'L0_attn_Wk', 'L0_attn_Wv', 'L0_attn_Wo', 'L0_ffn_w_gate', 'L0_ffn_c_fc',
        'L0_ffn_c_proj', 'L1_attn_Wq', 'L1_attn_Wk', 'L1_attn_Wv', 'L1_attn_Wb', 'L1_attn_Wdec', 'L1_attn_Wmix',
        'L1_attn_mix_bias', 'L1_attn_wq_conv', 'L1_attn_wk_conv', 'L1_attn_wv_conv', 'L1_attn_onorm_w', 'L1_attn_Wo',
        'L1_ffn_wqkv', 'scales', 'L1_ffn_wo', 'L1_ffn_ln_g', 'L1_ffn_ln_b', 'L1_ffn_w1',
        'L1_ffn_b1', 'L1_ffn_w2', 'L1_ffn_b2', 'constants']
_TRANSPOSED = {'L1_attn_Wq', 'L1_attn_Wk', 'L1_attn_Wv', 'L1_attn_Wb', 'L1_attn_Wdec', 'L1_attn_Wmix', 'L1_attn_Wo', 'L1_ffn_ln_g',
               'L1_ffn_ln_b'}
_FLAT = {'L0_ffn_c_fc', 'L0_ffn_c_proj'}


def laid_out(name, inputs):
    if name == 'constants':
        return constants()
    if name == 'scales':
        both = []
        for layer in range(DEPTH):
            for n in ('L1_ffn_q_scale', 'L1_ffn_k_scale'):
                a = np.asarray(inputs[n])[layer]
                both += [a, np.roll(a, D2 // 2)]
        return np.ascontiguousarray(np.broadcast_to(np.concatenate(both), (P, 4 * DEPTH * D2)))
    a = np.asarray(inputs[name])
    if name == 'L1_attn_mix_bias':
        a = np.repeat(a, DH1)[:, None]
    if name == 'L1_attn_onorm_w':
        a = np.tile(a, H1)[:, None]
    if name in _TRANSPOSED:
        a = a.T
    if name in _FLAT:
        a = a.reshape(-1, a.shape[-1])
    return np.ascontiguousarray(a)


def kernel(**inputs):
    import concourse.bacc as _bacc
    from concourse import mybir as _mybir
    from concourse.bass_utils import run_bass_kernel_spmd as _run

    nc = _bacc.Bacc("TRN2", target_bir_lowering=False, num_devices=1)
    arrays, args = {}, []
    for name in _INS:
        a = laid_out(name, inputs)
        arrays[f"in_{name}_dram"] = a
        args.append(nc.dram_tensor(f"in_{name}_dram", a.shape, _mybir.dt.from_np(a.dtype), kind="ExternalInput").ap())
    out = nc.dram_tensor("out_0_dram", (B, T, P), _mybir.dt.float32, kind="ExternalOutput").ap()
    network(nc, args, out)
    r = _run(nc, [arrays], core_ids=[0])
    return r.results[0]["out_0_dram"]
```

```python
from contextlib import ExitStack

import numpy as np

import concourse.bass as bass
from concourse import mybir

F32 = mybir.dt.float32
BF16 = mybir.dt.bfloat16
U32 = mybir.dt.uint32
ALU = mybir.AluOpType
ACT = mybir.ActivationFunctionType
AX_X = mybir.AxisListType.X

P = 128
B, T = 8, 512
NT = T // P
NTILE = B * NT
BANK = 512
NEG = -1e30

H0, DK0, DV0 = 16, 8, 64
G0 = 8
Q_PART, K_PART = (0, 0, 1, 0, 2, 1, 1), (0, 1, 0, 2, 0, 1, 2)
LSE_ROW = 8 * len(Q_PART)
NE, CAP, HALF = 8, 512, 192
HC = 96
H1, DH1, CH = 4, 32, 32
DEPTH, H2, D2, WIN = 2, 8, 64, 64
HID = int(P * 4 * 2 / 3)
HCH = [(0, 128), (128, 128), (256, HID - 256)]

C_ID, C_USTRICT, C_ONES, C_STEP = 0, 128, 256, 384
C_BLK32, C_CORNER = 512, 640
C_CAUSAL, C_CAUSALT = 768, 896
C_BAND, C_BANDT = 1024, 1216
C_DELTA = 1408
C_IOTA = C_DELTA + 320
C_KONE = C_IOTA + 8
C_SEL = C_KONE + 1
C_COS = C_SEL + H2
C_STACK = C_COS + 4 * NT * D2
C_STACKG = C_STACK + 6 * P
C_SHIFT = C_STACKG + 8
C_SHIFTG = C_SHIFT + P
C_END = C_SHIFTG + 8
(D_NEGLO, D_NEGLOT, D_INCLT, D_EYE, D_M1, D_M1T, D_M2T, D_M4T, D_M8T, D_M16T) = range(10)


def constants():
    c = np.zeros((P, C_END), np.float32)
    p = np.arange(P)[:, None]
    f = np.arange(P)[None, :]
    c[:, C_ID:C_ID + P] = p == f
    c[:, C_USTRICT:C_USTRICT + P] = p < f
    c[:, C_ONES:C_ONES + P] = 1.0
    c[:, C_STEP:C_STEP + P] = p == f - 1
    c[:, C_BLK32:C_BLK32 + P] = p // DH1 == f // DH1
    c[:, C_CORNER:C_CORNER + P] = (p == P - 1) & (f == 0)
    c[:, C_CAUSAL:C_CAUSAL + P] = np.where(f > p, NEG, 0.0)
    c[:, C_CAUSALT:C_CAUSALT + P] = np.where(p > f, NEG, 0.0)
    w = np.arange(P + WIN)[None, :]
    gap = p - (w - WIN)
    c[:, C_BAND:C_BAND + P + WIN] = np.where((gap < 0) | (gap > WIN), NEG, 0.0)
    gap = w - p
    c[:, C_BANDT:C_BANDT + P + WIN] = np.where((gap < 0) | (gap > WIN), NEG, 0.0)
    i = p % CH
    j = np.arange(CH)[None, :]

    def lower(a, b, s):
        return (a // (2 * s) == b // (2 * s)) & (a % (2 * s) >= s) & (b % (2 * s) < s)

    masks = [-1.0 * (i > j), -1.0 * (i < j), j >= i, i == j, lower(i, j, 1), lower(j, i, 1),
             lower(j, i, 2), lower(j, i, 4), lower(j, i, 8), lower(j, i, 16)]
    for n, m in enumerate(masks):
        c[:, C_DELTA + n * CH:C_DELTA + (n + 1) * CH] = m
    c[:, C_IOTA:C_IOTA + NE] = np.arange(NE)
    c[:, C_KONE] = (np.arange(P) % 64 >= LSE_ROW) & (np.arange(P) % 64 < LSE_ROW + 3)
    c[:, C_SEL:C_SEL + H2 // 2] = (p % (H2 // 2) == np.arange(H2 // 2)) & (p < 3 * H2 // 2)
    r = f % 64 // DK0
    mine = (p % 16 // DK0 == f // 64) & (p % DK0 == f % DK0)
    for n, part in enumerate((Q_PART, K_PART)):
        of = np.array(list(part) + [-1])[r]
        for k in range(3):
            a = C_STACK + (3 * n + k) * P
            c[:, a:a + P] = mine & (of == k)
    c[:, C_STACKG:C_STACKG + G0] = p // 16 == np.arange(G0)
    c[:, C_SHIFT:C_SHIFT + P] = (p < 3 * G0) & (f % 64 == LSE_ROW + p // G0) & (p % 2 == f // 64)
    c[:, C_SHIFTG:C_SHIFTG + G0 // 2] = p % G0 // 2 == np.arange(G0 // 2)
    half = np.arange(0, D2, 2, dtype=np.float32)
    inv = (np.float32(1.0) / np.float32(10000.0) ** (half / np.float32(D2))).astype(np.float32)
    t = np.arange(T, dtype=np.float32)
    freqs = (t[:, None] * inv[None, :]).astype(np.float32)
    base = ((half + np.float32(0.4 * D2)) / np.float32(1.4 * D2)).astype(np.float32)
    power = ((t - T // 2) / np.float32(WIN // 2)).astype(np.float32)
    scale = (base[None, :] ** power[:, None]).astype(np.float32)
    cos, sin = np.cos(freqs), np.sin(freqs)
    for n, tab in enumerate((cos * scale, sin * scale, cos / scale, sin / scale)):
        first = -tab if n % 2 else tab
        rows = np.concatenate([first, tab], axis=1)
        c[:, C_COS + n * NT * D2:C_COS + (n + 1) * NT * D2] = rows.reshape(NT, P, D2).transpose(1, 0, 2).reshape(P, -1)
    return c


ROUTE = "zeroed loaded cast stats moments variance rstd normed normedT normedT_kept kept logits".split()


def layer_norm_steps(nc, s, dve, x_tile, stats, moments, var_eps, rstd, out, tiles=NT):
    for t in range(tiles):
        nc.vector.bn_stats(stats[:, 6 * t:6 * t + 6], x_tile(t)).then_inc(s["stats"], 1)
    for t in range(tiles):
        dve.wait_ge(s["stats"], t + 1)
        nc.vector.bn_aggr(moments[:, 2 * t:2 * t + 2], stats[:, 6 * t:6 * t + 6]).then_inc(s["moments"], 1)
    dve.wait_ge(s["moments"], tiles)
    nc.vector.tensor_scalar(var_eps[:, :], moments[:, 1:2 * tiles:2], 1e-5, None, ALU.add).then_inc(s["variance"], 1)
    dve.wait_ge(s["rstd"], 1)
    for t in range(tiles):
        nc.vector.tensor_scalar(out(t), x_tile(t), moments[:, 2 * t:2 * t + 1], rstd[:, t:t + 1],
                                ALU.subtract, ALU.mult).then_inc(s["normed"], 1)


def load_table(nc, spare, eps, n, function):
    nc.scalar.activation(spare[:, n:n + 1], eps[:, 0:1], function)


def split_steps(nc, dve, s, rest, part, parts, heads, half):
    for n in range(3):
        dve.wait_ge(s["shift_rest"], 3 * half + n + 1)
        if n:
            dve.wait_ge(s["shift_parts"], 3 * half + n)
        nc.vector.tensor_copy(part, rest).then_inc(s["shift_part"], 1)
        dve.wait_ge(s["shift_part"], 3 * half + n + 1)
        nc.vector.tensor_copy(parts.rearrange("p (i r h) -> p i r h", r=3, h=heads)[:, :, n, :],
                              part.rearrange("p (i h) -> p i h", h=heads)).then_inc(s["shift_parts"], 1)
        if n < 2:
            nc.vector.tensor_tensor(rest, rest, part, ALU.subtract).then_inc(s["shift_rest"], 1)


def network(nc, ins, out):
    (x_in, w_q0, w_k0, w_v0, w_o0, w_gate, c_fc, c_proj, w_q1, w_k1, w_v1, w_beta, w_decay, w_mix, mix_bias,
     conv_q, conv_k, conv_v, onorm, w_o1, w_qkv, scales, w_oa, ln_g, ln_b, w_1, b_1, w_2, b_2, const_in) = ins

    with ExitStack() as ctx:
        def sb(name, cols, dt=F32, rows=P):
            return ctx.enter_context(nc.sbuf_tensor(name, [rows, cols], dt))

        pool = [ctx.enter_context(nc.semaphore(f"phase_{i}")) for i in range(120)]
        clearable = range(pool[0].num, pool[-1].num + 1)
        scattered = ctx.enter_context(nc.semaphore("scattered"))
        gathered = ctx.enter_context(nc.semaphore("gathered"))

        def phase(names):
            return dict(zip(names, pool))

        def end_phase():
            nc.all_engine_barrier(sems_to_clear=clearable)

        PS = ctx.enter_context(nc.psum_tensor("PS", [P, 8 * BANK], F32))

        def bank(k, a=0, b=BANK):
            return PS[:, BANK * k + a:BANK * k + b]

        slots_in = nc.dram_tensor("slots_in", (NE * CAP, P), F32, kind="Internal").ap()
        slots_out = nc.dram_tensor("slots_out", (NE * CAP, P), F32, kind="Internal").ap()

        cst = sb("cst", C_COS)
        ident = cst[:, C_ID:C_ID + P]
        ones_row = cst[0:1, C_ONES:C_ONES + P]
        causal16 = sb("causal16", P, BF16)
        causalT16 = sb("causalT16", P, BF16)
        band16 = sb("band16", P + WIN, BF16)
        bandT16 = sb("bandT16", P + WIN, BF16)
        ident16 = sb("ident16", P, BF16)

        wq0 = sb("wq0", P)
        wk0 = sb("wk0", P)
        stack16 = sb("stack16", G0 * 6 * P, BF16)
        shift16 = sb("shift16", G0 // 2 * P, BF16, 3 * G0)
        kz = sb("kz", H0 * T, BF16)
        wv0 = sb("wv0", H0 * DV0)
        wo0 = sb("wo0", H0 * DV0)
        wg = sb("wg", NE)

        x_all = sb("x_all", NTILE * P)
        xnT_all = sb("xnT_all", B * T)
        route_w = sb("route_w", 2 * NTILE)
        slot_from = sb("slot_from", 2 * NTILE, U32)

        stats = sb("stats", 6 * NT)
        moments = sb("moments", 2 * NT)
        var_eps = sb("var_eps", NT)
        rstd = sb("rstd", NT)
        minus_half = sb("minus_half", NT)
        xn_b = sb("xn_b", NT * P)
        xnT_b = sb("xnT_b", T)

        wq1 = sb("wq1", P)
        wk1 = sb("wk1", P)
        wv1 = sb("wv1", P)
        wo1 = sb("wo1", P)
        w_gates = sb("w_gates", 3 * P)
        conv_w = sb("conv_w", 12)
        column = sb("column", 2)
        wqkv = sb("wqkv", DEPTH * 1536)
        w_oa_sb = sb("w_oa_sb", DEPTH * 4 * P)
        w1_sb = sb("w1_sb", DEPTH * 2 * HID)
        w2_sb = sb("w2_sb", DEPTH * 3 * P)
        b1_sb = sb("b1_sb", DEPTH * 6)
        b2_sb = sb("b2_sb", DEPTH * P, F32, 1)
        ln_sb = sb("ln_sb", 2 * DEPTH)
        tables = sb("tables", DEPTH * 4 * NT * D2)
        kz2 = sb("kz2", H2 * T)
        select16 = sb("select16", H2 // 2 * P, BF16, 3 * H2 // 2)
        eps = sb("eps", 2)
        spare = sb("spare", 4)

        before = ctx.enter_context(ExitStack())

        def sb0(name, cols, dt=F32, rows=P):
            return before.enter_context(nc.sbuf_tensor(name, [rows, cols], dt))

        gates_in = sb0("gates_in", 3 * H1)
        scales_in = sb0("scales_in", 4 * DEPTH * D2)
        rotary = sb0("rotary", C_END - C_COS)
        xn_all = sb0("xn_all", NTILE * P)
        logits_all = sb0("logits_all", NTILE * NE)

        s = phase("loaded zeros cleared cast spread".split())
        with nc.Block() as block:
            zeros = xn_all
            LOADS = [(cst[:, :], const_in[:, 0:C_COS]), (rotary[:, :], const_in[:, C_COS:C_END]),
                     (wq0[:, :], w_q0), (wk0[:, :], w_k0), (wv0[:, :], w_v0), (wg[:, :], w_gate),
                     (wq1[:, :], w_q1), (wk1[:, :], w_k1), (wv1[:, :], w_v1), (wo1[:, :], w_o1),
                     (gates_in[:, 0:H1], w_beta), (gates_in[:, H1:2 * H1], w_decay), (gates_in[:, 2 * H1:3 * H1], w_mix),
                     (conv_w[:, 0:4], conv_q), (conv_w[:, 4:8], conv_k), (conv_w[:, 8:12], conv_v),
                     (column[:, 0:1], mix_bias), (column[:, 1:2], onorm),
                     (scales_in[:, :], scales), (b2_sb[:, :], b_2.rearrange("l (o n) -> o (l n)", o=1)),
                     (ln_sb[:, 0:DEPTH], ln_g), (ln_sb[:, DEPTH:2 * DEPTH], ln_b)]
            for l in range(DEPTH):
                LOADS += [(wqkv[:, l * 1536:(l + 1) * 1536], w_qkv[l]), (w1_sb[:, l * 2 * HID:(l + 1) * 2 * HID], w_1[l]),
                          (w_oa_sb[:, l * 512:(l + 1) * 512].rearrange("p (c n) -> p c n", n=P),
                           w_oa[l].rearrange("(c p) n -> p c n", p=P))]
                for c, (start, n) in enumerate(HCH):
                    k = (l * 3 + c) * P
                    LOADS.append((w2_sb[0:n, k:k + P], w_2[l, start:start + n, :]))
                    for half in range(2):
                        k = (l * 2 + half) * 3 + c
                        a = half * HID + start
                        LOADS.append((b1_sb[0:n, k:k + 1], b_1[l, a:a + n].unsqueeze(1)))

            @block.sync
            def _(sp):
                for dst, src in LOADS:
                    sp.dma_start(dst, src).then_inc(s["loaded"], 16)
                sp.dma_start(wo0[:, :].rearrange("p (c n) -> p c n", n=P),
                             w_o0.rearrange("(c p) n -> p c n", p=P)).then_inc(s["loaded"], 16)
                for q in range(4):
                    sp.dma_start(x_all[:, q * 1024:(q + 1) * 1024].rearrange("p (t f) -> p t f", f=P),
                                 x_in.rearrange("b (t p) f -> p (b t) f", p=P)[:, 8 * q:8 * q + 8, :]
                                 ).then_inc(s["loaded"], 16)
                sp.wait_ge(s["zeros"], 1)
                sp.dma_start(slots_in.rearrange("(p r) f -> p (r f)", p=P), zeros[:, :]).then_inc(s["cleared"], 16)
                sp.wait_ge(s["cleared"], 16)
                sp.wait_ge(s["loaded"], 16 * (len(LOADS) + 5))

            @block.gpsimd
            def _(gp):
                nc.gpsimd.memset(minus_half[:, :], -0.5)

            @block.vector
            def _(dve):
                nc.vector.memset(zeros[:, :], 0.0).then_inc(s["zeros"], 1)
                nc.vector.memset(kz[:, :], 0.0)
                nc.vector.memset(kz2[:, :], 0.0)
                dve.wait_ge(s["loaded"], 16 * (len(LOADS) + 5))
                nc.vector.tensor_copy(causal16[:, :], cst[:, C_CAUSAL:C_CAUSAL + P])
                nc.vector.tensor_copy(causalT16[:, :], cst[:, C_CAUSALT:C_CAUSALT + P])
                nc.vector.tensor_copy(band16[:, :], cst[:, C_BAND:C_BAND + P + WIN])
                nc.vector.tensor_copy(bandT16[:, :], cst[:, C_BANDT:C_BANDT + P + WIN])
                nc.vector.tensor_copy(ident16[:, :], ident)
                at = C_STACK - C_COS
                for g in range(G0):
                    nc.vector.tensor_scalar(stack16[:, g * 6 * P:(g + 1) * 6 * P], rotary[:, at:at + 6 * P],
                                            rotary[:, C_STACKG - C_COS + g:C_STACKG - C_COS + g + 1], None, ALU.mult)
                for g in range(G0 // 2):
                    nc.vector.tensor_scalar(shift16[:, g * P:(g + 1) * P],
                                            rotary[0:3 * G0, C_SHIFT - C_COS:C_SHIFT - C_COS + P],
                                            rotary[0:3 * G0, C_SHIFTG - C_COS + g:C_SHIFTG - C_COS + g + 1], None,
                                            ALU.mult)
                nc.vector.tensor_copy(w_gates[:, :].rearrange("p (g d) -> p g d", d=DH1),
                                      gates_in[:, :].unsqueeze(2).to_broadcast([P, 3 * H1, DH1]))
                nc.vector.tensor_copy(select16[:, :].rearrange("p (h d) -> p h d", d=P),
                                      cst[0:3 * H2 // 2, C_SEL:C_SEL + H2 // 2].unsqueeze(2).to_broadcast(
                                          [3 * H2 // 2, H2 // 2, P]))
                for l in range(DEPTH):
                    for n in range(4):
                        nc.vector.tensor_tensor(
                            tables[:, (4 * l + n) * NT * D2:(4 * l + n + 1) * NT * D2].rearrange("p (t d) -> p t d", d=D2),
                            rotary[:, n * NT * D2:(n + 1) * NT * D2].rearrange("p (t d) -> p t d", d=D2),
                            scales_in[:, (4 * l + n) * D2:(4 * l + n + 1) * D2].unsqueeze(1).to_broadcast([P, NT, D2]),
                            ALU.mult)
                nc.vector.memset(eps[:, 0:1], 1e-5)
                nc.vector.memset(eps[:, 1:2], 1e-6)
        end_phase()

        s = phase("stats moments variance rstd normed kept transposed T_copied T_kept logits logits_kept".split())
        stats2 = sb0("stats2", 2 * 6 * NT)
        moments2 = sb0("moments2", 2 * 2 * NT)
        var_eps2 = sb0("var_eps2", 2 * NT)
        rstd2 = sb0("rstd2", 2 * NT)
        minus_half2 = sb0("minus_half2", 2 * NT)
        xn_2 = sb0("xn_2", 2 * T)
        xnT_2 = sb0("xnT_2", 2 * T)
        with nc.Fori(0, B // 2) as b:
            with nc.Block() as block:
                @block.vector
                def _(dve):
                    layer_norm_steps(nc, s, dve, lambda t: x_all[:, bass.ds(b * 2 * T + t * P, P)], stats2, moments2,
                                     var_eps2, rstd2, lambda t: xn_2[:, t * P:(t + 1) * P], 2 * NT)
                    dve.wait_ge(s["transposed"], 2)
                    nc.vector.tensor_copy(xnT_2[:, T:2 * T], bank(1)).then_inc(s["T_copied"], 1)
                    dve.wait_ge(s["logits"], 1)
                    nc.vector.tensor_copy(logits_all[:, bass.ds(b * 2 * NT * NE, 2 * NT * NE)],
                                          bank(2, 0, 2 * NT * NE)).then_inc(s["logits_kept"], 1)

                @block.gpsimd
                def _(gp):
                    nc.gpsimd.memset(minus_half2[:, :], -0.5).then_inc(s["kept"], 1)
                    gp.wait_ge(s["kept"], 1)
                    gp.wait_ge(s["variance"], 1)
                    nc.gpsimd.tensor_tensor(rstd2[:, :], var_eps2[:, :], minus_half2[:, :], ALU.pow
                                            ).then_inc(s["rstd"], 1)
                    gp.wait_ge(s["normed"], 2 * NT)
                    nc.gpsimd.tensor_copy(xn_all[:, bass.ds(b * 2 * T, 2 * T)], xn_2[:, :]).then_inc(s["kept"], 1)

                @block.tensor
                def _(pe):
                    for t in range(2 * NT):
                        pe.wait_ge(s["normed"], t + 1)
                        last = nc.tensor.transpose(bank(t // NT, t % NT * P, (t % NT + 1) * P),
                                                   xn_2[:, t * P:(t + 1) * P], ident)
                        if t % NT == NT - 1:
                            last.then_inc(s["transposed"], 1)
                    pe.wait_ge(s["T_copied"], 2)
                    for t in range(2 * NT):
                        last = nc.tensor.matmul(bank(2, t * NE, (t + 1) * NE), xnT_2[:, t * P:(t + 1) * P], wg[:, :],
                                                start=True, stop=True)
                    last.then_inc(s["logits"], 1)

                @block.scalar
                def _(act):
                    act.wait_ge(s["transposed"], 1)
                    nc.scalar.copy(xnT_2[:, 0:T], bank(0)).then_inc(s["T_copied"], 1)
                    act.wait_ge(s["T_copied"], 2)
                    nc.scalar.copy(xnT_all[:, bass.ds(b * 2 * T, 2 * T)], xnT_2[:, :]).then_inc(s["T_kept"], 1)
            end_phase()

        N8 = NTILE * NE
        top = sb0("top", N8)
        top_i = sb0("top_i", N8, U32)
        choice = sb0("choice", 2 * NTILE)
        oh = sb0("oh", 2 * N8)
        both = sb0("both", N8)
        expo = sb0("expo", N8)
        gap2 = sb0("gap2", NTILE)
        wsum = sb0("wsum", NTILE)
        ranked = sb0("ranked", N8)
        tot = sb0("tot", N8)
        cum = sb0("cum", N8)
        prod = sb0("prod", 2 * N8)
        pos = sb0("pos", 2 * NTILE)
        valid = sb0("valid", 2 * NTILE)
        slot_f = sb0("slot_f", 2 * NTILE)
        past = sb0("past", 2 * NTILE)
        slot_to = sb0("slot_to", 2 * NTILE, U32)

        def te(ap):
            return ap.rearrange("p (t e) -> p t e", e=NE)

        s = phase("top index choice onehot both shifted expo wsum inverse weight counts totals cum rank prod pos "
                  "valid slot".split())
        with nc.Block() as block:
            @block.vector
            def _(dve):
                for n in range(NTILE):
                    nc.vector.max(top[:, n * NE:(n + 1) * NE], logits_all[:, n * NE:(n + 1) * NE]).then_inc(s["top"], 1)
                for n in range(NTILE):
                    dve.wait_ge(s["top"], n + 1)
                    nc.vector.max_index(top_i[:, n * NE:(n + 1) * NE], top[:, n * NE:(n + 1) * NE],
                                        logits_all[:, n * NE:(n + 1) * NE]).then_inc(s["index"], 1)
                dve.wait_ge(s["index"], NTILE)
                for k in range(2):
                    nc.vector.tensor_copy(choice[:, k * NTILE:(k + 1) * NTILE],
                                          te(top_i[:, :])[:, :, k]).then_inc(s["choice"], 1)
                dve.wait_ge(s["choice"], 2)
                for k in range(2):
                    nc.vector.tensor_tensor(
                        te(oh[:, k * N8:(k + 1) * N8]),
                        cst[:, C_IOTA:C_IOTA + NE].unsqueeze(1).to_broadcast([P, NTILE, NE]),
                        choice[:, k * NTILE:(k + 1) * NTILE].unsqueeze(2).to_broadcast([P, NTILE, NE]),
                        ALU.is_equal).then_inc(s["onehot"], 1)
                dve.wait_ge(s["onehot"], 2)
                nc.vector.tensor_tensor(both[:, :], oh[:, 0:N8], oh[:, N8:2 * N8], ALU.add).then_inc(s["both"], 1)
                nc.vector.tensor_tensor(te(expo[:, :]), te(logits_all[:, :]),
                                        te(top[:, :])[:, :, 0].unsqueeze(2).to_broadcast([P, NTILE, NE]),
                                        ALU.subtract).then_inc(s["shifted"], 1)
                nc.vector.tensor_tensor(gap2[:, :], te(top[:, :])[:, :, 1], te(top[:, :])[:, :, 0],
                                        ALU.subtract).then_inc(s["shifted"], 1)
                dve.wait_ge(s["expo"], 2)
                nc.vector.reduce_sum(wsum[:, :], te(expo[:, :]), AX_X).then_inc(s["wsum"], 1)
                dve.wait_ge(s["wsum"], 1)
                nc.vector.reciprocal(wsum[:, :], wsum[:, :]).then_inc(s["inverse"], 1)
                dve.wait_ge(s["totals"], 1)
                nc.vector.tensor_copy(tot[:, :], bank(1, 0, N8)).then_inc(s["counts"], 1)
                dve.wait_ge(s["counts"], 1)
                for e in range(NE):
                    nc.vector.tensor_tensor_scan(te(cum[:, :])[:, :, e], cst[:, C_ONES:C_ONES + NTILE],
                                                 te(tot[:, :])[:, :, e], 0.0, ALU.mult, ALU.add).then_inc(s["cum"], 1)
                dve.wait_ge(s["cum"], NE)
                nc.vector.tensor_tensor(ranked[:, :], cum[:, :], tot[:, :], ALU.subtract).then_inc(s["rank"], 1)
                dve.wait_ge(s["rank"], 1)
                nc.vector.tensor_tensor(ranked[:, :], ranked[:, :], bank(0, 0, N8), ALU.add).then_inc(s["rank"], 1)
                dve.wait_ge(s["rank"], 2)
                for k in range(2):
                    nc.vector.tensor_tensor(prod[:, k * N8:(k + 1) * N8], oh[:, k * N8:(k + 1) * N8], ranked[:, :],
                                            ALU.mult).then_inc(s["prod"], 1)
                dve.wait_ge(s["prod"], 2)
                nc.vector.reduce_sum(pos[:, :], te(prod[:, :]), AX_X).then_inc(s["pos"], 1)
                dve.wait_ge(s["pos"], 1)
                nc.vector.tensor_scalar(valid[:, :], pos[:, :], float(CAP), None, ALU.is_lt).then_inc(s["valid"], 1)
                dve.wait_ge(s["valid"], 1)
                weight = route_w[:, :].rearrange("p (t k) -> p t k", k=2)
                nc.vector.tensor_tensor(weight[:, :, 0], wsum[:, :], valid[:, 0:NTILE], ALU.mult)
                nc.vector.tensor_tensor(gap2[:, :], gap2[:, :], wsum[:, :], ALU.mult).then_inc(s["weight"], 1)
                dve.wait_ge(s["weight"], 1)
                nc.vector.tensor_tensor(weight[:, :, 1], gap2[:, :], valid[:, NTILE:2 * NTILE], ALU.mult)
                nc.vector.scalar_tensor_tensor(slot_f[:, :], choice[:, :], float(CAP), pos[:, :],
                                               ALU.mult, ALU.add).then_inc(s["slot"], 1)
                nc.vector.tensor_scalar(past[:, :], valid[:, :], -65536.0, 65536.0, ALU.mult, ALU.add).then_inc(s["slot"], 1)
                dve.wait_ge(s["slot"], 2)
                nc.vector.tensor_tensor(slot_to[:, :], slot_f[:, :], past[:, :], ALU.add).then_inc(s["slot"], 1)
                nc.vector.tensor_tensor(slot_from[:, :].rearrange("p (t k) -> p t k", k=2),
                                        slot_f[:, :].rearrange("p (k t) -> p t k", k=2),
                                        valid[:, :].rearrange("p (k t) -> p t k", k=2), ALU.mult).then_inc(s["slot"], 1)

            @block.scalar
            def _(act):
                act.wait_ge(s["shifted"], 2)
                nc.scalar.activation(expo[:, :], expo[:, :], ACT.Exp).then_inc(s["expo"], 1)
                nc.scalar.activation(gap2[:, :], gap2[:, :], ACT.Exp).then_inc(s["expo"], 1)

            @block.tensor
            def _(pe):
                pe.wait_ge(s["both"], 1)
                nc.tensor.matmul(bank(0, 0, N8), cst[:, C_USTRICT:C_USTRICT + P], both[:, :], start=True, stop=True)
                nc.tensor.matmul(bank(1, 0, N8), cst[:, C_ONES:C_ONES + P], both[:, :],
                                 start=True, stop=True).then_inc(s["totals"], 1)

            @block.gpsimd
            def _(gp):
                gp.wait_ge(s["slot"], 4)
                for n in range(NTILE):
                    for k in range(2):
                        nc.gpsimd.indirect_dma_start(
                            out=slots_in, out_offset=bass.IndirectOffsetOnAxis(
                                ap=slot_to[:, k * NTILE + n:k * NTILE + n + 1], axis=0),
                            in_=xn_all[:, n * P:(n + 1) * P], in_offset=None,
                            bounds_check=NE * CAP - 1, oob_is_err=False).then_inc(scattered, 16)
                gp.wait_ge(scattered, 16 * 2 * NTILE)
        end_phase()

        wfc = sb0("wfc", 2 * 4 * HC)
        wpr = sb0("wpr", 2 * 2 * P, F32, HC)
        rows = xn_all[:, 3072:4096]
        rowsT = sb0("rowsT", 2 * T)
        silu_a = sb0("silu_a", 2 * 2 * T, F32, HC)
        gated = xn_all[0:HC, 0:2048]
        rows_out = xn_all[:, 2048:3072]
        s = phase("loaded_0 loaded_1 transposed T_copied hidden silu gated projected copied stored".split())
        with nc.Fori(0, NE // 2) as e:
            with nc.Block() as block:
                @block.sync
                def _(sp):
                    for x in range(2):
                        sp.dma_start(rows[:, x * T:(x + 1) * T].rearrange("p (t f) -> p t f", f=P),
                                     slots_in[bass.ds(e * 2 * CAP + x * CAP, CAP), :].rearrange("(t p) f -> p t f", p=P)
                                     ).then_inc(s["loaded_%d" % x], 16)
                        sp.dma_start(wfc[:, x * 4 * HC:(x + 1) * 4 * HC], c_fc[bass.ds(e * 2 * P + x * P, P), :]
                                     ).then_inc(s["loaded_%d" % x], 16)
                        sp.dma_start(wpr[:, x * 2 * P:(x + 1) * 2 * P].rearrange("p (c n) -> p c n", n=P),
                                     c_proj[bass.ds(e * 2 * HALF + x * HALF, HALF), :].rearrange("(c p) n -> p c n", p=HC)
                                     ).then_inc(s["loaded_%d" % x], 16)
                    for x in range(2):
                        sp.wait_ge(s["copied"], x + 1)
                        sp.dma_start(slots_out[bass.ds(e * 2 * CAP + x * CAP, CAP), :].rearrange("(t p) f -> p t f", p=P),
                                     rows_out[:, x * T:(x + 1) * T].rearrange("p (t f) -> p t f", f=P)
                                     ).then_inc(s["stored"], 16)
                    sp.wait_ge(s["stored"], 32)

                @block.tensor
                def _(pe):
                    for x in range(2):
                        pe.wait_ge(s["loaded_%d" % x], 48)
                        for t in range(NT):
                            a = x * T + t * P
                            last = nc.tensor.transpose(bank(6 * x, t * P, (t + 1) * P), rows[:, a:a + P], ident)
                        last.then_inc(s["transposed"], 1)
                    for x in range(2):
                        pe.wait_ge(s["T_copied"], x + 1)
                        for n, c in enumerate((0, 2, 1, 3)):
                            if x:
                                pe.wait_ge(s["gated"], 1 + n // 2)
                            nc.tensor.matmul(PS[0:HC, BANK * (1 + c):BANK * (2 + c)],
                                             wfc[:, (4 * x + c) * HC:(4 * x + c + 1) * HC],
                                             rowsT[:, x * T:(x + 1) * T], start=True, stop=True).then_inc(s["hidden"], 1)
                    for x in range(2):
                        pe.wait_ge(s["gated"], 2 * x + 2)
                        for t in range(NT):
                            for c in range(2):
                                a = (2 * x + c) * T + t * P
                                last = nc.tensor.matmul(bank(5 + 2 * x, t * P, (t + 1) * P), gated[:, a:a + P],
                                                        wpr[:, (2 * x + c) * P:(2 * x + c + 1) * P],
                                                        start=(c == 0), stop=(c == 1))
                        last.then_inc(s["projected"], 1)

                @block.scalar
                def _(act):
                    for n in range(4):
                        c = n % 2
                        act.wait_ge(s["hidden"], 1 + 2 * n)
                        nc.scalar.activation(silu_a[:, n * T:(n + 1) * T], PS[0:HC, BANK * (1 + c):BANK * (2 + c)],
                                             ACT.Silu).then_inc(s["silu"], 1)

                @block.vector
                def _(dve):
                    for x in range(2):
                        dve.wait_ge(s["transposed"], x + 1)
                        nc.vector.tensor_copy(rowsT[:, x * T:(x + 1) * T], bank(6 * x)).then_inc(s["T_copied"], 1)
                    for n in range(4):
                        c = n % 2
                        dve.wait_ge(s["silu"], n + 1)
                        dve.wait_ge(s["hidden"], 2 + 2 * n)
                        nc.vector.tensor_tensor(gated[:, n * T:(n + 1) * T], silu_a[:, n * T:(n + 1) * T],
                                                PS[0:HC, BANK * (3 + c):BANK * (4 + c)], ALU.mult
                                                ).then_inc(s["gated"], 1)
                    for x in range(2):
                        dve.wait_ge(s["projected"], x + 1)
                        nc.vector.tensor_copy(rows_out[:, x * T:(x + 1) * T], bank(5 + 2 * x)).then_inc(s["copied"], 1)
            end_phase()

        before.close()
        x1 = sb("x1", NT * P)

        def sb1(name, cols, dt=F32, rows=P):
            return layer0.enter_context(nc.sbuf_tensor(name, [rows, cols], dt))

        layer0 = ctx.enter_context(ExitStack())
        HH0 = H0 // 2
        q_parts = sb1("q_parts", 3 * T, BF16)
        k_parts = sb1("k_parts", 3 * T, BF16)
        rest = sb1("rest", 2 * T)
        qS = sb1("qS", G0 * T, BF16)
        v0 = sb1("v0", NT * H0 * DV0)
        row_max = sb1("row_max", H0 * NT)
        bias0 = sb1("bias0", H0 * NT)
        sums0 = sb1("sums0", H0 * NT)
        log_sums = sb1("log_sums", H0 * NT)
        shift_rest = sb1("shift_rest", NT * H0)
        shift_part = sb1("shift_part", NT * H0, BF16)
        shift_parts = sb1("shift_parts", NT * 3 * H0)
        shiftT16 = sb1("shiftT16", 2 * T, BF16, 3 * HH0)
        probsT = sb1("probsT", 2 * 1280)
        ctx0T = sb1("ctx0T", G0 * T)
        from_b = sb1("from_b", 2 * NT, U32)
        weight_b = sb1("weight_b", 2 * NT)
        picked = ctx0T[:, 0:2 * NT * P]
        moe = rest[:, 0:NT * P]
        REGION = {0: 0, 1: 512, 3: 896, 2: 1024}
        QREGION = {3: 0, 2: 512, 0: 896, 1: 1024}

        scale0 = 1.0 / float(np.sqrt(DK0))
        with nc.Fori(0, B) as b:
            s = phase("xT_b from_b weight_b qk part rest v v_act v_dve stack k_low k_high q_stack scores max bias sum "
                      "log shift_rest shift_part shift_parts shiftT shiftT_copied shift_mm shifted scoresT probs "
                      "context ctxT attn moe_half moe silu gated x1".split())
            with nc.Block() as block:
                @block.gpsimd
                def _(gp):
                    nc.gpsimd.tensor_copy(from_b[:, :], slot_from[:, bass.ds(b * 2 * NT, 2 * NT)]).then_inc(s["from_b"], 1)
                    gp.wait_ge(s["from_b"], 1)
                    for n in range(2 * NT):
                        nc.gpsimd.indirect_dma_start(
                            out=picked[:, n * P:(n + 1) * P], out_offset=None, in_=slots_out,
                            in_offset=bass.IndirectOffsetOnAxis(ap=from_b[:, n:n + 1], axis=0),
                            bounds_check=NE * CAP - 1, oob_is_err=False).then_inc(gathered, 16)

                @block.tensor
                def _(pe):
                    pe.wait_ge(s["xT_b"], 1)
                    nc.tensor.matmul(bank(0), wq0[:, :], xnT_b[:, :], start=True, stop=True).then_inc(s["qk"], 1)
                    nc.tensor.matmul(bank(1), wk0[:, :], xnT_b[:, :], start=True, stop=True).then_inc(s["qk"], 1)
                    for n in range(2 * NT):
                        t, half = divmod(n, 2)
                        if n == 6:
                            pe.wait_ge(s["v_act"], 1)
                        if n == 7:
                            pe.wait_ge(s["v_dve"], 1)
                        nc.tensor.matmul(bank(2 + n % 6), xnT_b[:, t * P:(t + 1) * P],
                                         wv0[:, half * 512:(half + 1) * 512], start=True, stop=True
                                         ).then_inc(s["v"], 1)

                    def stack(g):
                        if g:
                            pe.wait_ge(s["k_low"], g)
                            pe.wait_ge(s["q_stack"], g)
                        for n, parts in ((1, k_parts), (0, q_parts)):
                            for k in range(3):
                                a = (g * 6 + 3 * n + k) * P
                                last = nc.tensor.matmul(bank(7 - n), stack16[:, a:a + P], parts[:, k * T:(k + 1) * T],
                                                        start=(k == 0), stop=(k == 2))
                            last.then_inc(s["stack"], 1)

                    def scores(h):
                        g = h // 2
                        if h >= 2:
                            pe.wait_ge(s["sum"], 4 * (h - 1))
                        base = 1536 * (h % 2)
                        for i in (3, 2, 0, 1):
                            a = base + QREGION[i]
                            nc.tensor.matmul(PS[:, a:a + (i + 1) * P], qS[:, g * T + i * P:g * T + (i + 1) * P],
                                             kz[:, h * T:h * T + (i + 1) * P], start=True, stop=False)
                            nc.tensor.matmul(PS[:, a + i * P:a + (i + 1) * P], ident16[:, :], causal16[:, :],
                                             start=False, stop=True).then_inc(s["scores"], 1)

                    pe.wait_ge(s["part"], 6)
                    pe.wait_ge(s["v_act"], NT)
                    pe.wait_ge(s["v_dve"], NT)
                    def shifts_T(half):
                        pe.wait_ge(s["shift_parts"], 3 * half + 3)
                        for i in range(NT):
                            a = (half * NT + i) * 3 * HH0
                            o = (6 + half) * BANK + i * P
                            last = nc.tensor.transpose(PS[0:3 * HH0, o:o + P], shift_parts[:, a:a + 3 * HH0], ident)
                        last.then_inc(s["shiftT"], 1)

                    def shift_rows(g, k):
                        pe.wait_ge(s["shiftT_copied"], 1 + g // 4)
                        nc.tensor.matmul(bank(k), shift16[:, g % 4 * P:(g % 4 + 1) * P],
                                         shiftT16[:, g // 4 * T:(g // 4 + 1) * T], start=True, stop=True
                                         ).then_inc(s["shift_mm"], 1)

                    stack(0)
                    for g in range(G0):
                        if g < G0 - 1:
                            stack(g + 1)
                        pe.wait_ge(s["k_low"], g + 1)
                        pe.wait_ge(s["q_stack"], g + 1)
                        if g == G0 - 1:
                            shifts_T(0)
                        scores(2 * g)
                        scores(2 * g + 1)
                    shift_rows(0, 7)
                    shift_rows(1, 6)

                    def scores_T(h):
                        g = h // 2
                        base = 1536 * (h % 2)
                        if h < 2:
                            pe.wait_ge(s["sum"], 4 * (H0 + h - 1))
                        else:
                            pe.wait_ge(s["probs"], h - 1)
                        if h % 2 == 0:
                            pe.wait_ge(s["shifted"], g + 1)
                        for j in (0, 1, 3, 2):
                            a = base + REGION[j]
                            n = T - j * P
                            nc.tensor.matmul(PS[:, a:a + n], kz[:, h * T + j * P:h * T + (j + 1) * P],
                                             qS[:, g * T + j * P:(g + 1) * T], start=True, stop=False)
                            last = nc.tensor.matmul(PS[:, a:a + P], ident16[:, :], causalT16[:, :],
                                                    start=False, stop=True)
                        last.then_inc(s["scoresT"], 1)

                    def context(h):
                        g, r = h // 2, 64 * (h % 2)
                        pe.wait_ge(s["probs"], h + 1)
                        if h % 2 == 0:
                            if g == 1:
                                pe.wait_ge(s["shiftT_copied"], 2)
                            else:
                                pe.wait_ge(s["shifted"], min(4 + g - (g > 0), G0))
                            if g >= 2:
                                pe.wait_ge(s["ctxT"], g - 1)
                        for j in range(NT):
                            a = 1280 * (h % 2) + REGION[j]
                            n = T - j * P
                            last = nc.tensor.matmul(PS[r:r + DV0, (6 + g % 2) * BANK + j * P:(7 + g % 2) * BANK],
                                                    v0[:, (j * H0 + h) * DV0:(j * H0 + h + 1) * DV0],
                                                    probsT[:, a:a + n], start=(j == 0), stop=(j == NT - 1),
                                                    tile_position=(0, r))
                        last.then_inc(s["context"], 1)

                    for h in range(H0 + 1):
                        if h == 1:
                            pe.wait_ge(s["shifted"], 1)
                            shift_rows(2, 7)
                        if h == 2:
                            pe.wait_ge(s["shifted"], 3)
                            shifts_T(1)
                        if h in (4, 6, 8, 10):
                            pe.wait_ge(s["ctxT"], h // 2 - 1)
                            shift_rows(2 + h // 2, 6 + h // 2 % 2)
                        if h < H0:
                            scores_T(h)
                        if h == 1:
                            pe.wait_ge(s["shifted"], 2)
                            shift_rows(3, 6)
                        if h >= 1:
                            context(h - 1)
                    pe.wait_ge(s["ctxT"], G0)
                    for t in range(NT):
                        for c in range(G0):
                            last = nc.tensor.matmul(bank(0, t * P, (t + 1) * P), ctx0T[:, c * T + t * P:c * T + (t + 1) * P],
                                                    wo0[:, c * P:(c + 1) * P], start=(c == 0), stop=(c == G0 - 1))
                    last.then_inc(s["attn"], 1)

                def v_copy(t, half):
                    return v0[:, (2 * t + half) * T:(2 * t + half + 1) * T], bank(2 + (2 * t + half) % 6)

                @block.scalar
                def _(act):
                    nc.scalar.copy(xnT_b[:, :], xnT_all[:, bass.ds(b * T, T)]).then_inc(s["xT_b"], 1)
                    for k in range(3):
                        for n, parts in enumerate((q_parts, k_parts)):
                            if k == 0:
                                act.wait_ge(s["qk"], n + 1)
                                src = bank(n)
                            else:
                                act.wait_ge(s["rest"], 2 * (k - 1) + n + 1)
                                src = rest[:, n * T:(n + 1) * T]
                            nc.scalar.copy(parts[:, k * T:(k + 1) * T], src).then_inc(s["part"], 1)
                        act.wait_ge(s["v"], 2 * k + 1)
                        nc.scalar.copy(*v_copy(k, 0)).then_inc(s["v_act"], 1)
                    act.wait_ge(s["v"], 7)
                    nc.scalar.copy(*v_copy(3, 0)).then_inc(s["v_act"], 1)

                    def stacks(g):
                        act.wait_ge(s["stack"], 2 * g + 1)
                        nc.scalar.activation(kz[0:64, 2 * g * T:(2 * g + 1) * T], bank(6)[0:64, :], ACT.Identity,
                                             bias=cst[0:64, C_KONE:C_KONE + 1]).then_inc(s["k_low"], 1)

                    def shift_logs(half):
                        at = slice(half * NT * HH0, (half + 1) * NT * HH0)
                        act.wait_ge(s["sum"], (half + 1) * NT * HH0)
                        nc.scalar.activation(log_sums[:, at], sums0[:, at], ACT.Ln).then_inc(s["log"], 1)

                    def shifts_copied(half):
                        act.wait_ge(s["shiftT"], half + 1)
                        nc.scalar.copy(shiftT16[:, half * T:(half + 1) * T],
                                       bank(6 + half)[0:3 * HH0, :]).then_inc(s["shiftT_copied"], 1)

                    load_table(nc, spare, eps, 0, ACT.Exp)
                    stacks(0)
                    for h in range(H0):
                        if h % 2 == 0 and h < H0 - 2:
                            stacks(h // 2 + 1)
                        if h == H0 - 2:
                            shifts_copied(0)
                        act.wait_ge(s["bias"], h + 1)
                        base = 1536 * (h % 2)
                        for n, i in enumerate((3, 2, 0, 1)):
                            if 4 * h + n >= 2:
                                act.wait_ge(s["sum"], 4 * h + n - 1)
                            a = base + QREGION[i]
                            nc.scalar.activation(rest[:, n % 2 * T:n % 2 * T + (i + 1) * P], PS[:, a:a + (i + 1) * P], ACT.Exp,
                                                 bias=bias0[:, h * NT + i:h * NT + i + 1], scale=scale0,
                                                 accum_out=sums0[:, h * NT + i:h * NT + i + 1]).then_inc(s["sum"], 1)
                        if h == HH0 - 1:
                            shift_logs(0)
                    shift_logs(1)
                    for h in range(H0):
                        act.wait_ge(s["scoresT"], h + 1)
                        if h >= 2:
                            act.wait_ge(s["context"], h - 1)
                        base = 1536 * (h % 2)
                        nc.scalar.activation(probsT[:, 1280 * (h % 2):1280 * (h % 2 + 1)], PS[:, base:base + 1280],
                                             ACT.Exp, scale=scale0).then_inc(s["probs"], 1)
                        if h == 1:
                            shifts_copied(1)
                    act.wait_ge(s["moe"], NT)
                    nc.scalar.activation(moe[:, :], moe[:, :], ACT.Silu).then_inc(s["silu"], 1)

                @block.vector
                def _(dve):
                    nc.vector.tensor_copy(weight_b[:, :], route_w[:, bass.ds(b * 2 * NT, 2 * NT)]).then_inc(s["weight_b"], 1)
                    for k in range(2):
                        for n, parts in enumerate((q_parts, k_parts)):
                            dve.wait_ge(s["part"], 2 * k + n + 1)
                            src = bank(n) if k == 0 else rest[:, n * T:(n + 1) * T]
                            nc.vector.tensor_tensor(rest[:, n * T:(n + 1) * T], src, parts[:, k * T:(k + 1) * T],
                                                    ALU.subtract).then_inc(s["rest"], 1)
                        dve.wait_ge(s["v"], 2 * k + 2)
                        nc.vector.tensor_copy(*v_copy(k, 1)).then_inc(s["v_dve"], 1)
                    for k in (2, 3):
                        dve.wait_ge(s["v"], 2 * k + 2)
                        nc.vector.tensor_copy(*v_copy(k, 1)).then_inc(s["v_dve"], 1)

                    def shifts(half):
                        at = slice(half * NT * HH0, (half + 1) * NT * HH0)
                        dve.wait_ge(s["log"], half + 1)
                        nc.vector.scalar_tensor_tensor(shift_rest[:, at].rearrange("p (i h) -> p h i", h=HH0),
                                                       log_sums[:, at].rearrange("p (h i) -> p h i", i=NT), -1.0 / scale0,
                                                       row_max[:, at].rearrange("p (h i) -> p h i", i=NT),
                                                       ALU.mult, ALU.subtract).then_inc(s["shift_rest"], 1)
                        split_steps(nc, dve, s, shift_rest[:, at], shift_part[:, at],
                                    shift_parts[:, half * NT * 3 * HH0:(half + 1) * NT * 3 * HH0], HH0, half)

                    def add_shift(g):
                        dve.wait_ge(s["shift_mm"], g + 1)
                        nc.vector.tensor_tensor(qS[:, g * T:(g + 1) * T], qS[:, g * T:(g + 1) * T],
                                                bank((7, 6, 7, 6, 6, 7, 6, 7)[g]), ALU.add).then_inc(s["shifted"], 1)

                    def stacks(g):
                        dve.wait_ge(s["stack"], 2 * g + 1)
                        nc.vector.tensor_scalar(kz[64:P, (2 * g + 1) * T:(2 * g + 2) * T], bank(6)[64:P, :],
                                                cst[64:P, C_KONE:C_KONE + 1], None, ALU.add).then_inc(s["k_high"], 1)
                        dve.wait_ge(s["stack"], 2 * g + 2)
                        nc.vector.tensor_copy(qS[:, g * T:(g + 1) * T], bank(7)).then_inc(s["q_stack"], 1)

                    stacks(0)
                    for h in range(H0):
                        if h % 2 == 0 and h < H0 - 2:
                            stacks(h // 2 + 1)
                        base = 1536 * (h % 2)
                        for n, i in enumerate((3, 2, 0, 1)):
                            dve.wait_ge(s["scores"], 4 * h + (1, 3, 3, 4)[n])
                            a = base + QREGION[i]
                            nc.vector.reduce_max(row_max[:, h * NT + i:h * NT + i + 1], PS[:, a:a + (i + 1) * P],
                                                 AX_X).then_inc(s["max"], 1)
                        dve.wait_ge(s["max"], 4 * h + 4)
                        nc.vector.tensor_scalar(bias0[:, h * NT:(h + 1) * NT], row_max[:, h * NT:(h + 1) * NT], -scale0,
                                                None, ALU.mult).then_inc(s["bias"], 1)
                        if h == HH0 + 1:
                            shifts(0)
                    for g in range(4):
                        add_shift(g)
                    shifts(1)
                    dve.wait_ge(s["weight_b"], 1)
                    dve.wait_ge(gathered, b * (16 * 2 * NT) + 16 * 2 * NT)
                    for t in range(NT):
                        nc.vector.tensor_scalar(moe[:, t * P:(t + 1) * P], picked[:, 2 * t * P:(2 * t + 1) * P],
                                                weight_b[:, 2 * t:2 * t + 1], None, ALU.mult).then_inc(s["moe_half"], 1)
                    for t in range(NT):
                        dve.wait_ge(s["moe_half"], t + 1)
                        nc.vector.scalar_tensor_tensor(moe[:, t * P:(t + 1) * P], picked[:, (2 * t + 1) * P:(2 * t + 2) * P],
                                                       weight_b[:, 2 * t + 1:2 * t + 2], moe[:, t * P:(t + 1) * P],
                                                       ALU.mult, ALU.add).then_inc(s["moe"], 1)
                    dve.wait_ge(s["moe"], NT)
                    for g in range(G0):
                        dve.wait_ge(s["context"], 2 * g + 2)
                        nc.vector.tensor_copy(ctx0T[:, g * T:(g + 1) * T], bank(6 + g % 2)).then_inc(s["ctxT"], 1)
                        if g < 4:
                            add_shift(4 + g)
                    dve.wait_ge(s["silu"], 1)
                    dve.wait_ge(s["attn"], 1)
                    nc.vector.tensor_tensor(x1[:, :], bank(0), moe[:, :], ALU.mult).then_inc(s["gated"], 1)
                    dve.wait_ge(s["gated"], 1)
                    nc.vector.tensor_tensor(x1[:, :], x1[:, :], x_all[:, bass.ds(b * T, T)], ALU.add).then_inc(s["x1"], 1)
            end_phase()
            layer0.close()

            layer1 = ctx.enter_context(ExitStack())

            def sb2(name, cols, dt=F32, rows=P):
                return layer1.enter_context(nc.sbuf_tensor(name, [rows, cols], dt))

            s1 = sb2("s1", T)
            out1 = sb2("out1", T)

            delta = ctx.enter_context(ExitStack())

            def sb3(name, cols, dt=F32, rows=P):
                return delta.enter_context(nc.sbuf_tensor(name, [rows, cols], dt))

            padded = sb3("padded", 3 * (T + 4))
            conv = sb3("conv", 3 * T)
            beta = sb3("beta", T)
            decay = sb3("decay", T)
            keep_in = sb3("keep_in", T)
            mix = sb3("mix", T)
            squares = sb3("squares", 2 * T)
            norm = sb3("norm", 2 * T)
            qk_n = sb3("qk_n", 2 * T)
            scaled = sb3("scaled", 2 * T)
            ema_in = sb3("ema_in", T)
            ema = sb3("ema", T)
            rows3 = sb3("rows3", 3 * T)
            low = sb3("low", 3 * T)
            inv_t = sb3("inv_t", 2 * T)
            level = squares[:, T:2 * T]
            product = norm[:, T:2 * T]
            uw = sb3("uw", 2 * T)
            u_new = sb3("u_new", P)
            state = sb3("state", 2 * P)
            diff = scaled[:, 0:T]
            NCH = T // CH

            def mask(n):
                a = C_DELTA + n * CH
                return cst[:, a:a + CH].unsqueeze(1).to_broadcast([P, NCH, CH])

            def g32(ap):
                return ap.rearrange("p (n j) -> p n j", j=CH)

            def chunks():
                for n in range(NCH):
                    t, c = divmod(n, 4)
                    for h in range(H1):
                        yield slice(32 * c, 32 * c + 32), (t * H1 + h) * CH, slice(32 * h, 32 * h + 32), n * CH, \
                            t * P + h * DH1

            s = phase("stats moments variance rstd normed transposed T_copied pads qkv pad_copied conv silu gates sigmoid squares sumsq root inverse qk_n scaled ema_in ema "
                      "rowsT rows_act kk low flipped inv level product product_copied updated added uw_mm uw_act uw_dve "
                      "w_state u_new s_updated s_copied out_mm diff mixed".split())
            with nc.Block() as block:
                @block.tensor
                def _(pe):
                    for t in range(NT):
                        pe.wait_ge(s["normed"], t + 1)
                        nc.tensor.transpose(bank(7, t * P, (t + 1) * P), xn_b[:, t * P:(t + 1) * P],
                                            ident).then_inc(s["transposed"], 1)
                    pe.wait_ge(s["T_copied"], 1)
                    for n, w in enumerate((wq1, wk1, wv1)):
                        nc.tensor.matmul(bank(n), w[:, :], xnT_b[:, :], start=True, stop=True).then_inc(s["qkv"], 1)
                    for n in range(3):
                        pe.wait_ge(s["pad_copied"], n + 1)
                        nc.tensor.matmul(bank(n), w_gates[:, n * P:(n + 1) * P], xnT_b[:, :], start=True,
                                         stop=True).then_inc(s["gates"], 1)
                    for m, n in enumerate((1, 0)):
                        pe.wait_ge(s["squares"], m + 1)
                        pe.wait_ge(s["sigmoid"], 4)
                        nc.tensor.matmul(bank(n), cst[:, C_BLK32:C_BLK32 + P], squares[:, n * T:(n + 1) * T],
                                         start=True, stop=True).then_inc(s["sumsq"], 1)
                    pe.wait_ge(s["root"], 2)
                    for n in range(3):
                        src = (qk_n[:, T:2 * T], scaled[:, 0:T], scaled[:, T:2 * T])[n]
                        if n == 0:
                            pe.wait_ge(s["qk_n"], 1)
                        else:
                            pe.wait_ge(s["scaled"], n)
                        for t in range(NT):
                            nc.tensor.transpose(bank(2 + n, t * P, (t + 1) * P), src[:, t * P:(t + 1) * P],
                                                ident).then_inc(s["rowsT"], 1)
                    pe.wait_ge(s["rows_act"], 3)
                    pairs = ((scaled, 0, qk_n, T), (qk_n, T, qk_n, 0))
                    for n, (a, ao, b_, bo) in enumerate(pairs):
                        if n:
                            pe.wait_ge(s["qk_n"], 2)
                        for rc, blk, rh, tok, _ in chunks():
                            o = BANK * (4 * n + rh.start // 32) + tok // P * CH
                            last = nc.tensor.matmul(PS[rc, o:o + CH],
                                                    a[rh, ao + tok:ao + tok + CH], b_[rh, bo + tok:bo + tok + CH],
                                                    start=True, stop=True, tile_position=(rh.start, rc.start))
                        last.then_inc(s["kk"], 1)
                    for l in range(4):
                        pe.wait_ge(s["level"], l + 1)
                        pe.wait_ge(s["added"], l + 1)
                        for rc, blk, _, _, _ in chunks():
                            last = nc.tensor.matmul(PS[rc, blk:blk + CH], level[rc, blk:blk + CH],
                                                    inv_t[rc, blk:blk + CH], start=True, stop=True,
                                                    tile_position=(rc.start, rc.start))
                        last.then_inc(s["product"], 1)
                        pe.wait_ge(s["product_copied"], l + 1)
                        pe.wait_ge(s["flipped"], l + 2)
                        for rc, blk, _, _, _ in chunks():
                            last = nc.tensor.matmul(PS[rc, BANK + blk:BANK + blk + CH],
                                                    inv_t[rc, T + blk:T + blk + CH], product[rc, blk:blk + CH],
                                                    start=True, stop=True, tile_position=(rc.start, rc.start))
                        last.then_inc(s["updated"], 1)
                    pe.wait_ge(s["flipped"], 6)
                    pe.wait_ge(s["low"], 8)
                    for rc, blk, _, _, feat in chunks():
                        last = nc.tensor.matmul(PS[rc, blk:blk + CH], inv_t[rc, T + blk:T + blk + CH],
                                                rows3[rc, 2 * T + feat:2 * T + feat + CH], start=True, stop=True,
                                                tile_position=(rc.start, rc.start))
                    last.then_inc(s["uw_mm"], 1)
                    for rc, blk, rh, tok, feat in chunks():
                        o = BANK * (1 + rc.start // 32) + tok // P * CH
                        last = nc.tensor.matmul(PS[rh, o:o + CH], rows3[rc, T + feat:T + feat + CH],
                                                inv_t[rc, T + blk:T + blk + CH], start=True, stop=True,
                                                tile_position=(rc.start, rh.start))
                    last.then_inc(s["uw_mm"], 1)
                    pe.wait_ge(s["uw_act"], 1)
                    pe.wait_ge(s["uw_dve"], 4)
                    todo = list(chunks())
                    for n in range(NCH):
                        mine = todo[n * H1:(n + 1) * H1]
                        rc, tok = mine[0][0], mine[0][3]
                        st = state[:, (n % 2) * P:(n % 2 + 1) * P]
                        if n:
                            pe.wait_ge(s["s_copied"], n)
                            nc.tensor.matmul(PS[rc, 0:P], uw[:, T + tok:T + tok + CH], st, start=True, stop=True,
                                             tile_position=(0, rc.start)).then_inc(s["w_state"], 1)
                        pe.wait_ge(s["u_new"], n + 1)
                        t = n // 4
                        nc.tensor.matmul(bank(1, 0, P), rows3[rc, t * P:(t + 1) * P], u_new[rc, :], start=(n == 0),
                                         stop=True, tile_position=(rc.start, 0),
                                         skip_group_check=True).then_inc(s["s_updated"], 1)
                        if n:
                            nc.tensor.matmul(bank(2, tok, tok + CH), st, qk_n[:, tok:tok + CH], start=True, stop=True)
                        for h, (rc, blk, rh, tok, feat) in enumerate(mine):
                            last = nc.tensor.matmul(PS[rh, 3 * BANK + tok:3 * BANK + tok + CH],
                                                    u_new[rc, h * DH1:(h + 1) * DH1],
                                                    low[rc, 2 * T + blk:2 * T + blk + CH], start=True, stop=True,
                                                    tile_position=(rc.start, rh.start))
                        last.then_inc(s["out_mm"], 1)

                @block.scalar
                def _(act):
                    act.wait_ge(s["transposed"], NT)
                    nc.scalar.copy(xnT_b[:, :], bank(7)).then_inc(s["T_copied"], 1)
                    act.wait_ge(s["pads"], 1)
                    for n in range(3):
                        act.wait_ge(s["qkv"], n + 1)
                        a = n * (T + 4) + 3
                        nc.scalar.copy(padded[:, a:a + T], bank(n)).then_inc(s["pad_copied"], 1)
                    act.wait_ge(s["gates"], 3)
                    nc.scalar.activation(beta[:, :], bank(0), ACT.Sigmoid).then_inc(s["sigmoid"], 1)
                    nc.scalar.activation(decay[:, :], bank(1), ACT.Sigmoid).then_inc(s["sigmoid"], 1)
                    nc.scalar.activation(keep_in[:, :], bank(1), ACT.Sigmoid, scale=-1.0).then_inc(s["sigmoid"], 1)
                    nc.scalar.activation(mix[:, :], bank(2), ACT.Sigmoid, bias=column[:, 0:1]).then_inc(s["sigmoid"], 1)
                    for n in range(3):
                        act.wait_ge(s["conv"], 4 * (n + 1))
                        nc.scalar.activation(conv[:, n * T:(n + 1) * T], conv[:, n * T:(n + 1) * T],
                                             ACT.Silu).then_inc(s["silu"], 1)
                    act.wait_ge(s["silu"], 3)
                    for n in (1, 0):
                        nc.scalar.square(squares[:, n * T:(n + 1) * T], conv[:, n * T:(n + 1) * T]
                                         ).then_inc(s["squares"], 1)
                    for m, n in enumerate((1, 0)):
                        act.wait_ge(s["sumsq"], m + 1)
                        nc.scalar.activation(norm[:, n * T:(n + 1) * T], bank(n), ACT.Sqrt,
                                             bias=eps[:, 1:2]).then_inc(s["root"], 1)
                    for n in range(3):
                        act.wait_ge(s["rowsT"], NT * (n + 1))
                        nc.scalar.copy(rows3[:, n * T:(n + 1) * T], bank(2 + n)).then_inc(s["rows_act"], 1)
                    for l in range(4):
                        act.wait_ge(s["product"], l + 1)
                        nc.scalar.copy(product[:, :], bank(0)).then_inc(s["product_copied"], 1)
                    act.wait_ge(s["uw_mm"], 1)
                    nc.scalar.copy(uw[:, 0:T], bank(0)).then_inc(s["uw_act"], 1)

                @block.gpsimd
                def _(gp):
                    gp.wait_ge(s["variance"], 1)
                    nc.gpsimd.tensor_tensor(rstd[:, :], var_eps[:, :], minus_half[:, :], ALU.pow).then_inc(s["rstd"], 1)
                    gp.wait_ge(s["silu"], 3)
                    gp.wait_ge(s["sigmoid"], 4)
                    nc.gpsimd.tensor_tensor(ema_in[:, :], conv[:, 2 * T:3 * T], keep_in[:, :], ALU.mult
                                            ).then_inc(s["ema_in"], 1)

                @block.vector
                def _(dve):
                    layer_norm_steps(nc, s, dve, lambda t: x1[:, t * P:(t + 1) * P], stats, moments,
                                     var_eps, rstd, lambda t: xn_b[:, t * P:(t + 1) * P])
                    nc.vector.memset(padded[:, :].rearrange("p (n c) -> p n c", n=3)[:, :, 0:3], 0.0
                                     ).then_inc(s["pads"], 1)
                    for n in range(3):
                        a = n * (T + 4)
                        to = conv[:, n * T:(n + 1) * T]
                        dve.wait_ge(s["pad_copied"], n + 1)
                        nc.vector.tensor_scalar(to, padded[:, a:a + T], conv_w[:, 4 * n:4 * n + 1], None,
                                                ALU.mult).then_inc(s["conv"], 1)
                        for j in range(1, 4):
                            dve.wait_ge(s["conv"], 4 * n + j)
                            nc.vector.scalar_tensor_tensor(to, padded[:, a + j:a + j + T],
                                                           conv_w[:, 4 * n + j:4 * n + j + 1], to,
                                                           ALU.mult, ALU.add).then_inc(s["conv"], 1)
                    for m, n in enumerate((1, 0)):
                        dve.wait_ge(s["root"], m + 1)
                        nc.vector.reciprocal(norm[:, n * T:(n + 1) * T], norm[:, n * T:(n + 1) * T]
                                             ).then_inc(s["inverse"], 1)
                        dve.wait_ge(s["inverse"], m + 1)
                        nc.vector.tensor_tensor(qk_n[:, n * T:(n + 1) * T], conv[:, n * T:(n + 1) * T],
                                                norm[:, n * T:(n + 1) * T], ALU.mult).then_inc(s["qk_n"], 1)
                        if n:
                            dve.wait_ge(s["qk_n"], 1)
                            nc.vector.tensor_tensor(scaled[:, 0:T], qk_n[:, T:2 * T], beta[:, :], ALU.mult
                                                    ).then_inc(s["scaled"], 1)
                            nc.vector.tensor_tensor(scaled[:, T:2 * T], conv[:, 2 * T:3 * T], beta[:, :], ALU.mult
                                                    ).then_inc(s["scaled"], 1)
                    dve.wait_ge(s["ema_in"], 1)
                    nc.vector.tensor_tensor_scan(ema[:, :], decay[:, :], ema_in[:, :], 0.0, ALU.mult, ALU.add
                                                 ).then_inc(s["ema"], 1)
                    def mask_products(n):
                        dve.wait_ge(s["kk"], n + 1)
                        m = C_DELTA + (D_NEGLO, D_INCLT)[n] * CH
                        for h in range(H1):
                            nc.vector.tensor_tensor(
                                low[:, 2 * n * T:(2 * n + 1) * T].rearrange("p (t h j) -> p t h j", h=H1, j=CH)[:, :, h, :],
                                g32(bank(4 * n + h, 0, P)),
                                cst[:, m:m + CH].unsqueeze(1).to_broadcast([P, NT, CH]), ALU.mult
                            ).then_inc(s["low"], 1)

                    mask_products(0)
                    dve.wait_ge(s["low"], 4)
                    nc.vector.transpose(low[:, T:2 * T], low[:, 0:T]).then_inc(s["flipped"], 1)
                    nc.vector.tensor_tensor(g32(inv_t[:, 0:T]), g32(low[:, 0:T]), mask(D_M1), ALU.mult
                                            ).then_inc(s["inv"], 1)
                    dve.wait_ge(s["inv"], 1)
                    nc.vector.tensor_tensor(g32(inv_t[:, 0:T]), g32(inv_t[:, 0:T]), mask(D_EYE), ALU.add
                                            ).then_inc(s["added"], 1)
                    for l in range(4):
                        if l:
                            dve.wait_ge(s["product"], l)
                        else:
                            dve.wait_ge(s["flipped"], 1)
                        nc.vector.tensor_tensor(g32(level[:, :]), g32(low[:, T:2 * T]), mask(D_M2T + l), ALU.mult
                                                ).then_inc(s["level"], 1)
                        dve.wait_ge(s["added"], l + 1)
                        if l:
                            dve.wait_ge(s["updated"], l)
                        nc.vector.transpose(inv_t[:, T:2 * T], inv_t[:, 0:T]).then_inc(s["flipped"], 1)
                        if l == 0:
                            mask_products(1)
                        dve.wait_ge(s["updated"], l + 1)
                        dve.wait_ge(s["flipped"], l + 2)
                        nc.vector.tensor_tensor(inv_t[:, 0:T], inv_t[:, 0:T], bank(1), ALU.add
                                                ).then_inc(s["added"], 1)
                    dve.wait_ge(s["added"], 5)
                    nc.vector.transpose(inv_t[:, T:2 * T], inv_t[:, 0:T]).then_inc(s["flipped"], 1)
                    dve.wait_ge(s["uw_mm"], 2)
                    for c in range(4):
                        nc.vector.tensor_copy(
                            uw[:, T:2 * T].rearrange("p (t c j) -> p t c j", c=4, j=CH)[:, :, c, :],
                            g32(bank(1 + c, 0, P))).then_inc(s["uw_dve"], 1)
                    block_mask = cst[:, C_BLK32:C_BLK32 + P]
                    for n in range(NCH):
                        t, c = divmod(n, 4)
                        rc = slice(32 * c, 32 * c + 32)
                        if n == 0:
                            dve.wait_ge(s["uw_act"], 1)
                            nc.vector.tensor_copy(u_new[rc, :], uw[rc, 0:P]).then_inc(s["u_new"], 1)
                        else:
                            dve.wait_ge(s["w_state"], n)
                            if n >= 4:
                                dve.wait_ge(s["out_mm"], n - 3)
                            nc.vector.tensor_tensor(u_new[rc, :], uw[rc, t * P:(t + 1) * P], PS[rc, 0:P],
                                                    ALU.subtract).then_inc(s["u_new"], 1)
                        if n < NCH - 1:
                            dve.wait_ge(s["s_updated"], n + 1)
                            if n:
                                dve.wait_ge(s["out_mm"], n)
                            a = ((n + 1) % 2) * P
                            nc.vector.tensor_tensor(state[:, a:a + P], bank(1, 0, P), block_mask, ALU.mult
                                                    ).then_inc(s["s_copied"], 1)
                    dve.wait_ge(s["out_mm"], NCH)
                    dve.wait_ge(s["ema"], 1)
                    nc.vector.tensor_copy(out1[:, :], bank(3)).then_inc(s["diff"], 1)
                    dve.wait_ge(s["diff"], 1)
                    nc.vector.tensor_tensor(out1[:, CH:T], out1[:, CH:T], bank(2, CH, T), ALU.add
                                            ).then_inc(s["diff"], 1)
                    dve.wait_ge(s["diff"], 2)
                    nc.vector.tensor_tensor(diff[:, :], ema[:, :], out1[:, :], ALU.subtract).then_inc(s["diff"], 1)
                    dve.wait_ge(s["diff"], 3)
                    nc.vector.tensor_tensor(diff[:, :], diff[:, :], mix[:, :], ALU.mult).then_inc(s["mixed"], 1)
                    dve.wait_ge(s["mixed"], 1)
                    nc.vector.tensor_tensor(out1[:, :], diff[:, :], out1[:, :], ALU.add).then_inc(s["mixed"], 1)
            end_phase()
            delta.close()

            KX = P + WIN
            HH = H2 // 2
            QK = 2 * H2 * D2
            y = sb2("y", NT * P)
            hT = sb2("hT", T)
            hs = sb2("hs", NT * P)
            v2 = sb2("v2", NT * H2 * D2)
            squares2 = sb2("squares2", 2 * QK)
            normed2 = sb2("normed2", 2 * QK)
            rot = sb2("rot", 2 * QK)
            rot_sin = sb2("rot_sin", 2 * QK)
            norm2 = sb2("norm2", NT * 2 * H2)
            clip2 = sb2("clip2", NT * 2 * H2)
            inv2 = sb2("inv2", NT * 2 * H2)
            q2 = sb2("q2", 4 * T)
            row_max2 = sb2("row_max2", H2 * NT)
            bias2 = sb2("bias2", H2 * NT)
            sums2 = sb2("sums2", H2 * NT)
            log_sums2 = sb2("log_sums2", H2 * NT)
            shift_rest2 = sb2("shift_rest2", NT * H2)
            shift_part2 = sb2("shift_part2", NT * H2, BF16)
            shift_parts2 = sb2("shift_parts2", NT * 3 * H2)
            shiftT2 = sb2("shiftT2", 2 * T, BF16, 3 * HH)
            probs2 = sb2("probs2", 2 * 704)
            ctx2T = rot
            gelu = rot_sin
            glu = normed2
            final = v2[:, 0:T]
            Q_AT, Q_KEYS = (0, 128, 320, 512), (P, KX, KX, KX)
            K_AT, K_QUERIES = (0, 192, 512, 384), (KX, KX, KX, P)

            for l in range(DEPTH):
                s = phase("yT shift_low shift_high qk_mm v v_copied sq ss root clip inverse normed_qk cos sin rotated rotated_q "
                          "turn_mm turned scores max bias sum log shift_rest shift_part shift_parts shiftT "
                          "shiftT_copied scoresT probs context ctxT wo y_new step_mm low high stats moments variance "
                          "rstd normed h_mm h_ready hidden gelu glu w2_mm y_out silu product final stored "
                          "o_sq o_ms o_root o_inverse o_final s1_mm s1".split())
                before_y = xn_b if l == 0 else y
                with nc.Block() as block:
                    def halves(buf, t):
                        return buf[:, (t % 2) * QK:(t % 2 + 1) * QK].rearrange("p (n h r d) -> p n h r d", n=2, h=H2, r=2)

                    def heads(buf, t):
                        return buf[:, (t % 2) * QK:(t % 2 + 1) * QK].rearrange("p (n h d) -> p n h d", n=2, h=H2)

                    def table(n, t):
                        a = ((l * 4 + n) * NT + t) * D2
                        return tables[:, a:a + D2]

                    @block.tensor
                    def _(pe):
                        if l:
                            for t in range(NT):
                                nc.tensor.transpose(bank(0, t * P, (t + 1) * P), y[:, t * P:(t + 1) * P],
                                                    ident).then_inc(s["yT"], 1)
                        pe.wait_ge(s["shift_high"], 2)
                        pe.wait_ge(s["shift_low"], 1)

                        def project(t):
                            if t >= 2:
                                pe.wait_ge(s["normed_qk"], t - 1)
                                pe.wait_ge(s["v_copied"], t - 1)
                            for n in range(3):
                                a = l * 1536 + n * 512
                                k = 2 * (t % 2) + n if n < 2 else 4 + t % 2
                                last = nc.tensor.matmul(bank(k), hT[:, t * P:(t + 1) * P], wqkv[:, a:a + 512],
                                                        start=True, stop=True)
                                if n == 1:
                                    last.then_inc(s["qk_mm"], 1)
                            last.then_inc(s["v"], 1)

                        def turn(t):
                            pe.wait_ge(s["rotated"], t + 1)
                            pe.wait_ge(s["rotated_q"], t + 1)
                            if t:
                                pe.wait_ge(s["turned"], 3 * t)
                            for c in range(8):
                                a = (t % 2) * QK + c * P
                                last = nc.tensor.transpose(bank(6 + c // 4, c % 4 * P, (c % 4 + 1) * P), rot[:, a:a + P],
                                                           ident)
                            last.then_inc(s["turn_mm"], 1)

                        project(0)
                        if l == 0:
                            pe.wait_ge(s["o_sq"], 1)
                            nc.tensor.matmul(bank(5), cst[:, C_BLK32:C_BLK32 + P], hs[:, :], start=True,
                                             stop=True).then_inc(s["o_ms"], 1)
                            pe.wait_ge(s["o_root"], 1)
                        for t in range(1, NT):
                            project(t)
                            if t >= 2:
                                turn(t - 2)
                        turn(NT - 2)
                        turn(NT - 1)
                        pe.wait_ge(s["turned"], 3 * NT)
                        def shifts_T(half):
                            pe.wait_ge(s["shift_parts"], 3 * half + 3)
                            for i in range(NT):
                                a = (half * NT + i) * 3 * HH
                                last = nc.tensor.transpose(PS[0:3 * HH, (6 + half) * BANK + i * P:(6 + half) * BANK + (i + 1) * P],
                                                           shift_parts2[:, a:a + 3 * HH], ident)
                            last.then_inc(s["shiftT"], 1)

                        for h in range(H2):
                            q0, base = (h // 2) * T, 2 * BANK * (h % 3)
                            if h >= 3:
                                pe.wait_ge(s["sum"], NT * (h - 2))
                            for i in range(NT):
                                a, n = base + Q_AT[i], Q_KEYS[i]
                                nc.tensor.matmul(PS[:, a:a + n], q2[:, q0 + i * P:q0 + (i + 1) * P],
                                                 kz2[:, h * T + (i + 1) * P - n:h * T + (i + 1) * P],
                                                 start=True, stop=False)
                                last = nc.tensor.matmul(PS[:, a:a + n], ident16[:, :], band16[:, KX - n:KX],
                                                        start=False, stop=True)
                            last.then_inc(s["scores"], 1)
                            if h == H2 - 2:
                                shifts_T(0)

                        def scores_T(h):
                            q0, base = (h // 2) * T, 2 * BANK * ((H2 + h) % 3)
                            if h < 3:
                                pe.wait_ge(s["sum"], NT * (H2 + h - 2))
                            else:
                                pe.wait_ge(s["probs"], h - 2)
                            if h % HH == 0:
                                pe.wait_ge(s["shiftT_copied"], h // HH + 1)
                            for j in range(NT):
                                a, n = base + K_AT[j], K_QUERIES[j]
                                nc.tensor.matmul(PS[:, a:a + n], kz2[:, h * T + j * P:h * T + (j + 1) * P],
                                                 q2[:, q0 + j * P:q0 + j * P + n], start=True, stop=False)
                                nc.tensor.matmul(PS[:, a:a + n], select16[:, (h % HH) * P:(h % HH + 1) * P],
                                                 shiftT2[:, h // HH * T + j * P:h // HH * T + j * P + n],
                                                 start=False, stop=False)
                                last = nc.tensor.matmul(PS[:, a:a + n], ident16[:, :], bandT16[:, 0:n],
                                                        start=False, stop=True)
                            last.then_inc(s["scoresT"], 1)

                        def context(h):
                            g, r = h // 2, 64 * (h % 2)
                            pe.wait_ge(s["probs"], h + 1)
                            if h >= 4:
                                pe.wait_ge(s["ctxT"], g - 1)
                            o = (6 + g % 2) * BANK
                            for j in range(NT):
                                a, n = 704 * (h % 2) + K_AT[j], K_QUERIES[j]
                                v = (j * H2 + h) * D2
                                last = nc.tensor.matmul(PS[r:r + D2, o + j * P:o + j * P + n], v2[:, v:v + D2],
                                                        probs2[:, a:a + n], start=(j == 0), stop=(j == NT - 1),
                                                        tile_position=(0, r), skip_group_check=True)
                            last.then_inc(s["context"], 1)

                        for h in range(H2 + 2):
                            if h == HH - 1:
                                shifts_T(1)
                            if h < H2:
                                scores_T(h)
                            if h >= 2:
                                context(h - 2)
                        pe.wait_ge(s["ctxT"], 4)
                        for t in range(NT):
                            for c in range(4):
                                k = l * 512 + c * P
                                last = nc.tensor.matmul(bank(0, t * P, (t + 1) * P),
                                                        ctx2T[:, c * T + t * P:c * T + (t + 1) * P],
                                                        w_oa_sb[:, k:k + P], start=(c == 0), stop=(c == 3))
                        last.then_inc(s["wo"], 1)
                        if l == 0:
                            pe.wait_ge(s["o_final"], 1)
                            for t in range(NT):
                                last = nc.tensor.matmul(bank(7, t * P, (t + 1) * P), out1[:, t * P:(t + 1) * P],
                                                        wo1[:, :], start=True, stop=True)
                            last.then_inc(s["s1_mm"], 1)
                        pe.wait_ge(s["y_new"], 1)
                        upper = y[:, :].rearrange("p (t r d) -> p t r d", r=2, d=64)[:, :, 1, :]
                        nc.tensor.matmul(bank(1, 0, 256), cst[:, C_STEP:C_STEP + P], upper, start=True, stop=True)
                        nc.tensor.matmul(bank(1, 64, 256), cst[:, C_CORNER:C_CORNER + P], upper[:, 0:3, :],
                                         start=False, stop=True, skip_group_check=True).then_inc(s["step_mm"], 1)
                        for t in range(NT):
                            pe.wait_ge(s["normed"], t + 1)
                            last = nc.tensor.transpose(bank(2, t * P, (t + 1) * P), hs[:, t * P:(t + 1) * P], ident)
                        last.then_inc(s["h_mm"], 1)
                        pe.wait_ge(s["h_ready"], 1)
                        for c, (start, n) in enumerate(HCH):
                            for half in range(2):
                                k = l * 2 * HID + half * HID + start
                                u = (3 + 2 * c + half) % 8
                                nc.tensor.matmul(PS[0:n, BANK * u:BANK * (u + 1)], w1_sb[:, k:k + n], hT[:, :],
                                                 start=True, stop=True).then_inc(s["hidden"], 1)
                        for c, (start, n) in enumerate(HCH):
                            pe.wait_ge(s["glu"], c + 1)
                            for t in range(NT):
                                o = bank(1, t * P, (t + 1) * P)
                                if c == 0:
                                    nc.tensor.matmul(o, ones_row, b2_sb[:, l * P:(l + 1) * P], start=(t == 0),
                                                     stop=(t == 0), skip_group_check=True)
                                k = (l * 3 + c) * P
                                last = nc.tensor.matmul(o, glu[0:n, c * T + t * P:c * T + (t + 1) * P],
                                                        w2_sb[0:n, k:k + P], start=False, stop=True,
                                                        skip_group_check=True)
                        last.then_inc(s["w2_mm"], 1)

                    @block.gpsimd
                    def _(gp):
                        for t in range(NT):
                            gp.wait_ge(s["normed_qk"], t + 1)
                            if t >= 2:
                                gp.wait_ge(s["rotated"], t - 1)
                                gp.wait_ge(s["rotated_q"], t - 1)
                            src, to = halves(normed2, t), halves(rot_sin, t)
                            for n in (1, 0):
                                for r in range(2):
                                    nc.gpsimd.tensor_tensor(
                                        to[:, n, :, r, :], src[:, n, :, 1 - r, :],
                                        table(2 * n + 1, t)[:, 32 * r:32 * r + 32].unsqueeze(1).to_broadcast([P, H2, 32]),
                                        ALU.mult).then_inc(s["sin"], 1)
                            gp.wait_ge(s["sin"], 4 * (t + 1))
                            gp.wait_ge(s["cos"], 2 * (t + 1))
                            k = (t % 2) * QK
                            nc.gpsimd.tensor_tensor(rot[:, k:k + 512], rot[:, k:k + 512], rot_sin[:, k:k + 512], ALU.add
                                                    ).then_inc(s["rotated_q"], 1)
                        gp.wait_ge(s["variance"], 1)
                        nc.gpsimd.tensor_tensor(rstd[:, :], var_eps[:, :], minus_half[:, :], ALU.pow).then_inc(s["rstd"], 1)

                    @block.scalar
                    def _(act):
                        src = xnT_b[:, :] if l == 0 else bank(0)
                        if l:
                            act.wait_ge(s["yT"], NT)
                        nc.scalar.copy(hT[0:64, :], src[0:64, :]).then_inc(s["shift_low"], 1)
                        nc.scalar.copy(hT[64:P, 1:T], src[64:P, 0:T - 1]).then_inc(s["shift_high"], 1)

                        load_table(nc, spare, eps, 0, ACT.Sqrt)
                        if l == 0:
                            nc.scalar.square(hs[:, :], out1[:, :]).then_inc(s["o_sq"], 1)

                        def turned(t):
                            act.wait_ge(s["turn_mm"], t + 1)
                            nc.scalar.copy(q2[:, :].rearrange("p (g c) -> p g c", c=T)[:, :, t * P:(t + 1) * P],
                                           bank(6).rearrange("p (g c) -> p g c", c=P)).then_inc(s["turned"], 1)
                            if t == NT - 1:
                                return
                            for e in range(2):
                                rows = slice(64 * e, 64 * e + 64)
                                nc.scalar.copy(
                                    kz2[rows, :].rearrange("p (g e c) -> p g e c", e=2, c=T)[:, :, e, t * P:(t + 1) * P],
                                    bank(7)[rows, :].rearrange("p (g c) -> p g c", c=P)).then_inc(s["turned"], 1)

                        for t in range(NT):
                            act.wait_ge(s["qk_mm"], t + 1)
                            if t >= 2:
                                act.wait_ge(s["ss"], t - 1)
                            k = t % 2
                            nc.scalar.square(squares2[:, k * QK:(k + 1) * QK], PS[:, k * QK:(k + 1) * QK]
                                             ).then_inc(s["sq"], 1)
                            act.wait_ge(s["v"], t + 1)
                            nc.scalar.copy(v2[:, t * 512:(t + 1) * 512], bank(4 + k)).then_inc(s["v_copied"], 1)
                            if l == 0 and t == 0:
                                act.wait_ge(s["o_ms"], 1)
                                nc.scalar.activation(y[:, :], bank(5), ACT.Sqrt, bias=eps[:, 0:1], scale=1.0 / DH1
                                                     ).then_inc(s["o_root"], 1)
                            act.wait_ge(s["ss"], t + 1)
                            nc.scalar.activation(norm2[:, t * 16:(t + 1) * 16], clip2[:, t * 16:(t + 1) * 16], ACT.Sqrt
                                                 ).then_inc(s["root"], 1)
                            if t >= 2:
                                turned(t - 2)
                        turned(NT - 2)
                        load_table(nc, spare, eps, 1, ACT.Exp)
                        turned(NT - 1)
                        def shift_logs(half):
                            act.wait_ge(s["sum"], NT * HH * (half + 1))
                            at = slice(half * NT * HH, (half + 1) * NT * HH)
                            nc.scalar.activation(log_sums2[:, at], sums2[:, at], ACT.Ln).then_inc(s["log"], 1)

                        def shifts_copied(half):
                            act.wait_ge(s["shiftT"], half + 1)
                            nc.scalar.copy(shiftT2[:, half * T:(half + 1) * T],
                                           bank(6 + half)[0:3 * HH, :]).then_inc(s["shiftT_copied"], 1)

                        for h in range(H2):
                            base = 2 * BANK * (h % 3)
                            act.wait_ge(s["bias"], h + 1)
                            for i in range(NT):
                                m = NT * h + i
                                if m >= 4:
                                    act.wait_ge(s["sum"], m - 3)
                                a, n = base + Q_AT[i], Q_KEYS[i]
                                nc.scalar.activation(squares2[:, i * T:i * T + n], PS[:, a:a + n], ACT.Exp,
                                                     bias=bias2[:, m:m + 1], scale=8.0,
                                                     accum_out=sums2[:, m:m + 1]).then_inc(s["sum"], 1)
                            if h == HH - 1:
                                shift_logs(0)
                            if h == H2 - 2:
                                shifts_copied(0)
                        shift_logs(1)
                        for h in range(H2):
                            act.wait_ge(s["scoresT"], h + 1)
                            if h >= 2:
                                act.wait_ge(s["context"], h - 1)
                            base = 2 * BANK * ((H2 + h) % 3)
                            nc.scalar.activation(probs2[:, 704 * (h % 2):704 * (h % 2 + 1)], PS[:, base:base + 704],
                                                 ACT.Exp, scale=8.0).then_inc(s["probs"], 1)
                            if h == HH - 2:
                                shifts_copied(1)
                        if l == 0:
                            act.wait_ge(s["s1_mm"], 1)
                            nc.scalar.copy(s1[:, :], bank(7)).then_inc(s["s1"], 1)
                        act.wait_ge(s["y_new"], 1)
                        nc.scalar.copy(hs[:, :].rearrange("p (t r d) -> p t r d", r=2, d=64)[:, :, 0, :],
                                       y[:, :].rearrange("p (t r d) -> p t r d", r=2, d=64)[:, :, 0, :]
                                       ).then_inc(s["low"], 1)
                        act.wait_ge(s["h_mm"], 1)
                        nc.scalar.activation(hT[:, :], bank(2), ACT.Identity, bias=ln_sb[:, DEPTH + l:DEPTH + l + 1],
                                             scale=ln_sb[:, l:l + 1]).then_inc(s["h_ready"], 1)
                        for c, (start, n) in enumerate(HCH):
                            act.wait_ge(s["hidden"], 2 * c + 2)
                            if c == 2:
                                act.wait_ge(s["glu"], 1)
                            k = (c % 2) * T
                            u = (4 + 2 * c) % 8
                            b1 = (l * 2 + 1) * 3 + c
                            nc.scalar.activation(gelu[0:n, k:k + T], PS[0:n, BANK * u:BANK * (u + 1)],
                                                 ACT.Gelu, bias=b1_sb[0:n, b1:b1 + 1]).then_inc(s["gelu"], 1)
                        if l == DEPTH - 1:
                            act.wait_ge(s["y_out"], 1)
                            nc.scalar.activation(final, y[:, :], ACT.Silu).then_inc(s["silu"], 1)

                    @block.vector
                    def _(dve):
                        nc.vector.memset(hT[64:P, 0:1], 0.0).then_inc(s["shift_high"], 1)

                        def add_rotated(t):
                            dve.wait_ge(s["sin"], 4 * t + 2)
                            dve.wait_ge(s["cos"], 2 * (t + 1))
                            k = (t % 2) * QK + 512
                            nc.vector.tensor_tensor(rot[:, k:k + 512], rot[:, k:k + 512], rot_sin[:, k:k + 512], ALU.add
                                                    ).then_inc(s["rotated"], 1)

                        for t in range(NT):
                            k = t % 2
                            at = slice(t * 16, (t + 1) * 16)
                            dve.wait_ge(s["sq"], t + 1)
                            nc.vector.reduce_sum(clip2[:, at], heads(squares2, t).rearrange("p n h d -> p (n h) d"),
                                                 AX_X).then_inc(s["ss"], 1)
                            if t:
                                add_rotated(t - 1)
                            dve.wait_ge(s["root"], t + 1)
                            nc.vector.tensor_scalar(norm2[:, at], norm2[:, at], 1e-12, None, ALU.max
                                                    ).then_inc(s["clip"], 1)
                            dve.wait_ge(s["clip"], t + 1)
                            nc.vector.reciprocal(inv2[:, at], norm2[:, at]).then_inc(s["inverse"], 1)
                            dve.wait_ge(s["inverse"], t + 1)
                            if t >= 2:
                                dve.wait_ge(s["sin"], 4 * (t - 1))
                                dve.wait_ge(s["cos"], 2 * (t - 1))
                            nc.vector.tensor_tensor(
                                heads(normed2, t).rearrange("p n h d -> p (n h) d"),
                                PS[:, k * QK:(k + 1) * QK].rearrange("p (g d) -> p g d", d=D2),
                                inv2[:, at].unsqueeze(2).to_broadcast([P, 2 * H2, D2]), ALU.mult
                            ).then_inc(s["normed_qk"], 1)
                            dve.wait_ge(s["normed_qk"], t + 1)
                            if t >= 2:
                                dve.wait_ge(s["turn_mm"], t - 1)
                            for n in range(2):
                                nc.vector.tensor_tensor(
                                    heads(rot, t)[:, n], heads(normed2, t)[:, n],
                                    table(2 * n, t).unsqueeze(1).to_broadcast([P, H2, D2]), ALU.mult
                                ).then_inc(s["cos"], 1)
                        add_rotated(NT - 1)
                        dve.wait_ge(s["turn_mm"], NT)
                        for e in range(2):
                            rows = slice(64 * e, 64 * e + 64)
                            nc.vector.tensor_copy(
                                kz2[rows, :].rearrange("p (g e c) -> p g e c", e=2, c=T)[:, :, e, T - P:T],
                                bank(7)[rows, :].rearrange("p (g c) -> p g c", c=P)).then_inc(s["turned"], 1)
                        def shifts(half):
                            at = slice(half * NT * HH, (half + 1) * NT * HH)
                            dve.wait_ge(s["log"], half + 1)
                            nc.vector.scalar_tensor_tensor(
                                shift_rest2[:, at].rearrange("p (i h) -> p h i", h=HH),
                                log_sums2[:, at].rearrange("p (h i) -> p h i", i=NT), -0.125,
                                row_max2[:, at].rearrange("p (h i) -> p h i", i=NT),
                                ALU.mult, ALU.subtract).then_inc(s["shift_rest"], 1)
                            split_steps(nc, dve, s, shift_rest2[:, at], shift_part2[:, at],
                                        shift_parts2[:, half * NT * 3 * HH:(half + 1) * NT * 3 * HH], HH, half)

                        for h in range(H2):
                            base = 2 * BANK * (h % 3)
                            m = NT * h
                            dve.wait_ge(s["scores"], h + 1)
                            nc.vector.reduce_max(row_max2[:, m:m + 1], PS[:, base:base + P], AX_X).then_inc(s["max"], 1)
                            nc.vector.reduce_max(row_max2[:, m + 1:m + 3],
                                                 PS[:, base + P:base + 512].rearrange("p (i k) -> p i k", k=KX),
                                                 AX_X).then_inc(s["max"], 1)
                            nc.vector.reduce_max(row_max2[:, m + 3:m + 4], PS[:, base + 512:base + 704], AX_X
                                                 ).then_inc(s["max"], 1)
                            dve.wait_ge(s["max"], 3 * (h + 1))
                            nc.vector.tensor_scalar(bias2[:, m:m + NT], row_max2[:, m:m + NT], -8.0, None, ALU.mult
                                                    ).then_inc(s["bias"], 1)
                            if h == HH:
                                shifts(0)
                        shifts(1)
                        if l == 0:
                            dve.wait_ge(s["o_root"], 1)
                            nc.vector.reciprocal(y[:, :], y[:, :]).then_inc(s["o_inverse"], 1)
                            dve.wait_ge(s["o_inverse"], 1)
                            nc.vector.scalar_tensor_tensor(out1[:, :], out1[:, :], column[:, 1:2], y[:, :],
                                                           ALU.mult, ALU.mult).then_inc(s["o_final"], 1)
                        for g in range(4):
                            dve.wait_ge(s["context"], 2 * g + 2)
                            nc.vector.tensor_copy(ctx2T[:, g * T:(g + 1) * T], bank(6 + g % 2)).then_inc(s["ctxT"], 1)
                        dve.wait_ge(s["wo"], 1)
                        if l == 0:
                            dve.wait_ge(s["o_final"], 1)
                        nc.vector.tensor_tensor(y[:, :], before_y[:, :], bank(0), ALU.add).then_inc(s["y_new"], 1)
                        dve.wait_ge(s["step_mm"], 1)
                        nc.vector.tensor_copy(hs[:, :].rearrange("p (t r d) -> p t r d", r=2, d=64)[:, :, 1, :],
                                              bank(1, 0, 256).rearrange("p (t d) -> p t d", d=64)).then_inc(s["high"], 1)
                        dve.wait_ge(s["low"], 1)
                        dve.wait_ge(s["high"], 1)
                        layer_norm_steps(nc, s, dve, lambda t: hs[:, t * P:(t + 1) * P], stats, moments,
                                         var_eps, rstd, lambda t: hs[:, t * P:(t + 1) * P])
                        for c, (start, n) in enumerate(HCH):
                            dve.wait_ge(s["gelu"], c + 1)
                            u = (3 + 2 * c) % 8
                            b1 = l * 6 + c
                            nc.vector.scalar_tensor_tensor(glu[0:n, c * T:(c + 1) * T],
                                                           PS[0:n, BANK * u:BANK * (u + 1)], b1_sb[0:n, b1:b1 + 1],
                                                           gelu[0:n, (c % 2) * T:(c % 2 + 1) * T], ALU.add, ALU.mult
                                                           ).then_inc(s["glu"], 1)
                        dve.wait_ge(s["w2_mm"], 1)
                        nc.vector.tensor_tensor(y[:, :], y[:, :], bank(1), ALU.add).then_inc(s["y_out"], 1)
                        if l == DEPTH - 1:
                            dve.wait_ge(s["silu"], 1)
                            nc.vector.tensor_tensor(final, final, s1[:, :], ALU.mult).then_inc(s["product"], 1)
                            dve.wait_ge(s["product"], 1)
                            nc.vector.tensor_tensor(final, final, x1[:, :], ALU.add).then_inc(s["final"], 1)

                    @block.sync
                    def _(sp):
                        if l == DEPTH - 1:
                            sp.wait_ge(s["final"], 1)
                            sp.dma_start(out[bass.ds(b, 1)].rearrange("o (t p) f -> p (o t) f", p=P),
                                         final.rearrange("p (t f) -> p t f", f=P)).then_inc(s["stored"], 16)
                            sp.wait_ge(s["stored"], 16)
                end_phase()




_INS = ['L0_attn_x', 'L0_attn_Wq', 'L0_attn_Wk', 'L0_attn_Wv', 'L0_attn_Wo', 'L0_ffn_w_gate', 'L0_ffn_c_fc',
        'L0_ffn_c_proj', 'L1_attn_Wq', 'L1_attn_Wk', 'L1_attn_Wv', 'L1_attn_Wb', 'L1_attn_Wdec', 'L1_attn_Wmix',
        'L1_attn_mix_bias', 'L1_attn_wq_conv', 'L1_attn_wk_conv', 'L1_attn_wv_conv', 'L1_attn_onorm_w', 'L1_attn_Wo',
        'L1_ffn_wqkv', 'scales', 'L1_ffn_wo', 'L1_ffn_ln_g', 'L1_ffn_ln_b', 'L1_ffn_w1',
        'L1_ffn_b1', 'L1_ffn_w2', 'L1_ffn_b2', 'constants']
_TRANSPOSED = {'L1_attn_Wq', 'L1_attn_Wk', 'L1_attn_Wv', 'L1_attn_Wb', 'L1_attn_Wdec', 'L1_attn_Wmix', 'L1_attn_Wo', 'L1_ffn_ln_g',
               'L1_ffn_ln_b'}
_FLAT = {'L0_ffn_c_fc', 'L0_ffn_c_proj'}


def laid_out(name, inputs):
    if name == 'constants':
        return constants()
    if name == 'scales':
        both = []
        for layer in range(DEPTH):
            for n in ('L1_ffn_q_scale', 'L1_ffn_k_scale'):
                a = np.asarray(inputs[n])[layer]
                both += [a, np.roll(a, D2 // 2)]
        return np.ascontiguousarray(np.broadcast_to(np.concatenate(both), (P, 4 * DEPTH * D2)))
    a = np.asarray(inputs[name])
    if name == 'L1_attn_mix_bias':
        a = np.repeat(a, DH1)[:, None]
    if name == 'L1_attn_onorm_w':
        a = np.tile(a, H1)[:, None]
    if name in _TRANSPOSED:
        a = a.T
    if name in _FLAT:
        a = a.reshape(-1, a.shape[-1])
    return np.ascontiguousarray(a)


def kernel(**inputs):
    import concourse.bacc as _bacc
    from concourse import mybir as _mybir
    from concourse.bass_utils import run_bass_kernel_spmd as _run

    nc = _bacc.Bacc("TRN2", target_bir_lowering=False, num_devices=1)
    arrays, args = {}, []
    for name in _INS:
        a = laid_out(name, inputs)
        arrays[f"in_{name}_dram"] = a
        args.append(nc.dram_tensor(f"in_{name}_dram", a.shape, _mybir.dt.from_np(a.dtype), kind="ExternalInput").ap())
    out = nc.dram_tensor("out_0_dram", (B, T, P), _mybir.dt.float32, kind="ExternalOutput").ap()
    network(nc, args, out)
    r = _run(nc, [arrays], core_ids=[0])
    return r.results[0]["out_0_dram"]
```
